# Optimizing a Trainium2 kernel written in Bass

```python
import numpy as np
import jax
import jax.numpy as jnp

def _softmax(x, axis=-1):
    return jax.nn.softmax(x, axis=axis)

def _gelu(x):
    return jax.nn.gelu(x, approximate=True)

def _silu(x):
    return jax.nn.silu(x)

def _sigmoid(x):
    return jax.nn.sigmoid(x)

def _layernorm(x, axis=-1, eps=1e-05):
    m = jnp.mean(x, axis=axis, keepdims=True)
    v = jnp.var(x, axis=axis, keepdims=True)
    return (x - m) / jnp.sqrt(v + eps)

def _scatter_add(tgt, idx, src, axis=0):
    return tgt.at[idx].add(src)

def _segment_sum(src, seg, n):
    return jax.ops.segment_sum(src, seg, n)
kernel_name = 'mk_decoder_preln_d2_seqx_r8_4de48b'

def setup_inputs(seed: int=0):
    np.random.seed(seed)
    _w = jnp.asarray

    def _rec_inputs():
        import jax
        import jax.numpy as jnp
        _rk = jax.random.key(seed)
        x = -0.0002928 + 1 * jax.random.normal(jax.random.fold_in(_rk, 1), (64, 64, 256), jnp.float32)
        _lenS = 64 - jax.random.randint(jax.random.fold_in(_rk, 7), (64,), 0, max(1, 64 // 4) + 1, jnp.int32)
        _lenS2 = 64 - jax.random.randint(jax.random.fold_in(_rk, 8), (64,), 0, max(1, 64 // 4) + 1, jnp.int32)
        _ctx_512P = jax.random.normal(jax.random.fold_in(_rk, 11), (64, 16, 64), jnp.float32)
        _ctx_512c = jax.random.dirichlet(jax.random.fold_in(_rk, 511), 0.3 * jnp.ones((16,), jnp.float32), (64, 64))
        _ctx_512t = jnp.einsum('bsk,bkd->bsd', _ctx_512c, _ctx_512P)
        _ctx_512t = _ctx_512t * jax.lax.rsqrt(jnp.mean(jnp.square(_ctx_512t)) + 1e-12) * 0.953939
        ctx_512 = 0.000227908 + 0.99994 * (_ctx_512t + 0.3 * jax.random.normal(jax.random.fold_in(_rk, 611), (64, 64, 64), jnp.float32))
        return (x, ctx_512)
    x, ctx_512 = _rec_inputs()

    def _L0_attn_setup():
        import jax, jax.numpy as jnp
        import numpy as np
        N_EMBD = 256
        EXPAND = 2
        D_INNER = N_EMBD * EXPAND
        D_STATE = 128
        N_HEADS = D_INNER // D_STATE
        HEAD_DIM = D_INNER // N_HEADS
        N_GROUPS = 1
        D_CONV = 4
        CHUNK = 64
        N_LAYERS = 48
        GS = N_GROUPS * D_STATE
        PROJ = 2 * D_INNER + N_HEADS + 2 * GS
        RMS_EPS = 1e-06

        def _ssd_scan(A, B, C, dt, x, chunk_size=CHUNK):
            batch, seq_len, n_heads, P = x.shape
            G, N = (B.shape[2], B.shape[3])
            Hg = n_heads // G
            Q = chunk_size
            pad_len = -seq_len % Q
            if pad_len:
                A = jnp.pad(A, ((0, 0), (0, pad_len), (0, 0)))
                B = jnp.pad(B, ((0, 0), (0, pad_len), (0, 0), (0, 0)))
                C = jnp.pad(C, ((0, 0), (0, pad_len), (0, 0), (0, 0)))
                dt = jnp.pad(dt, ((0, 0), (0, pad_len), (0, 0)))
                x = jnp.pad(x, ((0, 0), (0, pad_len), (0, 0), (0, 0)))
            T_pad = seq_len + pad_len
            n_chunks = T_pad // Q
            A_c = A.reshape(batch, n_chunks, Q, n_heads)
            B_c = B.reshape(batch, n_chunks, Q, G, N)
            C_c = C.reshape(batch, n_chunks, Q, G, N)
            dt_c = dt.reshape(batch, n_chunks, Q, n_heads)
            x_c = x.reshape(batch, n_chunks, Q, n_heads, P)
            log_a = A_c * dt_c
            cum_log_a = jnp.cumsum(log_a, axis=2)
            chunk_log_decay = cum_log_a[:, :, -1, :]
            log_diff = cum_log_a[:, :, :, None, :] - cum_log_a[:, :, None, :, :]
            causal = jnp.tril(jnp.ones((Q, Q), dtype=jnp.bool_))[None, None, :, :, None]
            L = jnp.exp(jnp.where(causal, log_diff, -jnp.inf))
            CB = jnp.einsum('bcign,bcjgn->bcijg', C_c, B_c)
            L_rs = L.reshape(batch, n_chunks, Q, Q, G, Hg)
            dt_rs = dt_c.reshape(batch, n_chunks, Q, G, Hg)
            x_rs = x_c.reshape(batch, n_chunks, Q, G, Hg, P)
            y_intra = jnp.einsum('bcijGH,bcijG,bcjGH,bcjGHp->bciGHp', L_rs, CB, dt_rs, x_rs)
            decay_to_end = jnp.exp(chunk_log_decay[:, :, None, :] - cum_log_a)
            decay_to_end_rs = decay_to_end.reshape(batch, n_chunks, Q, G, Hg)
            state_local = jnp.einsum('bcjGH,bcjGH,bcjGn,bcjGHp->bcGHnp', decay_to_end_rs, dt_rs, B_c, x_rs)
            chunk_decay = jnp.exp(chunk_log_decay).reshape(batch, n_chunks, G, Hg)

            def scan_op(left, right):
                d_l, s_l = left
                d_r, s_r = right
                return (d_l * d_r, d_r[..., None, None] * s_l + s_r)
            _, state_at_end = jax.lax.associative_scan(scan_op, (chunk_decay, state_local), axis=1)
            state_at_start = jnp.concatenate([jnp.zeros_like(state_at_end[:, :1]), state_at_end[:, :-1]], axis=1)
            decay_from_start = jnp.exp(cum_log_a).reshape(batch, n_chunks, Q, G, Hg)
            y_inter = jnp.einsum('bciGH,bciGn,bcGHnp->bciGHp', decay_from_start, C_c, state_at_start)
            y = (y_intra + y_inter).reshape(batch, T_pad, n_heads, P)
            if pad_len:
                y = y[:, :seq_len]
            return y
        key = jax.random.key(seed)
        ks = jax.random.split(key, 6)
        Bsz, T = (2, 256)
        x = jax.random.normal(ks[0], (Bsz, T, N_EMBD), jnp.float32)
        norm_scale = jnp.ones((N_EMBD,), jnp.float32)
        in_proj_w = 0.02 * jax.random.normal(ks[1], (N_EMBD, PROJ), jnp.float32)
        conv_weight = 0.02 * jax.random.normal(ks[2], (D_CONV, D_INNER), jnp.float32)
        conv_bias = jnp.zeros((D_INNER,), jnp.float32)
        A_log = jnp.log(jnp.arange(1, N_HEADS + 1, dtype=jnp.float32))
        dt_bias = 0.1 * jax.random.normal(ks[3], (N_HEADS,), jnp.float32)
        D = jnp.ones((D_INNER,), jnp.float32)
        out_proj_w = 0.02 / np.sqrt(2 * N_LAYERS) * jax.random.normal(ks[4], (D_INNER, N_EMBD), jnp.float32)
        return dict(x=x, norm_scale=norm_scale, in_proj_w=in_proj_w, conv_weight=conv_weight, conv_bias=conv_bias, A_log=A_log, dt_bias=dt_bias, D=D, out_proj_w=out_proj_w)
    _L0_attn_all = _L0_attn_setup()
    _L0_attn_in = {k: v for k, v in _L0_attn_all.items() if k in ('norm_scale', 'in_proj_w', 'conv_weight', 'conv_bias', 'A_log', 'dt_bias', 'D', 'out_proj_w')}
    del _L0_attn_all

    def _L0_xattn_setup():
        import jax, jax.numpy as jnp
        import numpy as np
        B, S, L = (2, 128, 128)
        DIM_Q, H, K, D_C, D_CQ, R = (256, 16, 128, 64, 192, 64)

        def _rope_tables(seq_len, dim, dtype):
            inv_freq = 1.0 / 10000.0 ** (jnp.arange(0, dim, 2, dtype=dtype) / dim)
            t = jnp.arange(seq_len, dtype=dtype)
            freqs = t[:, None] * inv_freq[None, :]
            sin = jnp.repeat(jnp.sin(freqs), 2, axis=-1)
            cos = jnp.repeat(jnp.cos(freqs), 2, axis=-1)
            return (sin, cos)

        def _rotate_half(x):
            h = x.shape[-1] // 2
            return jnp.concatenate([-x[..., h:], x[..., :h]], axis=-1)
        key = jax.random.key(seed)
        ks = jax.random.split(key, 8)
        s_in = 1.0 / np.sqrt(DIM_Q)
        s_k = 1.0 / np.sqrt(K)
        s_cq = 1.0 / np.sqrt(D_CQ)
        s_c = 1.0 / np.sqrt(D_C)
        return {'hidden_q': jax.random.normal(ks[0], (B, S, DIM_Q), jnp.float32), 'kv_c': jax.random.normal(ks[1], (B, L, D_C), jnp.float32), 'Wq': jax.random.normal(ks[2], (H * K, DIM_Q), jnp.float32) * s_in, 'w_kc_q': jax.random.normal(ks[3], (H, K, D_CQ), jnp.float32) * s_k, 'w_kc_kv': jax.random.normal(ks[4], (H, K, D_C), jnp.float32) * s_k, 'W_qr': jax.random.normal(ks[5], (H, D_CQ, R), jnp.float32) * s_cq / np.sqrt(R), 'W_kr': jax.random.normal(ks[6], (H, D_C, R), jnp.float32) * s_c, 'Wo': jax.random.normal(ks[7], (DIM_Q, H * K), jnp.float32) * s_k}
    _L0_xattn_all = _L0_xattn_setup()
    _L0_xattn_in = {k: v for k, v in _L0_xattn_all.items() if k in ('Wq', 'w_kc_q', 'w_kc_kv', 'W_qr', 'W_kr', 'Wo')}
    del _L0_xattn_all

    def _L0_ffn_setup():
        import jax, jax.numpy as jnp
        import numpy as np
        H = 256
        I = 256
        E_ROUTED = 7
        NS = 1
        TOPK = 2
        TEMP = 1.0

        def _moe_forward(x, Wr, br, gate_bias, Wup, bup, Wgate, bgate, Wdown, bdown, Wsu, bsu, Wsg, bsg, Wsd, bsd):
            B, S, _ = x.shape
            xt = x.reshape(-1, H)
            N = xt.shape[0]
            gate = (xt @ Wr + br) / TEMP
            bias_gate = gate + gate_bias
            _, ids = jax.lax.top_k(bias_gate, TOPK)
            sel_logits = jnp.take_along_axis(gate, ids, axis=-1)
            masked = jnp.full_like(gate, -jnp.inf)
            masked = masked.at[jnp.arange(N)[:, None], ids].set(sel_logits)
            probs = jax.nn.softmax(masked, axis=-1)
            u = jnp.einsum('nh,ehi->eni', xt, Wup) + bup[:, None, :]
            g = jax.nn.silu(jnp.einsum('eni,eij->enj', u, Wgate) + bgate[:, None, :]) * u
            eo = jnp.einsum('enj,ejh->enh', g, Wdown) + bdown[:, None, :]
            out = jnp.einsum('ne,enh->nh', probs, eo)
            su = (xt @ Wsu + bsu).reshape(N, NS, I)
            sg = jax.nn.silu(su @ Wsg + bsg) * su
            so = (sg @ Wsd + bsd).sum(axis=1)
            out = out + so
            return out.reshape(B, S, H)
        key = jax.random.key(seed)
        ks = jax.random.split(key, 20)
        s = lambda fan_in: 1.0 / np.sqrt(fan_in)
        inp = {'x': jax.random.normal(ks[0], (4, 128, H), dtype=jnp.float32), 'Wr': jax.random.normal(ks[1], (H, E_ROUTED), jnp.float32) * s(H), 'br': jax.random.normal(ks[2], (E_ROUTED,), jnp.float32) * s(H), 'gate_bias': jnp.zeros((E_ROUTED,), jnp.float32), 'Wup': jax.random.normal(ks[3], (E_ROUTED, H, I), jnp.float32) * s(H), 'bup': jax.random.normal(ks[4], (E_ROUTED, I), jnp.float32) * s(H), 'Wgate': jax.random.normal(ks[5], (E_ROUTED, I, I), jnp.float32) * s(I), 'bgate': jax.random.normal(ks[6], (E_ROUTED, I), jnp.float32) * s(I), 'Wdown': jax.random.normal(ks[7], (E_ROUTED, I, H), jnp.float32) * s(I), 'bdown': jax.random.normal(ks[8], (E_ROUTED, H), jnp.float32) * s(I), 'Wsu': jax.random.normal(ks[9], (H, NS * I), jnp.float32) * s(H), 'bsu': jax.random.normal(ks[10], (NS * I,), jnp.float32) * s(H), 'Wsg': jax.random.normal(ks[11], (I, I), jnp.float32) * s(I), 'bsg': jax.random.normal(ks[12], (I,), jnp.float32) * s(I), 'Wsd': jax.random.normal(ks[13], (I, H), jnp.float32) * s(I), 'bsd': jax.random.normal(ks[14], (H,), jnp.float32) * s(I)}
        return inp
    _L0_ffn_all = _L0_ffn_setup()
    _L0_ffn_in = {k: v for k, v in _L0_ffn_all.items() if k in ('Wr', 'br', 'gate_bias', 'Wup', 'bup', 'Wgate', 'bgate', 'Wdown', 'bdown', 'Wsu', 'bsu', 'Wsg', 'bsg', 'Wsd', 'bsd')}
    del _L0_ffn_all

    def _L1_attn_setup():
        import jax, jax.numpy as jnp
        import numpy as np
        B, T, H = (4, 256, 256)

        def _wkv(time_decay, time_first, k, v):
            td = -jnp.exp(time_decay.astype(jnp.float32))
            tf = time_first.astype(jnp.float32)
            kT = jnp.swapaxes(k, 0, 1).astype(jnp.float32)
            vT = jnp.swapaxes(v, 0, 1).astype(jnp.float32)
            bd = (k.shape[0], k.shape[2])
            init = (jnp.zeros(bd, jnp.float32), jnp.zeros(bd, jnp.float32), jnp.full(bd, -1e+38, jnp.float32))

            def step(carry, kv_t):
                num, den, mx = carry
                kt, vt = kv_t
                mfo = jnp.maximum(mx, kt + tf)
                e1 = jnp.exp(mx - mfo)
                e2 = jnp.exp(kt + tf - mfo)
                out = (e1 * num + e2 * vt) / (e1 * den + e2)
                mfs = jnp.maximum(mx + td, kt)
                e1s = jnp.exp(mx + td - mfs)
                e2s = jnp.exp(kt - mfs)
                return ((e1s * num + e2s * vt, e1s * den + e2s, mfs), out)
            _, outT = jax.lax.scan(step, init, (kT, vT))
            return jnp.swapaxes(outT, 0, 1).astype(k.dtype)
        key = jax.random.key(seed)
        ks = jax.random.split(key, 10)
        s = 0.02
        return {'hidden': jax.random.normal(ks[0], (B, T, H), jnp.float32), 'time_decay': jax.random.normal(ks[1], (H,), jnp.float32), 'time_first': jax.random.normal(ks[2], (H,), jnp.float32), 'time_mix_key': jax.random.uniform(ks[3], (1, 1, H), jnp.float32), 'time_mix_value': jax.random.uniform(ks[4], (1, 1, H), jnp.float32), 'time_mix_receptance': jax.random.uniform(ks[5], (1, 1, H), jnp.float32), 'Wk': jax.random.normal(ks[6], (H, H), jnp.float32) * s, 'Wv': jax.random.normal(ks[7], (H, H), jnp.float32) * s, 'Wr': jax.random.normal(ks[8], (H, H), jnp.float32) * s, 'Wo': jax.random.normal(ks[9], (H, H), jnp.float32) * s}
    _L1_attn_all = _L1_attn_setup()
    _L1_attn_in = {k: v for k, v in _L1_attn_all.items() if k in ('time_decay', 'time_first', 'time_mix_key', 'time_mix_value', 'time_mix_receptance', 'Wk', 'Wv', 'Wr', 'Wo')}
    del _L1_attn_all

    def _L1_xattn_setup():
        import jax, jax.numpy as jnp
        import numpy as np
        import math
        NUM_Q_HEADS = 32
        NUM_KV_HEADS = 8
        key = jax.random.key(seed)
        k1, k2, k3 = jax.random.split(key, 3)
        B, S, E = (2, 256, 256)
        kv_E = NUM_KV_HEADS * (E // NUM_Q_HEADS)
        q = jax.random.normal(k1, (B, S, E), dtype=jnp.float32)
        k = jax.random.normal(k2, (B, S, kv_E), dtype=jnp.float32)
        v = jax.random.normal(k3, (B, S, kv_E), dtype=jnp.float32)
        return {'q': q, 'k': k, 'v': v}
    _L1_xattn_all = _L1_xattn_setup()
    _L1_xattn_in = {k: v for k, v in _L1_xattn_all.items() if k in ()}
    del _L1_xattn_all

    def _L1_ffn_setup():
        import jax, jax.numpy as jnp
        import numpy as np
        TOP_K = 8
        NEG_INF = -1000000000.0
        key = jax.random.key(seed)
        ks = jax.random.split(key, 6)
        B, S, H, I, E, G, GS = (1, 256, 256, 176, 64, 8, 8)
        sc = 0.02
        return {'hidden_states': jax.random.normal(ks[0], (B, S, H), jnp.float32), 'gate_w': jax.random.normal(ks[1], (E, H), jnp.float32) * sc, 'mask_up_w': jax.random.normal(ks[2], (G, H, GS), jnp.float32) * sc, 'gate_proj_w': jax.random.normal(ks[3], (G, I, H), jnp.float32) * sc, 'up_proj_w': jax.random.normal(ks[4], (G, I, H), jnp.float32) * sc, 'down_proj_w': jax.random.normal(ks[5], (G, H, I), jnp.float32) * sc, 'inv_map': jnp.arange(G * GS, dtype=jnp.int64).reshape(G, GS)}
    _L1_ffn_all = _L1_ffn_setup()
    _L1_ffn_in = {k: v for k, v in _L1_ffn_all.items() if k in ('gate_w', 'mask_up_w', 'gate_proj_w', 'up_proj_w', 'down_proj_w', 'inv_map')}
    del _L1_ffn_all
    return {'x': x, 'ctx_512': ctx_512, 'L0_attn_norm_scale': _L0_attn_in['norm_scale'], 'L0_attn_in_proj_w': _L0_attn_in['in_proj_w'], 'L0_attn_conv_weight': _L0_attn_in['conv_weight'], 'L0_attn_conv_bias': _L0_attn_in['conv_bias'], 'L0_attn_A_log': _L0_attn_in['A_log'], 'L0_attn_dt_bias': _L0_attn_in['dt_bias'], 'L0_attn_D': _L0_attn_in['D'], 'L0_attn_out_proj_w': _L0_attn_in['out_proj_w'], 'L0_xattn_Wq': _L0_xattn_in['Wq'], 'L0_xattn_w_kc_q': _L0_xattn_in['w_kc_q'], 'L0_xattn_w_kc_kv': _L0_xattn_in['w_kc_kv'], 'L0_xattn_W_qr': _L0_xattn_in['W_qr'], 'L0_xattn_W_kr': _L0_xattn_in['W_kr'], 'L0_xattn_Wo': _L0_xattn_in['Wo'], 'L0_ffn_Wr': _L0_ffn_in['Wr'], 'L0_ffn_br': _L0_ffn_in['br'], 'L0_ffn_gate_bias': _L0_ffn_in['gate_bias'], 'L0_ffn_Wup': _L0_ffn_in['Wup'], 'L0_ffn_bup': _L0_ffn_in['bup'], 'L0_ffn_Wgate': _L0_ffn_in['Wgate'], 'L0_ffn_bgate': _L0_ffn_in['bgate'], 'L0_ffn_Wdown': _L0_ffn_in['Wdown'], 'L0_ffn_bdown': _L0_ffn_in['bdown'], 'L0_ffn_Wsu': _L0_ffn_in['Wsu'], 'L0_ffn_bsu': _L0_ffn_in['bsu'], 'L0_ffn_Wsg': _L0_ffn_in['Wsg'], 'L0_ffn_bsg': _L0_ffn_in['bsg'], 'L0_ffn_Wsd': _L0_ffn_in['Wsd'], 'L0_ffn_bsd': _L0_ffn_in['bsd'], 'L1_attn_time_decay': _L1_attn_in['time_decay'], 'L1_attn_time_first': _L1_attn_in['time_first'], 'L1_attn_time_mix_key': _L1_attn_in['time_mix_key'], 'L1_attn_time_mix_value': _L1_attn_in['time_mix_value'], 'L1_attn_time_mix_receptance': _L1_attn_in['time_mix_receptance'], 'L1_attn_Wk': _L1_attn_in['Wk'], 'L1_attn_Wv': _L1_attn_in['Wv'], 'L1_attn_Wr': _L1_attn_in['Wr'], 'L1_attn_Wo': _L1_attn_in['Wo'], 'L1_ffn_gate_w': _L1_ffn_in['gate_w'], 'L1_ffn_mask_up_w': _L1_ffn_in['mask_up_w'], 'L1_ffn_gate_proj_w': _L1_ffn_in['gate_proj_w'], 'L1_ffn_up_proj_w': _L1_ffn_in['up_proj_w'], 'L1_ffn_down_proj_w': _L1_ffn_in['down_proj_w'], 'L1_ffn_inv_map': _L1_ffn_in['inv_map']}

def reference(x, ctx_512, L0_attn_norm_scale, L0_attn_in_proj_w, L0_attn_conv_weight, L0_attn_conv_bias, L0_attn_A_log, L0_attn_dt_bias, L0_attn_D, L0_attn_out_proj_w, L0_xattn_Wq, L0_xattn_w_kc_q, L0_xattn_w_kc_kv, L0_xattn_W_qr, L0_xattn_W_kr, L0_xattn_Wo, L0_ffn_Wr, L0_ffn_br, L0_ffn_gate_bias, L0_ffn_Wup, L0_ffn_bup, L0_ffn_Wgate, L0_ffn_bgate, L0_ffn_Wdown, L0_ffn_bdown, L0_ffn_Wsu, L0_ffn_bsu, L0_ffn_Wsg, L0_ffn_bsg, L0_ffn_Wsd, L0_ffn_bsd, L1_attn_time_decay, L1_attn_time_first, L1_attn_time_mix_key, L1_attn_time_mix_value, L1_attn_time_mix_receptance, L1_attn_Wk, L1_attn_Wv, L1_attn_Wr, L1_attn_Wo, L1_ffn_gate_w, L1_ffn_mask_up_w, L1_ffn_gate_proj_w, L1_ffn_up_proj_w, L1_ffn_down_proj_w, L1_ffn_inv_map):
    import jax
    import jax.numpy as jnp

    def _L0_attn_ref(x, norm_scale, in_proj_w, conv_weight, conv_bias, A_log, dt_bias, D, out_proj_w):
        import jax, jax.numpy as jnp
        import numpy as np
        N_EMBD = 256
        EXPAND = 2
        D_INNER = N_EMBD * EXPAND
        D_STATE = 128
        N_HEADS = D_INNER // D_STATE
        HEAD_DIM = D_INNER // N_HEADS
        N_GROUPS = 1
        D_CONV = 4
        CHUNK = 64
        N_LAYERS = 48
        GS = N_GROUPS * D_STATE
        PROJ = 2 * D_INNER + N_HEADS + 2 * GS
        RMS_EPS = 1e-06

        def _ssd_scan(A, B, C, dt, x, chunk_size=CHUNK):
            batch, seq_len, n_heads, P = x.shape
            G, N = (B.shape[2], B.shape[3])
            Hg = n_heads // G
            Q = chunk_size
            pad_len = -seq_len % Q
            if pad_len:
                A = jnp.pad(A, ((0, 0), (0, pad_len), (0, 0)))
                B = jnp.pad(B, ((0, 0), (0, pad_len), (0, 0), (0, 0)))
                C = jnp.pad(C, ((0, 0), (0, pad_len), (0, 0), (0, 0)))
                dt = jnp.pad(dt, ((0, 0), (0, pad_len), (0, 0)))
                x = jnp.pad(x, ((0, 0), (0, pad_len), (0, 0), (0, 0)))
            T_pad = seq_len + pad_len
            n_chunks = T_pad // Q
            A_c = A.reshape(batch, n_chunks, Q, n_heads)
            B_c = B.reshape(batch, n_chunks, Q, G, N)
            C_c = C.reshape(batch, n_chunks, Q, G, N)
            dt_c = dt.reshape(batch, n_chunks, Q, n_heads)
            x_c = x.reshape(batch, n_chunks, Q, n_heads, P)
            log_a = A_c * dt_c
            cum_log_a = jnp.cumsum(log_a, axis=2)
            chunk_log_decay = cum_log_a[:, :, -1, :]
            log_diff = cum_log_a[:, :, :, None, :] - cum_log_a[:, :, None, :, :]
            causal = jnp.tril(jnp.ones((Q, Q), dtype=jnp.bool_))[None, None, :, :, None]
            L = jnp.exp(jnp.where(causal, log_diff, -jnp.inf))
            CB = jnp.einsum('bcign,bcjgn->bcijg', C_c, B_c)
            L_rs = L.reshape(batch, n_chunks, Q, Q, G, Hg)
            dt_rs = dt_c.reshape(batch, n_chunks, Q, G, Hg)
            x_rs = x_c.reshape(batch, n_chunks, Q, G, Hg, P)
            y_intra = jnp.einsum('bcijGH,bcijG,bcjGH,bcjGHp->bciGHp', L_rs, CB, dt_rs, x_rs)
            decay_to_end = jnp.exp(chunk_log_decay[:, :, None, :] - cum_log_a)
            decay_to_end_rs = decay_to_end.reshape(batch, n_chunks, Q, G, Hg)
            state_local = jnp.einsum('bcjGH,bcjGH,bcjGn,bcjGHp->bcGHnp', decay_to_end_rs, dt_rs, B_c, x_rs)
            chunk_decay = jnp.exp(chunk_log_decay).reshape(batch, n_chunks, G, Hg)

            def scan_op(left, right):
                d_l, s_l = left
                d_r, s_r = right
                return (d_l * d_r, d_r[..., None, None] * s_l + s_r)
            _, state_at_end = jax.lax.associative_scan(scan_op, (chunk_decay, state_local), axis=1)
            state_at_start = jnp.concatenate([jnp.zeros_like(state_at_end[:, :1]), state_at_end[:, :-1]], axis=1)
            decay_from_start = jnp.exp(cum_log_a).reshape(batch, n_chunks, Q, G, Hg)
            y_inter = jnp.einsum('bciGH,bciGn,bcGHnp->bciGHp', decay_from_start, C_c, state_at_start)
            y = (y_intra + y_inter).reshape(batch, T_pad, n_heads, P)
            if pad_len:
                y = y[:, :seq_len]
            return y
        residual = x
        b, t = (x.shape[0], x.shape[1])
        h = x * jax.lax.rsqrt(jnp.mean(x * x, axis=-1, keepdims=True) + RMS_EPS) * norm_scale
        proj = h @ in_proj_w
        gate = proj[..., :D_INNER]
        ssm_in = proj[..., D_INNER:2 * D_INNER]
        dt_raw = proj[..., 2 * D_INNER:2 * D_INNER + N_HEADS]
        Bm = proj[..., 2 * D_INNER + N_HEADS:2 * D_INNER + N_HEADS + GS].reshape(b, t, N_GROUPS, D_STATE)
        Cm = proj[..., 2 * D_INNER + N_HEADS + GS:].reshape(b, t, N_GROUPS, D_STATE)
        xp = jnp.pad(ssm_in, ((0, 0), (D_CONV - 1, 0), (0, 0)))
        w_t = conv_weight.T[:, None, :]
        y = jax.lax.conv_general_dilated(jnp.transpose(xp, (0, 2, 1)), w_t, window_strides=(1,), padding='VALID', feature_group_count=D_INNER)
        ssm_in = jnp.transpose(y, (0, 2, 1)) + conv_bias
        ssm_in = jax.nn.silu(ssm_in)
        dt = jax.nn.softplus(dt_raw + dt_bias)
        A = -jnp.exp(A_log)
        A_f = jnp.broadcast_to(A[None, None, :], (b, t, N_HEADS))
        x_h = ssm_in.reshape(b, t, N_HEADS, HEAD_DIM)
        y_ssd = _ssd_scan(A_f, Bm, Cm, dt, x_h).reshape(b, t, D_INNER)
        y_ssd = y_ssd + D * ssm_in
        y_ssd = y_ssd * jax.nn.silu(gate)
        return residual + y_ssd @ out_proj_w

    def _L0_xattn_ref(hidden_q, kv_c, Wq, w_kc_q, w_kc_kv, W_qr, W_kr, Wo):
        import jax, jax.numpy as jnp
        import numpy as np
        B, S, L = (2, 128, 128)
        DIM_Q, H, K, D_C, D_CQ, R = (256, 16, 128, 64, 192, 64)

        def _rope_tables(seq_len, dim, dtype):
            inv_freq = 1.0 / 10000.0 ** (jnp.arange(0, dim, 2, dtype=dtype) / dim)
            t = jnp.arange(seq_len, dtype=dtype)
            freqs = t[:, None] * inv_freq[None, :]
            sin = jnp.repeat(jnp.sin(freqs), 2, axis=-1)
            cos = jnp.repeat(jnp.cos(freqs), 2, axis=-1)
            return (sin, cos)

        def _rotate_half(x):
            h = x.shape[-1] // 2
            return jnp.concatenate([-x[..., h:], x[..., :h]], axis=-1)
        b, s, _ = hidden_q.shape
        l = kv_c.shape[1]
        q_hk = (hidden_q @ Wq.T).reshape(b, s, H, K)
        q_big = jnp.einsum('bshk,hkq->bshq', q_hk, w_kc_q)
        sin, cos = _rope_tables(l, D_C, kv_c.dtype)
        kv_rope = kv_c * cos[None] + _rotate_half(kv_c) * sin[None]
        q_r = jnp.einsum('bshq,hqr->bhsr', q_big, W_qr)
        k_r = jnp.einsum('bld,hdr->bhlr', kv_rope, W_kr)
        scores = jnp.einsum('bhsr,bhlr->bhsl', q_r, k_r)
        attn = jax.nn.softmax(scores, axis=-1)
        ctx_c = jnp.einsum('bhsl,bld->bhsd', attn, kv_rope)
        ctx_lat = jnp.einsum('bhsd,hkd->bshk', ctx_c, w_kc_kv)
        out = ctx_lat.reshape(b, s, H * K) @ Wo.T
        return out

    def _L0_ffn_ref(x, Wr, br, gate_bias, Wup, bup, Wgate, bgate, Wdown, bdown, Wsu, bsu, Wsg, bsg, Wsd, bsd):
        import jax, jax.numpy as jnp
        import numpy as np
        H = 256
        I = 256
        E_ROUTED = 7
        NS = 1
        TOPK = 2
        TEMP = 1.0

        def _moe_forward(x, Wr, br, gate_bias, Wup, bup, Wgate, bgate, Wdown, bdown, Wsu, bsu, Wsg, bsg, Wsd, bsd):
            B, S, _ = x.shape
            xt = x.reshape(-1, H)
            N = xt.shape[0]
            gate = (xt @ Wr + br) / TEMP
            bias_gate = gate + gate_bias
            _, ids = jax.lax.top_k(bias_gate, TOPK)
            sel_logits = jnp.take_along_axis(gate, ids, axis=-1)
            masked = jnp.full_like(gate, -jnp.inf)
            masked = masked.at[jnp.arange(N)[:, None], ids].set(sel_logits)
            probs = jax.nn.softmax(masked, axis=-1)
            u = jnp.einsum('nh,ehi->eni', xt, Wup) + bup[:, None, :]
            g = jax.nn.silu(jnp.einsum('eni,eij->enj', u, Wgate) + bgate[:, None, :]) * u
            eo = jnp.einsum('enj,ejh->enh', g, Wdown) + bdown[:, None, :]
            out = jnp.einsum('ne,enh->nh', probs, eo)
            su = (xt @ Wsu + bsu).reshape(N, NS, I)
            sg = jax.nn.silu(su @ Wsg + bsg) * su
            so = (sg @ Wsd + bsd).sum(axis=1)
            out = out + so
            return out.reshape(B, S, H)
        return _moe_forward(x, Wr, br, gate_bias, Wup, bup, Wgate, bgate, Wdown, bdown, Wsu, bsu, Wsg, bsg, Wsd, bsd)

    def _L1_attn_ref(hidden, time_decay, time_first, time_mix_key, time_mix_value, time_mix_receptance, Wk, Wv, Wr, Wo):
        import jax, jax.numpy as jnp
        import numpy as np
        B, T, H = (4, 256, 256)

        def _wkv(time_decay, time_first, k, v):
            td = -jnp.exp(time_decay.astype(jnp.float32))
            tf = time_first.astype(jnp.float32)
            kT = jnp.swapaxes(k, 0, 1).astype(jnp.float32)
            vT = jnp.swapaxes(v, 0, 1).astype(jnp.float32)
            bd = (k.shape[0], k.shape[2])
            init = (jnp.zeros(bd, jnp.float32), jnp.zeros(bd, jnp.float32), jnp.full(bd, -1e+38, jnp.float32))

            def step(carry, kv_t):
                num, den, mx = carry
                kt, vt = kv_t
                mfo = jnp.maximum(mx, kt + tf)
                e1 = jnp.exp(mx - mfo)
                e2 = jnp.exp(kt + tf - mfo)
                out = (e1 * num + e2 * vt) / (e1 * den + e2)
                mfs = jnp.maximum(mx + td, kt)
                e1s = jnp.exp(mx + td - mfs)
                e2s = jnp.exp(kt - mfs)
                return ((e1s * num + e2s * vt, e1s * den + e2s, mfs), out)
            _, outT = jax.lax.scan(step, init, (kT, vT))
            return jnp.swapaxes(outT, 0, 1).astype(k.dtype)
        shifted = jnp.pad(hidden, ((0, 0), (1, 0), (0, 0)))[:, :-1]
        key = hidden * time_mix_key + shifted * (1.0 - time_mix_key)
        value = hidden * time_mix_value + shifted * (1.0 - time_mix_value)
        rec = hidden * time_mix_receptance + shifted * (1.0 - time_mix_receptance)
        k = key @ Wk
        v = value @ Wv
        r = jax.nn.sigmoid(rec @ Wr)
        rwkv = _wkv(time_decay, time_first, k, v)
        return r * rwkv @ Wo

    def _L1_xattn_ref(q, k, v):
        import jax, jax.numpy as jnp
        import numpy as np
        import math
        NUM_Q_HEADS = 32
        NUM_KV_HEADS = 8
        B, S, E = q.shape
        H, KV = (NUM_Q_HEADS, NUM_KV_HEADS)
        D = E // H
        G = H // KV
        scale = math.sqrt(D)
        qh = q.reshape(B, S, KV, G, D).transpose(0, 2, 3, 1, 4)
        kh = k.reshape(B, S, KV, D).transpose(0, 2, 1, 3)
        vh = v.reshape(B, S, KV, D).transpose(0, 2, 1, 3)
        scores = jnp.einsum('bkgsd,bktd->bkgst', qh, kh) / scale
        weights = jax.nn.softmax(scores, axis=-1)
        out = jnp.einsum('bkgst,bktd->bkgsd', weights, vh)
        return out.transpose(0, 3, 1, 2, 4).reshape(B, S, E)

    def _L1_ffn_ref(hidden_states, gate_w, mask_up_w, gate_proj_w, up_proj_w, down_proj_w, inv_map):
        import jax, jax.numpy as jnp
        import numpy as np
        TOP_K = 8
        NEG_INF = -1000000000.0
        B, S, H = hidden_states.shape
        x = hidden_states.reshape(-1, H)
        N = x.shape[0]
        E = gate_w.shape[0]
        scores = jax.nn.softmax(x @ gate_w.T, axis=-1)
        topk_w, topk_idx = jax.lax.top_k(scores, TOP_K)
        w_e = jnp.zeros((N, E), x.dtype).at[jnp.arange(N)[:, None], topk_idx].add(topk_w)
        flat = w_e[:, inv_map]
        scalar = flat.sum(-1)
        soft = jax.nn.softmax(jnp.where(flat == 0, NEG_INF, flat), axis=-1)
        xg = x[:, None, :] + jnp.einsum('ngi,ghi->ngh', soft, mask_up_w)
        g = jnp.einsum('ngh,gih->ngi', xg, gate_proj_w)
        u = jnp.einsum('ngh,gih->ngi', xg, up_proj_w)
        a = jax.nn.silu(g) * u
        d = jnp.einsum('ngi,ghi->ngh', a, down_proj_w)
        y = jnp.einsum('ng,ngh->nh', scalar, d)
        return y.reshape(B, S, H)
    x = x + _L0_attn_ref(_layernorm(x, axis=-1), L0_attn_norm_scale, L0_attn_in_proj_w, L0_attn_conv_weight, L0_attn_conv_bias, L0_attn_A_log, L0_attn_dt_bias, L0_attn_D, L0_attn_out_proj_w)
    x = x + _L0_xattn_ref(_layernorm(x, axis=-1), ctx_512, L0_xattn_Wq, L0_xattn_w_kc_q, L0_xattn_w_kc_kv, L0_xattn_W_qr, L0_xattn_W_kr, L0_xattn_Wo)
    x = x + _L0_ffn_ref(_layernorm(x, axis=-1), L0_ffn_Wr, L0_ffn_br, L0_ffn_gate_bias, L0_ffn_Wup, L0_ffn_bup, L0_ffn_Wgate, L0_ffn_bgate, L0_ffn_Wdown, L0_ffn_bdown, L0_ffn_Wsu, L0_ffn_bsu, L0_ffn_Wsg, L0_ffn_bsg, L0_ffn_Wsd, L0_ffn_bsd)
    x = x + _L1_attn_ref(_layernorm(x, axis=-1), L1_attn_time_decay, L1_attn_time_first, L1_attn_time_mix_key, L1_attn_time_mix_value, L1_attn_time_mix_receptance, L1_attn_Wk, L1_attn_Wv, L1_attn_Wr, L1_attn_Wo)
    x = x + _L1_xattn_ref(_layernorm(x, axis=-1), ctx_512, ctx_512)
    x = x + _L1_ffn_ref(_layernorm(x, axis=-1), L1_ffn_gate_w, L1_ffn_mask_up_w, L1_ffn_gate_proj_w, L1_ffn_up_proj_w, L1_ffn_down_proj_w, L1_ffn_inv_map)
    return x

_drawn_inputs = setup_inputs


def setup_inputs(seed=0):
    import zlib

    import numpy as np

    out = dict(_drawn_inputs(seed))
    spreads = {'L0_attn_norm_scale': (1.0, 0.2),
     'L0_attn_conv_bias': (0.0, 0.1),
     'L0_attn_D': (1.0, 0.2),
     'L0_ffn_gate_bias': (0.0, 0.1)}
    factors = {}
    for name, (base, spread) in spreads.items():
        noise = np.random.default_rng([zlib.crc32(name.encode()), seed]).standard_normal(out[name].shape)
        drawn = base * np.exp(spread * noise) if base else spread * noise
        out[name] = jnp.asarray(drawn.astype(out[name].dtype))
    for name, factor in factors.items():
        out[name] = (out[name] * factor).astype(out[name].dtype)
    return out
```

```python
from contextlib import ExitStack

import numpy as np
import concourse.bass as bass
from concourse import mybir

ALU = mybir.AluOpType
ACT = mybir.ActivationFunctionType
F32 = mybir.dt.float32
I32 = mybir.dt.int32
AX = mybir.AxisListType.X

P = 128
NT = 32
TB = 2
NB = 4
NBLK = NT // TB
NTH = 2
NH = 16
NEG = -1.0e38


class Queue:

    def __init__(self, sem, eng):
        self.sem, self.eng, self.n, self.seen = sem, eng, 0, {}

    def wait(self, *tokens):
        for sem, value in tokens:
            if self.seen.get(id(sem), 0) < value:
                self.seen[id(sem)] = value
                if self.eng is not None:
                    self.eng.wait_ge(sem, value)

    def put(self, fn, *tokens):
        self.wait(*tokens)
        self.n += 1
        if self.eng is not None:
            fn(self.eng).then_inc(self.sem, 1)
        return (self.sem, self.n)

    def dma(self, fn, sem):
        if self.eng is not None:
            fn(self.eng).then_inc(sem, 16)


CONSTS = {"ident": 128, "tri": 128, "gt": 128, "cos": 64, "sin": 64, "mv": 64, "mk": 8, "mg": 8, "eid": 1}
PARAMS = {
    "w_in": 2 * 1284, "nscale": 2, "convw": 16, "convb": 4, "dskip": 4, "alog": 4, "dtb": 4, "w_out": 4 * 256,
    "rb": 7, "gb": 7, "mix": 6, "tdf": 4, "w_kvro": 8 * 256,
}


def build(nc, t, out):
    ctx = ExitStack()
    with ctx:
        def sb(name, n, parts=P, dt=F32):
            return ctx.enter_context(nc.sbuf_tensor(name, [parts, n], dt))

        sems = {}

        def sem(name):
            if name not in sems:
                sems[name] = ctx.enter_context(nc.semaphore(name))
            return sems[name]

        SB = {n: sb("c_" + n, w) for n, w in {**CONSTS, **PARAMS}.items()}
        X = sb("X", NT * 256)[:, :].rearrange("p (t c) -> p t c", t=NT)
        Aw = sb("Aw", 2 * 1024)[:, :].rearrange("p (k n) -> p k n", k=2)
        Bw = sb("Bw", 8 * 256)[:, :].rearrange("p (h n) -> p h n", h=8)
        BIG = sb("BIG", 12448)
        acst = sb("acst", 64)
        mhalf = sb("mhalf", 8)
        td65 = sb("td65", 2 * NB * 65)
        om = sb("om", 6)
        invt = sb("invt", 64, 64, I32)
        bdn = sb("bdn", 256, 8)
        arenas = [sb(f"arena{i}", 7800) for i in range(NTH)]
        stores = [sb(f"small{i}", 640) for i in range(NTH)]
        banks = [ctx.enter_context(nc.psum_tensor(f"ps{i}", [P, 512], F32)) for i in range(8)]

        def program(name, eng):
            T, V, A, G, S = (Queue(sem("s_" + n), eng if n == name else None) for n in ("pe", "dve", "act", "pool", "sp"))

            ident = SB["ident"][:, :]

            loads = {}

            def load(name, dst, src, wait=()):
                s = sem("l_" + name)
                S.wait(*wait)
                S.dma(lambda e: e.dma_start(dst, src), s)
                loads[name] = (s, 16)

            for name in ("ident", "w_in", "nscale"):
                load(name, SB[name][:, :], t[name])
            xsem = []

            def load_x(n):
                s = sem(f"l_x{n}")
                S.dma(lambda e: e.dma_start(X[:, 4 * n:4 * n + 4, :],
                                                    t["x"][512 * n:512 * n + 512, :].rearrange("(t p) c -> p t c", p=P)),
                      s)
                xsem.append((s, 16))

            load_x(0)
            for name in ("convw", "convb", "dskip", "alog", "dtb", "tri", "gt", "w_out"):
                load(name, SB[name][:, :], t[name])
            load_x(1)

            o = 0

            def big(n, parts=P):
                nonlocal o
                r = BIG[0:parts, o:o + n]
                o += n
                return r

            wkcq = big(2 * 8 * 128, 96).rearrange("p (c h k) -> p c h k", c=2, h=8)
            wqr = big(8 * 192, 64).rearrange("p (h c) -> p h c", h=8)
            wkr = big(8 * 64, 64).rearrange("p (h c) -> p h c", h=8)
            wq = big(8 * 256).rearrange("p (h c) -> p h c", h=8)
            wkc = big(8 * 64).rearrange("p (h c) -> p h c", h=8)
            wo = big(8 * 256).rearrange("p (h c) -> p h c", h=8)
            g1 = big(2 * 8 * 64, 96).rearrange("p (c h d) -> p c h d", c=2, h=8)
            g2 = big(8 * 64).rearrange("p (h d) -> p h d", h=8)
            assert o <= 12448

            def load_pre(half, wait):
                hs = slice(8 * half, 8 * half + 8)
                for name, dst, src in (("wkcq", wkcq, t["wkcq"][:, :, hs, :]), ("wqr", wqr, t["wqr"][:, hs, :]),
                                       ("wkr", wkr, t["wkr"][:, hs, :]), ("wq", wq, t["wq"][:, hs, :]),
                                       ("wkc", wkc, t["wkc"][:, hs, :]), ("wo", wo, t["wo"][:, hs, :])):
                    load(f"{name}_{half}", dst, src, wait)

            load_pre(0, ())
            for n in range(2, 8):
                load_x(n)
            for name in ("cos", "sin", "mv", "mk", "mg", "eid", "rb", "gb", "mix", "tdf", "w_kvro"):
                load(name, SB[name][:, :], t[name])
            s_inv = sem("l_invt")
            S.dma(lambda e: e.dma_start(invt[:, :], t["invt"]), s_inv)
            loads["invt"] = (s_inv, 16)

            UP, UG, UD = (BIG[:, 4096 * n:4096 * n + 4096].rearrange("p (e k n) -> p e k n", e=8, k=2) for n in range(3))
            moe_b = BIG[:, 12288:12320].rearrange("p (a e k) -> p a e k", a=2, e=8)
            moe_r = BIG[:, 12320:12334].rearrange("p (k n) -> p k n", k=2)
            WG = BIG[:, 0:5632].rearrange("p (k n) -> p k n", k=2)
            WD = BIG[:, 5632:8448].rearrange("p (k n) -> p k n", k=11)
            MG = BIG[0:64, 8448:11264]
            MW = BIG[:, 11264:11392].rearrange("p (k n) -> p k n", k=2)
            GW = BIG[:, 11392:11520].rearrange("p (k n) -> p k n", k=2)
            PM = BIG[0:64, 11520:11584]

            w_in = SB["w_in"][:, :].rearrange("p (k n) -> p k n", k=2)
            w_out = SB["w_out"][:, :].rearrange("p (k n) -> p k n", k=4)
            convw = SB["convw"][:, :].rearrange("p (f k) -> p f k", f=4)
            kvro = SB["w_kvro"][:, :].rearrange("p (m k n) -> p m k n", m=4, k=2)
            mix = SB["mix"][:, :].rearrange("p (m k) -> p m k", m=3)
            omx = om[:, :].rearrange("p (m k) -> p m k", m=3)
            td65v = td65[:, :].rearrange("p (k b s) -> p k b s", k=2, b=NB)
            tdf = SB["tdf"]

            def mm(out_ap, lhsT, rhs, start, stop):
                return lambda e: e.matmul(out_ap, lhsT, rhs, start=start, stop=stop, skip_group_check=True)

            half = V.put(lambda e: e.memset(mhalf[:, :], -0.5))
            win_ok = []
            V.wait(loads["w_in"], loads["nscale"])
            for k in range(2):
                win_ok.append(V.put(lambda e, k=k: e.tensor_scalar(w_in[:, k, :], w_in[:, k, :],
                                                                   SB["nscale"][:, k:k + 1], None, ALU.mult)))
            win_ok = win_ok[-1]
            ea = A.put(lambda e: e.activation(acst[:, 0:4], SB["alog"][:, :], ACT.Exp), loads["alog"])
            a_ok = V.put(lambda e: e.tensor_scalar(acst[:, 4:8], acst[:, 0:4], -1.0, None, ALU.mult), ea)

            class Thread:
                def __init__(self, i):
                    self.i, self.free, self.at = i, [(T.sem, 0)] * 4, 0
                    self.done = []

                def bank(self):
                    b = self.at % 4
                    self.at += 1
                    T.wait(self.free[b])
                    return b, banks[4 * self.i + b]

                def start(self):
                    self.ao = self.so = 0
                    for q in (T, V, A, G, S):
                        q.wait(*self.done)

                def cut(self, n, parts=P):
                    self.ao += n
                    assert self.ao <= 7800, self.ao
                    return arenas[self.i][0:parts, self.ao - n:self.ao]

                def sm(self, n):
                    self.so += n
                    assert self.so <= 640
                    return stores[self.i][:, self.so - n:self.so]

                def end(self, *tokens):
                    self.done = [(q.sem, q.n) for q in (T, V, A, G)] + list(tokens)

            threads = [Thread(i) for i in range(NTH)]

            def norm(th, blk, hview, rms=None):
                st = th.sm(12).rearrange("p (t c) -> p t c", t=TB)
                mv = th.sm(4).rearrange("p (t c) -> p t c", t=TB)
                w = th.sm(16).rearrange("p (a t) -> p a t", t=TB)
                V.wait(xsem[blk * TB // 4])
                for i in range(TB):
                    a = V.put(lambda e, i=i: e.bn_stats(st[:, i, :], X[:, blk * TB + i, :]))
                for i in range(TB):
                    a = V.put(lambda e, i=i: e.bn_aggr(mv[:, i, :], st[:, i, :]), a)
                a = V.put(lambda e: e.tensor_scalar(w[:, 0, :], mv[:, :, 1], 1e-5, None, ALU.add), a)
                g = G.put(lambda e: e.tensor_tensor(w[:, 1, :], w[:, 0, :], mhalf[:, 0:TB], ALU.pow), a, half)
                if rms is not None:
                    g = G.put(lambda e: e.tensor_tensor(w[:, 2, :], w[:, 1, :], w[:, 1, :], ALU.mult), g)
                    g = G.put(lambda e: e.tensor_tensor(w[:, 3, :], w[:, 2, :], mv[:, :, 1], ALU.mult), g)
                    g = G.put(lambda e: e.tensor_scalar(w[:, 4, :], w[:, 3, :], 1e-6, None, ALU.add), g)
                    g = G.put(lambda e: e.tensor_tensor(w[:, 5, :], w[:, 4, :], mhalf[:, 0:TB], ALU.pow), g)
                V.wait(g)
                for i in range(TB):
                    for dst, src in hview(i, X[:, blk * TB + i, :]):
                        a = V.put(lambda e, i=i, dst=dst, src=src: e.tensor_scalar(
                            dst, src, mv[:, i, 0:1], w[:, 1, i:i + 1], ALU.subtract, ALU.mult))
                    if rms is not None:
                        b = V.put(lambda e, i=i: e.tensor_scalar(rms(i), hview(i, None)[0][0], w[:, 5, i:i + 1], None,
                                                                 ALU.mult), a)
                        a = b
                return a

            def turned(th, h, ready, dst):
                b, ps = th.bank()
                T.wait(loads["ident"])
                for k in range(2):
                    for i in range(TB):
                        tok = T.put(lambda e, k=k, i=i: e.transpose(ps[:, k * 256 + i * P:k * 256 + i * P + P],
                                                                    h[:, i, k * P:k * P + P], ident), ready)
                th.free[b] = c = A.put(lambda e: e.activation(dst, ps[:, :].rearrange("p (k n) -> p k n", k=2)
                                                              if len(dst.shape) == 3 else
                                                              ps[:, :].rearrange("p (k b s) -> p k b s", k=2, b=NB),
                                                              ACT.Copy), tok)
                return c

    
            def stage1(th, blk):
                th.start()
                t0 = blk * TB
                hl = th.cut(512).rearrange("p (t c) -> p t c", t=TB)
                h = th.cut(512).rearrange("p (t c) -> p t c", t=TB)
                hT = th.cut(512).rearrange("p (k n) -> p k n", k=2)
                sT = th.cut(1024).rearrange("p (f n) -> p f n", f=4)
                gT = th.cut(1024).rearrange("p (f n) -> p f n", f=4)
                BC = th.cut(512).rearrange("p (f n) -> p f n", f=2)
                hn = norm(th, blk, lambda i, x: [(hl[:, i, :], x)], lambda i: h[:, i, :])
                xa = G.put(lambda e: e.tensor_tensor(X[:, t0:t0 + TB, :], X[:, t0:t0 + TB, :], hl[:, :, :], ALU.add), hn)
                yield
                ht = turned(th, h, hn, hT[:, :, :])
                yield
                dz = th.sm(64).rearrange("p (a c) -> p a c", a=8)
                b, ps = th.bank()
                T.wait(ht, win_ok)
                for i in range(TB):
                    for k in range(2):
                        tok = T.put(mm(ps[:, 4 * i:4 * i + 4], hT[:, k, i * P:i * P + P], w_in[:, k, 1024:1028],
                                       k == 0, k == 1))
                dtb = SB["dtb"][:, :].unsqueeze(1).broadcast_to([P, TB, 4])
                d2 = lambda j: dz[:, j, :].rearrange("p (t c) -> p t c", t=TB)
                th.free[b] = v = V.put(lambda e: e.tensor_tensor(d2(0), ps[:, 0:8].rearrange("p (t c) -> p t c", t=TB),
                                                                 dtb, ALU.add), tok, loads["dtb"])
                v = V.put(lambda e: e.scalar_tensor_tensor(dz[:, 1, :], dz[:, 0, :], -1.0, dz[:, 0, :], ALU.mult, ALU.max), v)
                v2 = V.put(lambda e: e.tensor_scalar(dz[:, 4, :], dz[:, 0, :], 0.0, None, ALU.max))
                a = A.put(lambda e: e.activation(dz[:, 2, :], dz[:, 1, :], ACT.Exp, scale=-1.0), v)
                a = A.put(lambda e: e.activation(dz[:, 3, :], dz[:, 2, :], ACT.Ln, bias=1.0), a)
                v = V.put(lambda e: e.tensor_tensor(dz[:, 5, :], dz[:, 3, :], dz[:, 4, :], ALU.add), a, v2)
                dt_ok = V.put(lambda e: e.tensor_tensor(d2(6), d2(5), acst[:, 4:8].unsqueeze(1).broadcast_to([P, TB, 4]),
                                                        ALU.mult), v, a_ok)
                cv = th.cut(1024).rearrange("p (f n) -> p f n", f=4)
                V.wait(loads["convw"], loads["convb"])
                for g in range(2):
                    b, ps = th.bank()
                    for f in range(2):
                        for k in range(2):
                            c0 = 512 + (2 * g + f) * P
                            tok = T.put(mm(ps[:, f * 256:f * 256 + 256], w_in[:, k, c0:c0 + P], hT[:, k, :],
                                           k == 0, k == 1))
                    yield
                    for f in range(2):
                        ff = 2 * g + f
                        src = ps[:, f * 256:f * 256 + 256]
                        s3 = src.rearrange("p (b s) -> p b s", b=NB)
                        c3 = cv[:, ff, :].rearrange("p (b s) -> p b s", b=NB)
                        v = V.put(lambda e: e.tensor_scalar(cv[:, ff, :], src, convw[:, ff, 3:4],
                                                            SB["convb"][:, ff:ff + 1], ALU.mult, ALU.add), tok)
                        for d in (1, 2, 3):
                            v = V.put(lambda e: e.scalar_tensor_tensor(c3[:, :, d:64], s3[:, :, 0:64 - d],
                                                                       convw[:, ff, 3 - d:4 - d], c3[:, :, d:64],
                                                                       ALU.mult, ALU.add), v)
                    th.free[b] = v
                    s_ok = A.put(lambda e: e.activation(sT[:, 2 * g:2 * g + 2, :], cv[:, 2 * g:2 * g + 2, :], ACT.Silu), v)
                for g in range(2):
                    b, ps = th.bank()
                    for f in range(2):
                        for k in range(2):
                            c0 = (2 * g + f) * P
                            tok = T.put(mm(ps[:, f * 256:f * 256 + 256], w_in[:, k, c0:c0 + P], hT[:, k, :],
                                           k == 0, k == 1))
                    th.free[b] = g_ok = A.put(lambda e: e.activation(
                        gT[:, 2 * g:2 * g + 2, :], ps[:, :].rearrange("p (f n) -> p f n", f=2), ACT.Silu), tok)
                    yield
                b, ps = th.bank()
                for f in range(2):
                    for k in range(2):
                        tok = T.put(mm(ps[:, f * 256:f * 256 + 256], w_in[:, k, 1028 + f * P:1156 + f * P], hT[:, k, :],
                                       k == 0, k == 1))
                th.free[b] = bc_ok = A.put(lambda e: e.activation(
                    BC[:, :, :], ps[:, :].rearrange("p (f n) -> p f n", f=2), ACT.Copy), tok)
                yield
                T.wait(loads["tri"])
                for i in range(TB):
                    ts = slice(i * P, i * P + P)
                    xt = th.cut(512).rearrange("p (f n) -> p f n", f=4)
                    Gh = th.cut(512).rearrange("p (f n) -> p f n", f=4)
                    E = cv[:, 2 * i:2 * i + 2, :].rearrange("p a (b n) -> p (a b) n", b=2)
                    cbm = th.sm(128)
                    b, ps = th.bank()
                    for f in range(4):
                        tok = T.put(lambda e: e.transpose(ps[:, f * P:f * P + P], sT[:, f, ts], ident), s_ok)
                    th.free[b] = xt_ok = A.put(lambda e: e.activation(
                        xt[:, :, :], ps[:, :].rearrange("p (f n) -> p f n", f=4), ACT.Copy), tok)
                    G.wait(dt_ok, loads["gt"])
                    for f in range(4):
                        gh = G.put(lambda e: e.tensor_scalar(Gh[:, f, :], SB["gt"][:, :],
                                                             dz[:, 6, 4 * i + f:4 * i + f + 1], None, ALU.mult))
                    b, ps2 = th.bank()
                    cb = T.put(mm(ps2[:, 0:P], BC[:, 0, ts], BC[:, 1, ts], True, True), bc_ok)
                    th.free[b] = cm = V.put(lambda e: e.tensor_tensor(cbm, ps2[:, 0:P], SB["tri"][:, :], ALU.mult),
                                            cb, loads["tri"])
                    b, ps3 = th.bank()
                    for f in range(4):
                        tok = T.put(mm(ps3[:, f * P:f * P + P], Gh[:, f, :], SB["tri"][:, :], True, True), gh)
                    th.free[b] = ex = A.put(lambda e: e.activation(
                        E, ps3[:, :].rearrange("p (f n) -> p f n", f=4), ACT.Exp), tok)
                    yield
                    for f in range(4):
                        m_ok = V.put(lambda e: e.scalar_tensor_tensor(Gh[:, f, :], E[:, f, :],
                                                                      dz[:, 5, 4 * i + f:4 * i + f + 1], cbm,
                                                                      ALU.mult, ALU.mult), ex, cm)
                    b, ps4 = th.bank()
                    for f in range(4):
                        tok = T.put(mm(ps4[:, f * P:f * P + P], xt[:, f, :], Gh[:, f, :], True, True), m_ok, xt_ok)
                    V.wait(loads["dskip"])
                    for f in range(4):
                        y = V.put(lambda e: e.scalar_tensor_tensor(xt[:, f, :], sT[:, f, ts], SB["dskip"][:, f:f + 1],
                                                                   ps4[:, f * P:f * P + P], ALU.mult, ALU.add), tok)
                    th.free[b] = y
                    y = G.put(lambda e: e.tensor_tensor(xt[:, :, :], xt[:, :, :], gT[:, :, ts], ALU.mult), y, g_ok)
                    yield
                    b, ps5 = th.bank()
                    for f in range(4):
                        tok = T.put(mm(ps5[:, 0:256], xt[:, f, :], w_out[:, f, :], f == 0, f == 3), y, loads["w_out"])
                    th.free[b] = V.put(lambda e: e.tensor_tensor(X[:, t0 + i, :], ps5[:, 0:256], X[:, t0 + i, :],
                                                                 ALU.add), tok, xa)
                th.end()

            def products(th):
                th.start()
                prev = None
                for hf in range(2):
                    if hf:
                        load_pre(1, (prev_t, prev_v, prev_a))
                    L = {n: loads[f"{n}_{hf}"] for n in ("wkcq", "wqr", "wkr", "wq", "wkc", "wo")}
                    for c in range(2):
                        b, ps = th.bank()
                        for h in range(8):
                            tok = T.put(mm(ps[0:96, h * 64:h * 64 + 64], wqr[:, h, c * 96:c * 96 + 96], wkr[:, h, :],
                                           True, True), L["wqr"], L["wkr"])
                        th.free[b] = v = V.put(lambda e: e.tensor_copy(
                            g1[:, c, :, :], ps[0:96, :].rearrange("p (h d) -> p h d", h=8)), tok)
                        yield
                    b, ps = th.bank()
                    for h in range(8):
                        for c in range(2):
                            tok = T.put(mm(ps[:, h * 64:h * 64 + 64], wkcq[:, c, h, :], g1[:, c, h, :],
                                           c == 0, c == 1), v, L["wkcq"])
                    th.free[b] = v = V.put(lambda e: e.tensor_copy(
                        g2[:, :, :], ps[:, :].rearrange("p (h d) -> p h d", h=8)), tok)
                    yield
                    for k in range(2):
                        b, ps = th.bank()
                        for h in range(8):
                            tok = T.put(mm(ps[:, h * 64:h * 64 + 64], wq[:, h, k * P:k * P + P], g2[:, h, :],
                                           True, True), v, L["wq"])
                        th.free[b] = prev_a = A.put(lambda e: e.activation(Aw[:, k, hf * 512:hf * 512 + 512], ps[:, :],
                                                                           ACT.Copy), tok)
                        yield
                    for q in range(4):
                        b, ps = th.bank()
                        for e2 in range(2):
                            tok = T.put(mm(ps[64 * e2:64 * e2 + 64, 0:256], wkc[:, 2 * q + e2, :], wo[:, 2 * q + e2, :],
                                           True, True), L["wkc"], L["wo"])
                        th.free[b] = prev_v = V.put(lambda e: e.tensor_copy(Bw[:, 4 * hf + q, :], ps[:, 0:256]), tok)
                        prev_t = tok
                        yield
                th.pre = (prev_t, prev_v, prev_a)
                pre_done.extend(th.pre)
                th.end()

            pre_done = []

            def ctx_rows(th, blk, dst):
                s = th.csem
                th.cn += 2
                for e2 in range(2):
                    S.dma(lambda e: e.dma_start(dst[64 * e2:64 * e2 + 64, :, :],
                                                        t["ctx"][NB * blk:NB * blk + NB, :, :].rearrange("b l d -> l b d")),
                      s)
                return (s, 16 * th.cn)

            def row_softmax(th, src, dst, mxs, sms, groups, tok, scale=1.0, n=64):
                v = V.put(lambda e: e.tensor_reduce(mxs, src, AX, ALU.max), tok)
                free = v = V.put(lambda e: e.tensor_tensor(dst, src, mxs.unsqueeze(2).broadcast_to([P, groups, n]),
                                                           ALU.subtract), v)
                a = A.put(lambda e: e.activation(dst, dst, ACT.Exp, scale=scale), v)
                v = V.put(lambda e: e.tensor_reduce(sms, dst, AX, ALU.add), a)
                return free, V.put(lambda e: e.reciprocal(sms, sms), v)

            def stage2(th, blk):
                th.start()
                t0 = blk * TB
                h = th.cut(512).rearrange("p (t c) -> p t c", t=TB)
                hT = th.cut(512).rearrange("p (k n) -> p k n", k=2)
                qT = th.cut(2048).rearrange("p (h n) -> p h n", h=8)
                CT = th.cut(256).rearrange("p (b d) -> p b d", b=NB)
                R1 = th.cut(256).rearrange("p (b d) -> p b d", b=NB)
                R2 = th.cut(256).rearrange("p (b d) -> p b d", b=NB)
                BD = th.cut(512).rearrange("p (b d) -> p b d", b=NB)
                BDT = th.cut(512).rearrange("p (b d) -> p b d", b=NB)
                Pm = th.cut(1024).rearrange("p (h n) -> p h n", h=8)
                PT = th.cut(1024).rearrange("p (h n) -> p h n", h=8)
                cT = hT
                ct = ctx_rows(th, blk, CT)
                z = G.put(lambda e: e.memset(BD[:, :, :], 0.0))
                hn = norm(th, blk, lambda i, x: [(h[:, i, :], x)])
                cosb = SB["cos"][:, :].unsqueeze(1).broadcast_to([P, NB, 64])
                r1 = G.put(lambda e: e.tensor_tensor(R1[:, :, :], CT[:, :, :], cosb, ALU.mult), ct, loads["cos"], loads["sin"])
                for a0 in range(2):
                    r1 = G.put(lambda e: e.tensor_tensor(
                        R2[:, :, 32 * a0:32 * a0 + 32], CT[:, :, 32 - 32 * a0:64 - 32 * a0],
                        SB["sin"][:, 32 * a0:32 * a0 + 32].unsqueeze(1).broadcast_to([P, NB, 32]), ALU.mult))
                for e2 in range(2):
                    rows = slice(64 * e2, 64 * e2 + 64)
                    kv = V.put(lambda e: e.tensor_tensor(BD[rows, :, rows], R1[rows, :, :], R2[rows, :, :], ALU.add),
                               r1, z)
                yield
                ht = turned(th, h, hn, hT[:, :, :])
                b, ps = th.bank()
                for j in range(NB):
                    tok = T.put(lambda e: e.transpose(ps[:, j * P:j * P + P], BD[:, j, :], ident), kv)
                th.free[b] = kt = A.put(lambda e: e.activation(BDT[:, :, :], ps[:, :].rearrange("p (b n) -> p b n", b=NB),
                                                               ACT.Copy), tok)
                yield
                T.wait(*pre_done)
                for g in range(4):
                    b, ps = th.bank()
                    for f in range(2):
                        hp = 2 * g + f
                        for k in range(2):
                            tok = T.put(mm(ps[:, f * 256:f * 256 + 256], Aw[:, k, hp * P:hp * P + P], hT[:, k, :],
                                           k == 0, k == 1), ht)
                    th.free[b] = qk = A.put(lambda e: e.activation(
                        qT[:, 2 * g:2 * g + 2, :], ps[:, :].rearrange("p (f n) -> p f n", f=2), ACT.Copy), tok)
                    yield
                pv_read = (T.sem, 0)
                for i in range(TB):
                    mxs = th.sm(16)
                    sms = th.sm(16)
                    for g in range(2):
                        b, ps = th.bank()
                        for b2 in range(2):
                            for q in range(4):
                                tok = T.put(mm(ps[64 * b2:64 * b2 + 64, q * P:q * P + P],
                                               qT[:, 4 * g + q, i * P + 64 * b2:i * P + 64 * b2 + 64],
                                               BDT[:, 2 * i + b2, :], True, True), qk, kt)
                        dst = Pm[:, 4 * g:4 * g + 4, :].rearrange("p h (e l) -> p (h e) l", e=2)
                        V.wait(pv_read)
                        fr, v = row_softmax(th, ps[:, :].rearrange("p (h l) -> p h l", h=8), dst,
                                            mxs[:, 8 * g:8 * g + 8], sms[:, 8 * g:8 * g + 8], 8, tok)
                        th.free[b] = fr
                        p_ok = G.put(lambda e: e.tensor_tensor(
                            dst, dst, sms[:, 8 * g:8 * g + 8].unsqueeze(2).broadcast_to([P, 8, 64]), ALU.mult), v)
                        yield
                        b, ps = th.bank()
                        for q in range(4):
                            tok = T.put(lambda e: e.transpose(ps[:, q * P:q * P + P], Pm[:, 4 * g + q, :], ident), p_ok)
                        A.wait(pv_read)
                        th.free[b] = pt = A.put(lambda e: e.activation(
                            PT[:, 4 * g:4 * g + 4, :], ps[:, :].rearrange("p (h n) -> p h n", h=4), ACT.Copy), tok)
                    cT = qT[:, :, i * P:i * P + P]
                    yield
                    for b2 in range(2):
                        b, ps = th.bank()
                        tok = T.put(mm(ps[:, :], BD[:, 2 * i + b2, :], PT[:, :, 64 * b2:64 * b2 + 64], True, True), pt)
                        th.free[b] = cx = A.put(lambda e: e.activation(
                            cT[:, :, 64 * b2:64 * b2 + 64], ps[:, :].rearrange("p (h n) -> p h n", h=8), ACT.Copy), tok)
                    pv_read = tok
                    yield
                    b, ps = th.bank()
                    for q in range(8):
                        tok = T.put(mm(ps[:, 0:256], cT[:, q, :], Bw[:, q, :], q == 0, q == 7), cx)
                    th.free[b] = V.put(lambda e: e.tensor_tensor(X[:, t0 + i, :], ps[:, 0:256], X[:, t0 + i, :],
                                                                 ALU.add), tok)
                th.end()

            def load_moe():
                w = tuple(pre_done)
                load("moe_r", moe_r, t["moe_r"], w)
                load("moe_b", moe_b, t["moe_b"], w)
                load("bdn", bdn[:, :], t["bdn"], w)
                for e in range(8):
                    load(f"moe{e}", BIG[:, 0:12288].rearrange("p (a e n) -> p a e n", a=3, e=8)[:, :, e, :],
                         t["moe_w"][:, e, :].rearrange("p (a n) -> p a n", a=3), w)

            def stage3(th, blk):
                th.start()
                t0 = blk * TB
                h = th.cut(512).rearrange("p (t c) -> p t c", t=TB)
                hT = th.cut(512).rearrange("p (k n) -> p k n", k=2)
                U = [th.cut(512).rearrange("p (k n) -> p k n", k=2) for _ in range(2)]
                Z = [th.cut(512).rearrange("p (k n) -> p k n", k=2) for _ in range(2)]
                pT = th.cut(256, 8)
                hn = norm(th, blk, lambda i, x: [(h[:, i, :], x)])
                yield
                ht = turned(th, h, hn, hT[:, :, :])
                yield
                b, ps = th.bank()
                for i in range(TB):
                    for k in range(2):
                        tok = T.put(mm(ps[:, 8 * i:8 * i + 7], hT[:, k, i * P:i * P + P], moe_r[:, k, :],
                                       k == 0, k == 1), ht, loads["moe_r"])
                r = lambda n: th.sm(TB * n).rearrange("p (t n) -> p t n", t=TB)
                gl, W, W2, t8, ms, t2, gm, pr, mx, sm = (r(7), r(13), r(13), r(8), r(7), r(7), r(7), r(8), r(1), r(1))
                z = G.put(lambda e: e.memset(W[:, :, 7:13], 3.0e38))
                z = G.put(lambda e: e.memset(pr[:, :, 7:8], 1.0))
                bc = lambda n: SB[n][:, :].unsqueeze(1).broadcast_to([P, TB, 7])
                th.free[b] = v = V.put(lambda e: e.tensor_tensor(
                    gl[:, :, :], ps[:, 0:16].rearrange("p (t n) -> p t n", t=TB)[:, :, 0:7], bc("rb"), ALU.add),
                    tok, loads["rb"], loads["gb"])
                v = V.put(lambda e: e.tensor_tensor(W[:, :, 0:7], gl[:, :, :], bc("gb"), ALU.add), v, z)
                for i in range(TB):
                    v1 = V.put(lambda e: e.max(t8[:, i, :], W[:, i, :]), v)
                    v1 = V.put(lambda e: e.match_replace(W2[:, i, :], t8[:, i, :], W[:, i, :], -3.3e38), v1)
                v = V.put(lambda e: e.tensor_tensor(ms[:, :, :], W2[:, :, 0:7], W[:, :, 0:7], ALU.not_equal), v1)
                v = V.put(lambda e: e.tensor_scalar(t2[:, :, :], ms[:, :, :], 1e30, -1e30, ALU.mult, ALU.add), v)
                v = V.put(lambda e: e.tensor_tensor(gm[:, :, :], gl[:, :, :], ms[:, :, :], ALU.mult), v)
                v = V.put(lambda e: e.tensor_tensor(gm[:, :, :], gm[:, :, :], t2[:, :, :], ALU.add), v)
                v = V.put(lambda e: e.tensor_reduce(mx[:, :, 0], gm[:, :, :], AX, ALU.max), v)
                v = V.put(lambda e: e.tensor_tensor(gm[:, :, :], gm[:, :, :], mx[:, :, :].broadcast_to([P, TB, 7]),
                                                    ALU.subtract), v)
                a = A.put(lambda e: e.activation(gm[:, :, :], gm[:, :, :], ACT.Exp), v)
                v = V.put(lambda e: e.tensor_reduce(sm[:, :, 0], gm[:, :, :], AX, ALU.add), a)
                v = V.put(lambda e: e.reciprocal(sm[:, :, :], sm[:, :, :]), v)
                prob = V.put(lambda e: e.tensor_tensor(pr[:, :, 0:7], gm[:, :, :], sm[:, :, :].broadcast_to([P, TB, 7]),
                                                       ALU.mult), v)
                yield
                ups, downs = {}, [(T.sem, 0)] * 2
                zfree = [(T.sem, 0)] * 2

                def up(x):
                    b, ps = th.bank()
                    for f in range(2):
                        for k in range(2):
                            tok = T.put(mm(ps[:, f * 256:f * 256 + 256], UP[:, x, k, f * P:f * P + P], hT[:, k, :],
                                           k == 0, k == 1), ht, loads[f"moe{x}"])
                    A.wait(loads["moe_b"], zfree[x % 2])
                    for f in range(2):
                        a = A.put(lambda e: e.activation(U[x % 2][:, f, :], ps[:, f * 256:f * 256 + 256], ACT.Identity,
                                                         bias=moe_b[:, 0, x, f:f + 1]), tok)
                    th.free[b] = ups[x] = a

                up(7)
                yield
                order = [7, 0, 1, 2, 3, 4, 5, 6]
                U_of = {}
                for n, x in enumerate(order):
                    b, ps = th.bank()
                    u = U[x % 2]
                    for f in range(2):
                        for k in range(2):
                            tok = T.put(mm(ps[:, f * 256:f * 256 + 256], UG[:, x, k, f * P:f * P + P], u[:, k, :],
                                           k == 0, k == 1), ups[x])
                    zz = Z[n % 2]
                    A.wait(downs[n % 2])
                    for f in range(2):
                        a = A.put(lambda e: e.activation(zz[:, f, :], ps[:, f * 256:f * 256 + 256], ACT.Silu,
                                                         bias=moe_b[:, 1, x, f:f + 1]), tok)
                    th.free[b] = a
                    zfree[x % 2] = zr = G.put(lambda e: e.tensor_tensor(zz[:, :, :], zz[:, :, :], u[:, :, :], ALU.mult), a)
                    if n < 7:
                        up(order[n + 1])
                    yield
                    if n == 1:
                        b, ps = th.bank()
                        for i in range(TB):
                            tok = T.put(lambda e: e.transpose(ps[0:8, i * P:i * P + P], pr[:, i, :], ident), prob)
                        th.free[b] = pt = V.put(lambda e: e.tensor_copy(pT, ps[0:8, 0:256]), tok)
                    b, ps = th.bank()
                    for i in range(TB):
                        for k in range(2):
                            last = k == 1 and n != 2
                            tok = T.put(mm(ps[:, i * 256:i * 256 + 256], zz[:, k, i * P:i * P + P], UD[:, x, k, :],
                                           k == 0, last), zr)
                    downs[n % 2] = tok
                    if n == 0:
                        for i in range(TB):
                            v = V.put(lambda e: e.tensor_tensor(X[:, t0 + i, :], ps[:, i * 256:i * 256 + 256],
                                                                X[:, t0 + i, :], ALU.add), tok)
                    else:
                        for i in range(TB):
                            v = V.put(lambda e: e.scalar_tensor_tensor(
                                X[:, t0 + i, :], ps[:, i * 256:i * 256 + 256], pr[:, i, x:x + 1], X[:, t0 + i, :],
                                ALU.mult, ALU.add), tok, prob, (V.sem, V.n))
                    th.free[b] = v
                    yield
                b, ps = th.bank()
                for i in range(TB):
                    tok = T.put(mm(ps[:, i * 256:i * 256 + 256], pT[:, i * P:i * P + P], bdn[:, :], True, True),
                                pt, loads["bdn"])
                th.free[b] = V.put(lambda e: e.tensor_tensor(
                    X[:, t0:t0 + TB, :], ps[:, :].rearrange("p (t n) -> p t n", t=TB), X[:, t0:t0 + TB, :], ALU.add),
                    tok, (V.sem, V.n))
                th.end()
                moe_last[blk] = list(th.done)

            moe_last = {}

            def stage4(th, blk):
                th.start()
                t0 = blk * TB
                h = th.cut(512).rearrange("p (t c) -> p t c", t=TB)
                pad = lambda: th.cut(2 * NB * 65)
                flat = {}

                def p4(n):
                    flat[n] = pad()
                    return flat[n].rearrange("p (k b s) -> p k b s", k=2, b=NB)

                f4 = lambda: th.cut(512).rearrange("p (k b s) -> p k b s", k=2, b=NB)
                H = p4("H")
                mx = [f4() for _ in range(3)]
                K, MX, E1, E2, GV = (p4(n) for n in ("K", "MX", "E1", "E2", "GV"))
                Vv, C, D = f4(), f4(), f4()
                for n, w, val in (("H", H, 0.0), ("K", K, NEG), ("E1", E1, 0.0), ("E2", E2, 0.0), ("GV", GV, 0.0)):
                    z = G.put(lambda e, w=w, val=val: e.memset(w[:, :, :, 0:1], val))
                hn = norm(th, blk, lambda i, x: [(h[:, i, :], x)])
                yield
                A.wait(z)
                ht = turned(th, h, hn, H[:, :, :, 1:65])
                yield
                for m in range(3):
                    for k in range(2):
                        g = G.put(lambda e: e.tensor_scalar(mx[m][:, k, :, :], H[:, k, :, 0:64], omx[:, m, k:k + 1], None,
                                                            ALU.mult), ht, om_ok)
                        mok = V.put(lambda e: e.scalar_tensor_tensor(mx[m][:, k, :, :], H[:, k, :, 1:65],
                                                                     mix[:, m, k:k + 1], mx[m][:, k, :, :],
                                                                     ALU.mult, ALU.add), g)
                    b, ps = th.bank()
                    for f in range(2):
                        for k in range(2):
                            tok = T.put(mm(ps[:, f * 256:f * 256 + 256], kvro[:, m, k, f * P:f * P + P],
                                           mx[m][:, k, :, :], k == 0, k == 1), mok, loads["w_kvro"])
                    src = ps[:, :].rearrange("p (k b s) -> p k b s", k=2, b=NB)
                    if m == 0:
                        kok = A.put(lambda e: e.activation(K[:, :, :, 1:65], src, ACT.Copy), tok)
                    elif m == 1:
                        vok = kok = A.put(lambda e: e.activation(Vv[:, :, :, :], src, ACT.Copy), tok)
                    else:
                        rok = kok = A.put(lambda e: e.activation(mx[0][:, :, :, :], src, ACT.Exp, scale=-1.0), tok)
                    th.free[b] = kok
                    if m == 0:
                        k1 = kok
                    yield
                pv, cu = slice(0, 64), slice(1, 65)
                v = V.put(lambda e: e.tensor_tensor_scan(flat["MX"], td65[:, :], flat["K"], NEG, ALU.add, ALU.max),
                          k1, td_ok)
                mxo = v
                for k in range(2):
                    e1 = V.put(lambda e: e.scalar_tensor_tensor(E1[:, k, :, cu], MX[:, k, :, pv], tdn[:, k:k + 1],
                                                                MX[:, k, :, cu], ALU.add, ALU.subtract), mxo)
                ee1 = A.put(lambda e: e.activation(E1[:, :, :, cu], E1[:, :, :, cu], ACT.Exp), e1)
                g = G.put(lambda e: e.tensor_tensor(E2[:, :, :, cu], K[:, :, :, cu], MX[:, :, :, cu], ALU.subtract), mxo)
                ee2 = A.put(lambda e: e.activation(E2[:, :, :, cu], E2[:, :, :, cu], ACT.Exp), g)
                yield
                for k in range(2):
                    c = V.put(lambda e: e.scalar_tensor_tensor(C[:, k, :, :], K[:, k, :, cu], tfn[:, k:k + 1],
                                                               MX[:, k, :, pv], ALU.add, ALU.max))
                for k in range(2):
                    d = V.put(lambda e: e.scalar_tensor_tensor(D[:, k, :, :], K[:, k, :, cu], tfn[:, k:k + 1],
                                                               C[:, k, :, :], ALU.add, ALU.subtract), c)
                g = G.put(lambda e: e.tensor_tensor(C[:, :, :, :], MX[:, :, :, pv], C[:, :, :, :], ALU.subtract), d)
                e2 = A.put(lambda e: e.activation(D[:, :, :, :], D[:, :, :, :], ACT.Exp), d)
                e1 = A.put(lambda e: e.activation(C[:, :, :, :], C[:, :, :, :], ACT.Exp), g)
                gv = G.put(lambda e: e.tensor_tensor(GV[:, :, :, cu], E2[:, :, :, cu], Vv[:, :, :, :], ALU.mult), ee2, vok)
                den = V.put(lambda e: e.tensor_tensor_scan(flat["H"], flat["E1"], flat["E2"], 0.0, ALU.mult, ALU.add),
                            ee1, ee2)
                num = V.put(lambda e: e.tensor_tensor_scan(flat["MX"], flat["E1"], flat["GV"], 0.0, ALU.mult, ALU.add),
                            gv, g)
                yield
                o1 = V.put(lambda e: e.tensor_tensor(mx[1][:, :, :, :], C[:, :, :, :], MX[:, :, :, pv], ALU.mult), e1, num)
                o2 = G.put(lambda e: e.tensor_tensor(Vv[:, :, :, :], D[:, :, :, :], Vv[:, :, :, :], ALU.mult), e2)
                o3 = G.put(lambda e: e.tensor_tensor(mx[1][:, :, :, :], mx[1][:, :, :, :], Vv[:, :, :, :], ALU.add), o1, o2)
                d1 = V.put(lambda e: e.tensor_tensor(mx[2][:, :, :, :], C[:, :, :, :], H[:, :, :, pv], ALU.mult), den)
                d1 = V.put(lambda e: e.tensor_tensor(mx[2][:, :, :, :], mx[2][:, :, :, :], D[:, :, :, :], ALU.add), d1, e2)
                fl = lambda a: a.rearrange("p k b s -> p (k b s)")
                d1 = V.put(lambda e: e.scalar_tensor_tensor(fl(mx[2]), fl(mx[0]), 1.0, fl(mx[2]), ALU.add, ALU.mult),
                           d1, rok)
                d1 = V.put(lambda e: e.reciprocal(fl(mx[2]), fl(mx[2])), d1)
                yield
                oo = V.put(lambda e: e.tensor_tensor(fl(mx[1]), fl(mx[1]), fl(mx[2]), ALU.mult), d1, o3)
                oT = mx[1].rearrange("p k b s -> p k (b s)")
                b, ps = th.bank()
                for i in range(TB):
                    for k in range(2):
                        tok = T.put(mm(ps[:, i * 256:i * 256 + 256], oT[:, k, i * P:i * P + P], kvro[:, 3, k, :],
                                       k == 0, k == 1), oo)
                th.free[b] = V.put(lambda e: e.tensor_tensor(
                    X[:, t0:t0 + TB, :], ps[:, :].rearrange("p (t n) -> p t n", t=TB), X[:, t0:t0 + TB, :], ALU.add), tok)
                th.end()

            def stage5(th, blk):
                th.start()
                t0 = blk * TB
                hq = th.cut(1024).rearrange("p (t g a kd) -> p t g a kd", t=TB, g=4, a=2)
                QB = th.cut(1024).rearrange("p (t g n) -> p t g n", t=TB, g=4)
                CT = th.cut(256).rearrange("p (b d) -> p b d", b=NB)
                CK = th.cut(128).rearrange("p (t l) -> p t l", t=TB)
                BK = th.cut(1024).rearrange("p (t k l) -> p t k l", t=TB, k=8)
                BV = th.cut(256).rearrange("p (b d) -> p b d", b=NB)
                Pm = [th.cut(512).rearrange("p (k l) -> p k l", k=8) for _ in range(2)]
                PT = [th.cut(512).rearrange("p (k l) -> p k l", k=4) for _ in range(2)]
                O = th.cut(512).rearrange("p (t c) -> p t c", t=TB)
                ct = ctx_rows(th, blk, CT)
                th.cn += 1
                S.dma(lambda e: e.dma_start(CK[:, :, :], t["ctxT"][t0:t0 + TB, :, :].rearrange("t p l -> p t l")),
                      th.csem)
                ct = (th.csem, 16 * th.cn)
                z = G.put(lambda e: e.memset(QB[:, :, :, :], 0.0))
                mk = SB["mk"][:, :].unsqueeze(2).broadcast_to([P, 8, 64])
                G.wait(loads["mk"], loads["mv"])
                for i in range(TB):
                    bk = G.put(lambda e: e.tensor_tensor(BK[:, i, :, :], CK[:, i, :].unsqueeze(1).broadcast_to([P, 8, 64]),
                                                         mk, ALU.mult), ct)
                bv = G.put(lambda e: e.tensor_tensor(BV[:, :, :], CT[:, :, :],
                                                     SB["mv"][:, :].unsqueeze(1).broadcast_to([P, NB, 64]), ALU.mult))

                def views(i, x):
                    x = None if x is None else x.rearrange("p (k g d) -> p g k d", k=8, g=4)
                    return [(hq[:, i, :, a, :].rearrange("p g (k d) -> p g k d", k=8), x) for a in range(2)]

                hn = norm(th, blk, views)
                yield
                for i in range(TB):
                    b, ps = th.bank()
                    for g in range(4):
                        tok = T.put(lambda e: e.transpose(ps[:, g * P:g * P + P],
                                                          hq[:, i, g, :, :].rearrange("p a n -> p (a n)"), ident), hn)
                    for e2 in range(2):
                        rows = slice(64 * e2, 64 * e2 + 64)
                        qb = A.put(lambda e: e.activation(
                            QB[rows, i, :, rows], ps[:, :].rearrange("p (g n) -> p g n", g=4)[rows, :, rows], ACT.Copy),
                            tok, z)
                    th.free[b] = qb
                yield
                ptr = [(T.sem, 0)] * 2
                for i in range(TB):
                    mxs = th.sm(32).rearrange("p (g k) -> p g k", g=4)
                    sms = th.sm(32).rearrange("p (g k) -> p g k", g=4)
                    ob = 3
                    opend = []
                    pvs = []
                    Ps = [None] * 4
                    ptoks = {}

                    def scores(g):
                        b, ps = th.bank3()
                        tok = T.put(mm(ps[:, :], QB[:, i, g, :], BK[:, i, :, :], True, True), qb, bk)
                        V.wait(th.tr[g % 2])
                        fr, v = row_softmax(th, ps[:, :].rearrange("p (k l) -> p k l", k=8), Pm[g % 2][:, :, :],
                                            mxs[:, g, :], sms[:, g, :], 8, tok, scale=8.0 ** -0.5)
                        th.free[b] = fr
                        ptoks[g] = v

                    def turn(g):
                        b, ps = th.bank3()
                        for q in range(4):
                            tok = T.put(lambda e: e.transpose(ps[:, q * P:q * P + P],
                                                              Pm[g % 2][:, 2 * q:2 * q + 2, :]
                                                              .rearrange("p k l -> p (k l)"), ident), ptoks[g])
                        th.tr[g % 2] = tok
                        A.wait(ptr[g % 2])
                        th.free[b] = pt = A.put(lambda e: e.activation(
                            PT[g % 2][:, :, :], ps[:, :].rearrange("p (k l) -> p k l", k=4), ACT.Copy), tok)
                        return pt

                    def values(g, pt):
                        ops = banks[4 * th.i + 3][:, :].rearrange("p (b n) -> p b n", b=2)
                        for q in range(4):
                            c0 = g * 64 + q * 16
                            tok = T.put(mm(ops[:, :, c0:c0 + 16], PT[g % 2][:, q, :],
                                           BV[:, 2 * i:2 * i + 2, 16 * q:16 * q + 16], True, True), pt, bv)
                        ptr[g % 2] = tok
                        return tok

                    T.wait(th.free[3])
                    scores(0)
                    yield
                    for g in range(4):
                        if g < 3:
                            scores(g + 1)
                        yield
                        pt = turn(g)
                        yield
                        tok = values(g, pt)
                    for b2 in range(2):
                        rows = slice(64 * b2, 64 * b2 + 64)
                        ops = banks[4 * th.i + 3][:, :].rearrange("p (b n) -> p b n", b=2)
                        v = V.put(lambda e: e.tensor_tensor(
                            O[rows, i, :].rearrange("p (k g d) -> p g k d", k=8, g=4),
                            ops[rows, b2, :].rearrange("p (g k d) -> p g k d", g=4, k=8),
                            sms[rows, :, :].unsqueeze(3).broadcast_to([64, 4, 8, 8]), ALU.mult), tok, ptoks[3])
                    th.free[3] = v
                    G.put(lambda e: e.tensor_tensor(X[:, t0 + i, :], X[:, t0 + i, :], O[:, i, :], ALU.add), v)
                th.end()

            def load_ffn():
                w = tuple(x for blk in range(NBLK - NTH, NBLK) for x in moe_last[blk])
                load("WG", WG, t["wg"].rearrange("p (k n) -> p k n", k=2), w)
                load("MW", MW, t["mw"].rearrange("p (k n) -> p k n", k=2), w)
                load("GW", GW, t["gw"].rearrange("p (k n) -> p k n", k=2), w)
                load("WD", WD, t["wd"].rearrange("p (k n) -> p k n", k=11), w)

            def prep_ffn(th):
                th.start()
                f = th.cut(256, 64).rearrange("p (a n) -> p a n", a=4)
                v = V.put(lambda e: e.tensor_copy(f[:, 0, :], invt[:, :]), loads["invt"])
                v = V.put(lambda e: e.tensor_scalar(f[:, 1, :], f[:, 0, :], 0.0, 64.0, ALU.is_lt, ALU.mult), v)
                v = V.put(lambda e: e.tensor_tensor(f[:, 2, :], f[:, 0, :], f[:, 1, :], ALU.add), v)
                v = V.put(lambda e: e.tensor_scalar(f[:, 3, :], f[:, 2, :], 0.0, 63.0, ALU.max, ALU.min), v)
                pm = V.put(lambda e: e.tensor_scalar(PM, f[:, 3, :], SB["eid"][0:64, 0:1], None, ALU.is_equal),
                           v, loads["eid"], *[x for blk in range(NBLK - NTH, NBLK) for x in moe_last[blk]])
                for g in range(8):
                    b, ps = th.bank()
                    for k in range(2):
                        tok = T.put(mm(ps[0:64, 0:352], MW[:, k, :], WG[:, k, g * 352:g * 352 + 352], k == 0, k == 1),
                                    loads["MW"], loads["WG"])
                    th.free[b] = v = V.put(lambda e: e.tensor_scalar(MG[:, g * 352:g * 352 + 352], ps[0:64, 0:352],
                                                                     SB["mg"][0:64, g:g + 1], None, ALU.mult),
                                           tok, loads["mg"])
                    yield
                ffn_ok.extend((pm, v))
                th.end()

            ffn_ok = []

            def stage6(th, blk):
                th.start()
                t0 = blk * TB
                h = th.cut(512).rearrange("p (t c) -> p t c", t=TB)
                hT = th.cut(512).rearrange("p (k n) -> p k n", k=2)
                r = lambda n: th.cut(TB * n).rearrange("p (t n) -> p t n", t=TB)
                sc, we, t8 = r(64), r(64), r(8)
                mx = th.sm(32)
                weT = th.cut(256, 64)
                soT = th.cut(256, 64)
                s8 = th.cut(8 * 16).rearrange("p (a t g) -> p a t g", a=8, t=TB)
                fl, nz = r(64), r(64)
                sg = th.cut(2 * 176).rearrange("p (a n) -> p a n", a=2)
                AG = th.cut(1408)
                AT = th.cut(1408).rearrange("p (k n) -> p k n", k=11)
                hn = norm(th, blk, lambda i, x: [(h[:, i, :], x)])
                yield
                ht = turned(th, h, hn, hT[:, :, :])
                yield
                b, ps = th.bank()
                for i in range(TB):
                    for k in range(2):
                        tok = T.put(mm(ps[:, 64 * i:64 * i + 64], hT[:, k, i * P:i * P + P], GW[:, k, :],
                                       k == 0, k == 1), ht, loads["GW"])
                fr, v = row_softmax(th, ps[:, 0:128].rearrange("p (t n) -> p t n", t=TB), sc[:, :, :], mx[:, 0:2],
                                    mx[:, 2:4], TB, tok)
                th.free[b] = fr
                v = V.put(lambda e: e.tensor_tensor(sc[:, :, :], sc[:, :, :],
                                                    mx[:, 2:4].unsqueeze(2).broadcast_to([P, TB, 64]), ALU.mult), v)
                for i in range(TB):
                    v1 = V.put(lambda e: e.max(t8[:, i, :], sc[:, i, :]), v)
                    v1 = V.put(lambda e: e.match_replace(we[:, i, :], t8[:, i, :], sc[:, i, :], 0.0), v1)
                v = V.put(lambda e: e.tensor_tensor(we[:, :, :], sc[:, :, :], we[:, :, :], ALU.subtract), v1)
                yield
                b, ps = th.bank()
                for i in range(TB):
                    tok = T.put(lambda e: e.transpose(ps[0:64, i * P:i * P + P], we[:, i, :], ident), v)
                th.free[b] = v = V.put(lambda e: e.tensor_copy(weT, ps[0:64, 0:256]), tok)
                yield
                b, ps = th.bank()
                T.wait(*ffn_ok)
                for i in range(TB):
                    tok = T.put(mm(ps[:, 64 * i:64 * i + 64], weT[:, i * P:i * P + P], PM, True, True), v)
                f3 = ps[:, 0:128].rearrange("p (a i) -> p a i", i=8)
                s2 = lambda n: s8[:, n, :, :].rearrange("p t g -> p (t g)")
                g3 = lambda w: w[:, :, :].rearrange("p t (g i) -> p (t g) i", i=8)
                s_ok = V.put(lambda e: e.tensor_reduce(s2(0), f3, AX, ALU.add), tok)
                v = V.put(lambda e: e.tensor_scalar(g3(nz), f3, 0.0, -1e9, ALU.is_equal, ALU.mult))
                th.free[b] = v = V.put(lambda e: e.tensor_tensor(g3(fl), f3, g3(nz), ALU.add), v)
                v = V.put(lambda e: e.tensor_reduce(s2(1), g3(fl), AX, ALU.max), v)
                bc = lambda n: s2(n).unsqueeze(2).broadcast_to([P, TB * 8, 8])
                v = V.put(lambda e: e.tensor_tensor(g3(fl), g3(fl), bc(1), ALU.subtract), v)
                a = A.put(lambda e: e.activation(fl[:, :, :], fl[:, :, :], ACT.Exp), v)
                v = V.put(lambda e: e.tensor_reduce(s2(2), g3(fl), AX, ALU.add), a)
                v = V.put(lambda e: e.reciprocal(s2(3), s2(2)), v)
                v = V.put(lambda e: e.tensor_tensor(g3(fl), g3(fl), bc(3), ALU.mult), v)
                yield
                b, ps = th.bank()
                for i in range(TB):
                    tok = T.put(lambda e: e.transpose(ps[0:64, i * P:i * P + P], fl[:, i, :], ident), v)
                th.free[b] = so = V.put(lambda e: e.tensor_copy(soT, ps[0:64, 0:256]), tok)
                yield
                atr = (T.sem, 0)
                sgr = [(V.sem, 0)] * 2
                agr = (T.sem, 0)
                fin = []
                for i in range(TB):
                    ts = slice(i * P, i * P + P)
                    for g in range(8):
                        b, ps = th.bank()
                        gs = slice(g * 352, g * 352 + 352)
                        for k in range(2):
                            T.put(mm(ps[:, 0:352], hT[:, k, ts], WG[:, k, gs], k == 0, False))
                        tok = T.put(mm(ps[:, 0:352], soT[:, ts], MG[:, gs], False, True), so)
                        a = A.put(lambda e: e.activation(sg[:, g % 2, :], ps[:, 0:176], ACT.Silu), tok, sgr[g % 2])
                        V.wait(agr)
                        th.free[b] = sgr[g % 2] = v = V.put(lambda e: e.scalar_tensor_tensor(
                            AG[:, g * 176:g * 176 + 176], sg[:, g % 2, :], s8[:, 0, i, g:g + 1], ps[:, 176:352],
                            ALU.mult, ALU.mult), a, s_ok)
                        yield
                    for c in range(3):
                        b, ps = th.bank()
                        n = min(4, 11 - 4 * c)
                        for q in range(n):
                            c0 = (4 * c + q) * P
                            tok = T.put(lambda e: e.transpose(ps[:, q * P:q * P + P], AG[:, c0:c0 + P], ident), v)
                        th.free[b] = at = A.put(lambda e: e.activation(
                            AT[:, 4 * c:4 * c + n, :], ps[:, 0:n * P].rearrange("p (k n) -> p k n", k=n), ACT.Copy),
                            tok, atr)
                    agr = tok
                    yield
                    b, ps = th.bank()
                    for q in range(11):
                        tok = T.put(mm(ps[:, 0:256], AT[:, q, :], WD[:, q, :], q == 0, q == 10), at, loads["WD"])
                    atr = tok
                    th.free[b] = v = V.put(lambda e: e.tensor_tensor(X[:, t0 + i, :], ps[:, 0:256], X[:, t0 + i, :],
                                                                     ALU.add), tok)
                    S.wait(v)
                    S.dma(lambda e: e.dma_start(out[(t0 + i) * P:(t0 + i) * P + P, :], X[:, t0 + i, :]),
                      s_out)
                th.end()

            s_out = sem("s_out")
            for th in threads:
                th.csem, th.cn = sem(f"s_ctx{th.i}"), 0
                th.tr = [(T.sem, 0)] * 2

                def bank3(th=th):
                    b = th.at % 3
                    th.at += 1
                    T.wait(th.free[b])
                    return b, banks[4 * th.i + b]
                th.bank3 = bank3

            def run(jobs):
                live = [None] * NTH
                jobs = list(jobs)
                while jobs or any(live):
                    for th in threads:
                        if live[th.i] is None and jobs:
                            live[th.i] = jobs.pop(0)(th)
                        if live[th.i] is not None:
                            try:
                                next(live[th.i])
                            except StopIteration:
                                live[th.i] = None

            job = lambda f, blk: (lambda th: f(th, blk))
            run([job(stage1, 0), job(stage1, 1), products] + [job(stage1, b) for b in range(2, NBLK)])
            load_moe()
            om_ok = V.put(lambda e: e.tensor_scalar(om[:, :], SB["mix"][:, :], -1.0, 1.0, ALU.mult, ALU.add), loads["mix"])
            tdn, tfn = acst[:, 16:18], SB["tdf"][:, 2:4]
            a = A.put(lambda e: e.activation(acst[:, 12:14], tdf[:, 0:2], ACT.Exp), loads["tdf"])
            v = V.put(lambda e: e.tensor_scalar(tdn, acst[:, 12:14], -1.0, None, ALU.mult), a)
            z = G.put(lambda e: e.memset(td65[:, :], 0.0))
            for k in range(2):
                v = V.put(lambda e: e.tensor_scalar(td65v[:, k, :, 1:65], td65v[:, k, :, 1:65], tdn[:, k:k + 1], None,
                                                    ALU.add), v, z)
            td_ok = G.put(lambda e: e.memset(td65v[:, :, :, 0:1], NEG), v)
            run([job(stage2, b) for b in range(NBLK)])
            run([job(stage3, b) for b in range(NBLK)])
            load_ffn()
            run([job(stage4, b) for b in range(NBLK)])
            run([prep_ffn] + [job(stage5, b) for b in range(NBLK)])
            run([job(stage6, b) for b in range(NBLK)])
            S.wait((s_out, 16 * NT))


        program("", None)
        block = ctx.enter_context(nc.Block())

        @block.sync
        def _(eng):
            program("sp", eng)

        @block.tensor
        def _(eng):
            program("pe", eng)

        @block.vector
        def _(eng):
            program("dve", eng)

        @block.scalar
        def _(eng):
            program("act", eng)

        @block.gpsimd
        def _(eng):
            program("pool", eng)


def constants():
    i = np.arange(128)
    same = (i[:, None] // 64) == (i[None, :] // 64)
    f = np.float32
    inv = (f(1.0) / np.power(f(10000.0), np.arange(0, 64, 2, dtype=f) / f(64))).astype(f)
    fr = np.arange(64, dtype=f)[:, None] * inv[None, :]
    s, c = np.repeat(np.sin(fr), 2, axis=-1).astype(f), np.repeat(np.cos(fr), 2, axis=-1).astype(f)
    s[:, :32] = -s[:, :32]
    col = np.arange(64)
    return {
        "ident": np.eye(128, dtype=f),
        "tri": (same & (i[:, None] <= i[None, :])).astype(f),
        "gt": (same & (i[:, None] > i[None, :])).astype(f),
        "cos": np.ascontiguousarray(np.concatenate([c, c])), "sin": np.ascontiguousarray(np.concatenate([s, s])),
        "mv": ((i[:, None] // 64) == ((col[None, :] // 8) % 2)).astype(f),
        "mk": (((i[:, None] % 64) // 8) == np.arange(8)[None, :]).astype(f),
        "mg": (((i[:, None] % 64) // 8) == np.arange(8)[None, :]).astype(f),
        "eid": i[:, None].astype(f),
    }


def kernel(**inputs):
    import concourse.bacc as bacc
    from concourse.bass_utils import run_bass_kernel_spmd

    a = {k: np.asarray(v) for k, v in inputs.items()}

    def ks(w, k=2):
        n = w.shape[-1]
        return w.reshape(k, 128, n).transpose(1, 0, 2).reshape(128, k * n)

    def rep(v):
        return np.broadcast_to(v.reshape(1, -1), (128, v.size))

    L0 = lambda n: a["L0_" + n]
    L1 = lambda n: a["L1_" + n]
    ar = dict(constants())
    ctx = a["ctx_512"]
    ar["x"] = a["x"].reshape(4096, 256)
    ar["ctx"] = ctx
    ar["ctxT"] = ctx.transpose(0, 2, 1).reshape(32, 128, 64)
    ar["w_in"] = ks(L0("attn_in_proj_w"))
    ar["nscale"] = L0("attn_norm_scale").reshape(2, 128).T
    ar["convw"] = L0("attn_conv_weight").reshape(4, 4, 128).transpose(2, 1, 0).reshape(128, 16)
    ar["convb"] = L0("attn_conv_bias").reshape(4, 128).T
    ar["dskip"] = L0("attn_D").reshape(4, 128).T
    ar["alog"] = rep(L0("attn_A_log"))
    ar["dtb"] = rep(L0("attn_dt_bias"))
    ar["w_out"] = ks(L0("attn_out_proj_w"), 4)
    ar["wq"] = L0("xattn_Wq").reshape(16, 128, 256).transpose(1, 0, 2)
    ar["wkcq"] = L0("xattn_w_kc_q").reshape(16, 128, 2, 96).transpose(3, 2, 0, 1)
    ar["wqr"] = L0("xattn_W_qr").transpose(2, 0, 1)
    ar["wkr"] = L0("xattn_W_kr").transpose(2, 0, 1)
    ar["wkc"] = L0("xattn_w_kc_kv").transpose(1, 0, 2)
    ar["wo"] = L0("xattn_Wo").reshape(256, 16, 128).transpose(2, 1, 0)
    up = np.concatenate([L0("ffn_Wup"), L0("ffn_Wsu")[None]])
    ga = np.concatenate([L0("ffn_Wgate"), L0("ffn_Wsg")[None]])
    dn = np.concatenate([L0("ffn_Wdown"), L0("ffn_Wsd")[None]])
    w = np.stack([up, ga, dn]).reshape(3, 8, 2, 128, 256)
    ar["moe_w"] = w.transpose(3, 1, 0, 2, 4).reshape(128, 8, 1536)
    bb = np.stack([np.concatenate([L0("ffn_bup"), L0("ffn_bsu")[None]]),
                   np.concatenate([L0("ffn_bgate"), L0("ffn_bsg")[None]])])
    ar["moe_b"] = bb.reshape(2, 8, 2, 128).transpose(3, 0, 1, 2)
    ar["bdn"] = np.concatenate([L0("ffn_bdown"), L0("ffn_bsd")[None]])
    ar["moe_r"] = L0("ffn_Wr").reshape(2, 128, 7).transpose(1, 0, 2)
    ar["rb"] = rep(L0("ffn_br"))
    ar["gb"] = rep(L0("ffn_gate_bias"))
    mixes = np.stack([L1("attn_time_mix_key"), L1("attn_time_mix_value"), L1("attn_time_mix_receptance")])
    ar["mix"] = mixes.reshape(3, 2, 128).transpose(2, 0, 1).reshape(128, 6)
    ar["tdf"] = np.stack([L1("attn_time_decay"), L1("attn_time_first")]).reshape(4, 128).T
    ar["w_kvro"] = np.stack([L1("attn_Wk"), L1("attn_Wv"), L1("attn_Wr"), L1("attn_Wo")]) \
        .reshape(4, 2, 128, 256).transpose(2, 0, 1, 3).reshape(128, 2048)
    gu = np.concatenate([L1("ffn_gate_proj_w"), L1("ffn_up_proj_w")], axis=1)
    ar["wg"] = gu.reshape(8 * 352, 2, 128).transpose(2, 1, 0).reshape(128, 5632)
    ar["mw"] = L1("ffn_mask_up_w").transpose(1, 0, 2).reshape(2, 128, 64).transpose(1, 0, 2).reshape(128, 128)
    ar["gw"] = L1("ffn_gate_w").reshape(64, 2, 128).transpose(2, 1, 0).reshape(128, 128)
    ar["wd"] = L1("ffn_down_proj_w").transpose(0, 2, 1).reshape(11, 128, 256).transpose(1, 0, 2).reshape(128, 2816)
    ar["invt"] = np.broadcast_to(L1("ffn_inv_map").reshape(1, 64), (64, 64))

    nc = bacc.Bacc("TRN2", target_bir_lowering=False, num_devices=1)
    arrays, aps = {}, {}
    for name, v in ar.items():
        v = np.ascontiguousarray(v)
        arrays["in_" + name] = v
        aps[name] = nc.dram_tensor("in_" + name, v.shape, mybir.dt.from_np(v.dtype), kind="ExternalInput").ap()
    out = nc.dram_tensor("out_0", (4096, 256), F32, kind="ExternalOutput").ap()
    build(nc, aps, out)
    r = run_bass_kernel_spmd(nc, [arrays], core_ids=[0])
    return r.results[0]["out_0"].reshape(64, 64, 256)
```

```python
from contextlib import ExitStack

import numpy as np
import concourse.bass as bass
from concourse import mybir

ALU = mybir.AluOpType
ACT = mybir.ActivationFunctionType
F32 = mybir.dt.float32
I32 = mybir.dt.int32
AX = mybir.AxisListType.X

P = 128
NT = 32
TB = 2
NB = 4
NBLK = NT // TB
NTH = 3
ARENA = 5680
SMALL = 400
LANE_BANKS = [(0, 1, 2), (3, 4, 5), (6, 7)]
NH = 16
NEG = -1.0e38


class Call:

    def __init__(self, select, args, kwargs):
        self.select, self.args, self.kwargs = select, args, kwargs

    def on(self, eng):
        return self.select(eng)(*self.args, **self.kwargs)


def op(select, *args, **kwargs):
    return Call(select, args, kwargs)


def width(ap):
    n = 1
    for d in ap.shape[1:]:
        n *= d
    return n


def pointers(args):
    return sum(not isinstance(a, (int, float)) and a is not None and len(a.shape) == 2 and a.shape[1] == 1
               for a in args)


class Lengths:

    def matmul(self, out, lhsT, rhs, **_):
        return 4 * width(rhs) / 2.4

    def transpose(self, out, in_, ident):
        return 108

    def activation(self, out, in_, func, bias=0.0, **_):
        return 70 + width(out) / 1.2 + 93 * pointers([bias])

    def tensor_scalar(self, out, in0, scalar1, scalar2, *_):
        return 65 + width(out) / 0.96 / (2 if "SB" in str(in0.space) else 1) + 65 * min(1, pointers([scalar1, scalar2]))

    def scalar_tensor_tensor(self, out, in0, scalar, *_):
        return 65 + width(out) / 0.96 + 65 * pointers([scalar])

    def flat(self, out, *_):
        return 68 + width(out) / 0.96

    def reciprocal(self, out, in_):
        return 68 + 6.25 * width(out)

    def reduce(self, out, in_, *_):
        return 68 + width(in_) / 0.96

    def match_replace(self, out, *_):
        return 136 + width(out) / 0.96

    def scan(self, out, *_):
        return 68 + width(out) / 0.96

    def dma_start(self, out, in_):
        return 60

    tensor_tensor = tensor_copy = memset = bn_aggr = flat
    tensor_reduce = bn_stats = max = reduce
    tensor_tensor_scan = scan


class PoolLengths(Lengths):
    def tensor_tensor(self, out, in0, in1, how):
        return 150 + width(out) * (2.1 if how != ALU.pow else 250)

    def tensor_scalar(self, out, *_):
        return 150 + width(out) * 1.5

    def memset(self, out, _):
        return 40 + width(out) * 0.85


TABLES = {ACT.Exp: 1, ACT.Silu: 2, ACT.Ln: 3}
TABLE_NS = 1283
SWITCH_NS = 1283
LAG = {"pe": 197, "act": 150, "dve": 128, "pool": 80, "sp": 2500}


class Ins:
    def __init__(self, queue, call, after, lane, job):
        self.queue, self.call, self.after, self.lane, self.job = queue, call, after, lane, job
        self.sem, self.step, self.value, self.end, self.used = None, 1, 0, None, False


class Queue:

    def __init__(self, name, sem, lengths):
        self.name, self.sem, self.lengths = name, sem, lengths
        self.lanes, self.pending, self.lane, self.job = {}, {}, -1, 0
        self.order = []

    def wait(self, *tokens):
        self.pending.setdefault(self.lane, []).extend(x for x in tokens if x is not None)

    def put(self, call, *tokens):
        self.wait(*tokens)
        ins = Ins(self, call, self.pending.pop(self.lane, []), self.lane, self.job)
        ins.sem = self.sem
        self.lanes.setdefault(self.lane, []).append(ins)
        return ins

    def dma(self, call, sem, *tokens):
        ins = self.put(call, *tokens)
        ins.sem, ins.step, ins.used = sem, 16, True
        return ins

    @property
    def last(self):
        lane = self.lanes.get(self.lane)
        return lane[-1] if lane else None

    def play(self, eng):
        seen = {}
        for ins in self.order:
            for dep in ins.after:
                if seen.get(id(dep.sem), 0) < dep.value:
                    seen[id(dep.sem)] = dep.value
                    eng.wait_ge(dep.sem, dep.value)
            done = ins.call.on(eng)
            if ins.used:
                done.then_inc(ins.sem, ins.step)


def order(queues):
    clock = {q: 0.0 for q in queues}
    heads = {(q, lane): 0 for q in queues for lane in q.lanes}
    ready = {}
    counts = {}
    table = [0]

    def other(ins):
        t = TABLES.get(ins.call.args[2], 0) if ins.queue.name == "act" else 0
        return t if t != table[0] else 0

    left = sum(len(v) for q in queues for v in q.lanes.values())
    while left:
        best = None
        for (q, lane), n in heads.items():
            ins = q.lanes[lane][n] if n < len(q.lanes[lane]) else None
            if ins is None:
                continue
            at = ready.get(ins)
            if at is None:
                at = 0.0
                for dep in ins.after:
                    if dep.end is None:
                        at = None
                        break
                    at = max(at, dep.end + LAG[dep.queue.name] + (60 if q.name == "pe" else 0))
                if at is None:
                    continue
                ready[ins] = at
            key = (max(at, clock[q]) + (SWITCH_NS if other(ins) else 0), ins.job)
            if best is None or key < best[0]:
                best = (key, q, lane, ins)
        assert best is not None, "the lanes wait for each other"
        (start, _), q, lane, ins = best
        heads[(q, lane)] += 1
        length = ins.call.on(q.lengths)
        if other(ins):
            table[0] = other(ins)
            start += TABLE_NS - SWITCH_NS
        clock[q] = start + length
        ins.end = clock[q]
        q.order.append(ins)
        left -= 1
    for q in queues:
        for ins in q.order:
            for dep in ins.after:
                dep.used = True
    for q in queues:
        for ins in q.order:
            if ins.used:
                counts[id(ins.sem)] = counts.get(id(ins.sem), 0) + ins.step
                ins.value = counts[id(ins.sem)]
    return max(clock.values())


CONSTS = {"ident": 128, "tri": 128, "gt": 128, "cos": 64, "sin": 64, "mv": 64, "mk": 8, "mg": 8, "eid": 1}
PARAMS = {
    "w_in": 2 * 1284, "nscale": 2, "convw": 16, "convb": 4, "dskip": 4, "alog": 4, "dtb": 4, "w_out": 4 * 256,
    "rb": 7, "gb": 7, "mix": 6, "tdf": 4, "w_kvro": 8 * 256,
}


def build(nc, t, out):
    ctx = ExitStack()
    with ctx:
        def sb(name, n, parts=P, dt=F32):
            return ctx.enter_context(nc.sbuf_tensor(name, [parts, n], dt))

        sems = {}

        def sem(name):
            if name not in sems:
                sems[name] = ctx.enter_context(nc.semaphore(name))
            return sems[name]

        SB = {n: sb("c_" + n, w) for n, w in {**CONSTS, **PARAMS}.items()}
        X = sb("X", NT * 256)[:, :].rearrange("p (t c) -> p t c", t=NT)
        Aw = sb("Aw", 2 * 1024)[:, :].rearrange("p (k n) -> p k n", k=2)
        Bw = sb("Bw", 8 * 256)[:, :].rearrange("p (h n) -> p h n", h=8)
        BIG = sb("BIG", 12448)
        acst = sb("acst", 64)
        mhalf = sb("mhalf", 8)
        td65 = sb("td65", 2 * NB * 65)
        om = sb("om", 6)
        invt = sb("invt", 64, 64, I32)
        bdn = sb("bdn", 256, 8)
        arenas = [sb(f"arena{i}", ARENA) for i in range(NTH)]
        stores = [sb(f"small{i}", SMALL) for i in range(NTH)]
        banks = [ctx.enter_context(nc.psum_tensor(f"ps{i}", [P, 512], F32)) for i in range(8)]

        def program():
            T = Queue("pe", sem("s_pe"), Lengths())
            V = Queue("dve", sem("s_dve"), Lengths())
            A = Queue("act", sem("s_act"), Lengths())
            G = Queue("pool", sem("s_pool"), PoolLengths())
            S = Queue("sp", sem("s_sp"), Lengths())
            queues = (T, V, A, G, S)

            ident = SB["ident"][:, :]

            loads = {}

            def load(name, dst, src, wait=()):
                s = sem("l_" + name)
                S.wait(*wait)
                loads[name] = S.dma(op(lambda e: e.dma_start, dst, src), s)

            for name in ("ident", "w_in", "nscale"):
                load(name, SB[name][:, :], t[name])
            xsem = []

            def load_x(n):
                xsem.append(S.dma(op(lambda e: e.dma_start, X[:, 4 * n:4 * n + 4, :],
                    t["x"][512 * n:512 * n + 512, :].rearrange("(t p) c -> p t c", p=P)),
                      sem(f"l_x{n}")))

            load_x(0)
            for name in ("convw", "convb", "dskip", "alog", "dtb", "tri", "gt", "w_out"):
                load(name, SB[name][:, :], t[name])
            load_x(1)

            for n in range(2, 8):
                load_x(n)
            for name in ("cos", "sin", "mv", "mk", "mg", "eid", "rb", "gb", "mix", "tdf", "w_kvro"):
                load(name, SB[name][:, :], t[name])
            load("invt", invt[:, :], t["invt"])

            UP, UG, UD = (BIG[:, 4096 * n:4096 * n + 4096].rearrange("p (e k n) -> p e k n", e=8, k=2) for n in range(3))
            moe_b = BIG[:, 12288:12320].rearrange("p (a e k) -> p a e k", a=2, e=8)
            moe_r = BIG[:, 12320:12334].rearrange("p (k n) -> p k n", k=2)
            WG = BIG[:, 0:5632].rearrange("p (k n) -> p k n", k=2)
            WD = BIG[:, 5632:8448].rearrange("p (k n) -> p k n", k=11)
            MG = BIG[0:64, 8448:11264]
            MW = BIG[:, 11264:11392].rearrange("p (k n) -> p k n", k=2)
            GW = BIG[:, 11392:11520].rearrange("p (k n) -> p k n", k=2)
            PM = BIG[0:64, 11520:11584]

            w_in = SB["w_in"][:, :].rearrange("p (k n) -> p k n", k=2)
            w_out = SB["w_out"][:, :].rearrange("p (k n) -> p k n", k=4)
            convw = SB["convw"][:, :].rearrange("p (f k) -> p f k", f=4)
            kvro = SB["w_kvro"][:, :].rearrange("p (m k n) -> p m k n", m=4, k=2)
            mix = SB["mix"][:, :].rearrange("p (m k) -> p m k", m=3)
            omx = om[:, :].rearrange("p (m k) -> p m k", m=3)
            td65v = td65[:, :].rearrange("p (k b s) -> p k b s", k=2, b=NB)
            tdf = SB["tdf"]

            def mm(out_ap, lhsT, rhs, start, stop):
                return op(lambda e: e.matmul, out_ap, lhsT, rhs, start=start, stop=stop, skip_group_check=True)

            half = V.put(op(lambda e: e.memset, mhalf[:, :], -0.5))
            win_ok = []
            V.wait(loads["w_in"], loads["nscale"])
            for k in range(2):
                win_ok.append(V.put(op(lambda e: e.tensor_scalar, w_in[:, k, :], w_in[:, k, :],
                    SB["nscale"][:, k:k + 1], None, ALU.mult)))
            win_ok = win_ok[-1]
            ea = A.put(op(lambda e: e.activation, acst[:, 0:4], SB["alog"][:, :], ACT.Exp), loads["alog"])
            a_ok = V.put(op(lambda e: e.tensor_scalar, acst[:, 4:8], acst[:, 0:4], -1.0, None, ALU.mult), ea)

            jobs = [0]

            class Thread:
                def __init__(self, i):
                    self.i, self.done, self.at = i, [], 0
                    self.banks = LANE_BANKS[i]
                    self.free = {b: None for b in self.banks}
                    self.csem = sem(f"s_ctx{i}")

                def bank(self):
                    b = self.banks[self.at % len(self.banks)]
                    self.at += 1
                    T.wait(self.free[b])
                    return b, banks[b]

                def start(self, blk=None, rank=0):
                    jobs[0] += 1
                    for q in queues:
                        q.lane, q.job = self.i, jobs[0]
                    self.ao = self.so = 0
                    for q in (V, G, S):
                        q.wait(*self.done)
                    if blk is not None:
                        for q in (V, G):
                            q.wait(*xdone.get(blk, ()))

                def cut(self, n, parts=P):
                    self.ao += n
                    assert self.ao <= ARENA, self.ao
                    return arenas[self.i][0:parts, self.ao - n:self.ao]

                def sm(self, n):
                    self.so += n
                    assert self.so <= SMALL, self.so
                    return stores[self.i][:, self.so - n:self.so]

                def end(self, blk=None):
                    self.done = [q.last for q in (T, V, A, G)]
                    if blk is not None:
                        xdone[blk] = list(self.done)
                    for q in queues:
                        q.lane, q.job = -1, 0

            xdone = {}
            threads = [Thread(i) for i in range(NTH)]

            def norm(th, blk, hview, rms=None):
                st = th.sm(12).rearrange("p (t c) -> p t c", t=TB)
                mv = th.sm(4).rearrange("p (t c) -> p t c", t=TB)
                w = th.sm(16).rearrange("p (a t) -> p a t", t=TB)
                V.wait(xsem[blk * TB // 4])
                for i in range(TB):
                    a = V.put(op(lambda e: e.bn_stats, st[:, i, :], X[:, blk * TB + i, :]))
                for i in range(TB):
                    a = V.put(op(lambda e: e.bn_aggr, mv[:, i, :], st[:, i, :]), a)
                a = V.put(op(lambda e: e.tensor_scalar, w[:, 0, :], mv[:, :, 1], 1e-5, None, ALU.add), a)
                g = G.put(op(lambda e: e.tensor_tensor, w[:, 1, :], w[:, 0, :], mhalf[:, 0:TB], ALU.pow), a, half)
                if rms is not None:
                    g = G.put(op(lambda e: e.tensor_tensor, w[:, 2, :], w[:, 1, :], w[:, 1, :], ALU.mult), g)
                    g = G.put(op(lambda e: e.tensor_tensor, w[:, 3, :], w[:, 2, :], mv[:, :, 1], ALU.mult), g)
                    g = G.put(op(lambda e: e.tensor_scalar, w[:, 4, :], w[:, 3, :], 1e-6, None, ALU.add), g)
                    g = G.put(op(lambda e: e.tensor_tensor, w[:, 5, :], w[:, 4, :], mhalf[:, 0:TB], ALU.pow), g)
                V.wait(g)
                for i in range(TB):
                    for dst, src in hview(i, X[:, blk * TB + i, :]):
                        a = V.put(op(lambda e: e.tensor_scalar, 
                    dst, src, mv[:, i, 0:1], w[:, 1, i:i + 1], ALU.subtract, ALU.mult))
                    if rms is not None:
                        b = V.put(op(lambda e: e.tensor_scalar, rms(i), hview(i, None)[0][0], w[:, 5, i:i + 1], None,
                    ALU.mult), a)
                        a = b
                return a

            def turned(th, h, ready, dst):
                b, ps = th.bank()
                T.wait(loads["ident"])
                for k in range(2):
                    for i in range(TB):
                        tok = T.put(op(lambda e: e.transpose, ps[:, k * 256 + i * P:k * 256 + i * P + P],
                    h[:, i, k * P:k * P + P], ident), ready)
                th.free[b] = c = A.put(op(lambda e: e.activation, dst, ps[:, :].rearrange("p (k n) -> p k n", k=2)
                    if len(dst.shape) == 3 else
                    ps[:, :].rearrange("p (k b s) -> p k b s", k=2, b=NB),
                    ACT.Copy), tok)
                return c

    
            def stage1(th, blk):
                th.start(blk)
                t0 = blk * TB
                hl = th.cut(512).rearrange("p (t c) -> p t c", t=TB)
                h = th.cut(512).rearrange("p (t c) -> p t c", t=TB)
                hT = th.cut(512).rearrange("p (k n) -> p k n", k=2)
                sT = th.cut(1024).rearrange("p (f n) -> p f n", f=4)
                gT = th.cut(1024).rearrange("p (f n) -> p f n", f=4)
                BC = th.cut(512).rearrange("p (f n) -> p f n", f=2)
                hn = norm(th, blk, lambda i, x: [(hl[:, i, :], x)], lambda i: h[:, i, :])
                xa = G.put(op(lambda e: e.tensor_tensor, X[:, t0:t0 + TB, :], X[:, t0:t0 + TB, :], hl[:, :, :], ALU.add), hn)
                ht = turned(th, h, hn, hT[:, :, :])
                dz = th.sm(64).rearrange("p (a c) -> p a c", a=8)
                b, ps = th.bank()
                T.wait(ht, win_ok)
                for i in range(TB):
                    for k in range(2):
                        tok = T.put(mm(ps[:, 4 * i:4 * i + 4], hT[:, k, i * P:i * P + P], w_in[:, k, 1024:1028],
                                       k == 0, k == 1))
                dtb = SB["dtb"][:, :].unsqueeze(1).broadcast_to([P, TB, 4])
                d2 = lambda j: dz[:, j, :].rearrange("p (t c) -> p t c", t=TB)
                th.free[b] = v = V.put(op(lambda e: e.tensor_tensor, d2(0), ps[:, 0:8].rearrange("p (t c) -> p t c", t=TB),
                    dtb, ALU.add), tok, loads["dtb"])
                v = V.put(op(lambda e: e.scalar_tensor_tensor, dz[:, 1, :], dz[:, 0, :], -1.0, dz[:, 0, :], ALU.mult, ALU.max), v)
                v2 = V.put(op(lambda e: e.tensor_scalar, dz[:, 4, :], dz[:, 0, :], 0.0, None, ALU.max))
                a = A.put(op(lambda e: e.activation, dz[:, 2, :], dz[:, 1, :], ACT.Exp, scale=-1.0), v)
                a = A.put(op(lambda e: e.activation, dz[:, 3, :], dz[:, 2, :], ACT.Ln, bias=1.0), a)
                v = V.put(op(lambda e: e.tensor_tensor, dz[:, 5, :], dz[:, 3, :], dz[:, 4, :], ALU.add), a, v2)
                dt_ok = V.put(op(lambda e: e.tensor_tensor, d2(6), d2(5), acst[:, 4:8].unsqueeze(1).broadcast_to([P, TB, 4]),
                    ALU.mult), v, a_ok)
                cv = th.cut(1024).rearrange("p (f n) -> p f n", f=4)
                g2nd = th.cut(512)
                V.wait(loads["convw"], loads["convb"])
                for g in range(2):
                    b, ps = th.bank()
                    for f in range(2):
                        for k in range(2):
                            c0 = 512 + (2 * g + f) * P
                            tok = T.put(mm(ps[:, f * 256:f * 256 + 256], w_in[:, k, c0:c0 + P], hT[:, k, :],
                                           k == 0, k == 1))
                    for f in range(2):
                        ff = 2 * g + f
                        src = ps[:, f * 256:f * 256 + 256]
                        s3 = src.rearrange("p (b s) -> p b s", b=NB)
                        c3 = cv[:, ff, :].rearrange("p (b s) -> p b s", b=NB)
                        v = V.put(op(lambda e: e.tensor_scalar, cv[:, ff, :], src, convw[:, ff, 3:4],
                    SB["convb"][:, ff:ff + 1], ALU.mult, ALU.add), tok)
                        for d in (1, 2, 3):
                            v = V.put(op(lambda e: e.scalar_tensor_tensor, c3[:, :, d:64], s3[:, :, 0:64 - d],
                    convw[:, ff, 3 - d:4 - d], c3[:, :, d:64],
                    ALU.mult, ALU.add), v)
                    th.free[b] = v
                    s_ok = A.put(op(lambda e: e.activation, sT[:, 2 * g:2 * g + 2, :], cv[:, 2 * g:2 * g + 2, :], ACT.Silu), v)
                for g in range(2):
                    b, ps = th.bank()
                    for f in range(2):
                        for k in range(2):
                            c0 = (2 * g + f) * P
                            tok = T.put(mm(ps[:, f * 256:f * 256 + 256], w_in[:, k, c0:c0 + P], hT[:, k, :],
                                           k == 0, k == 1))
                    th.free[b] = g_ok = A.put(op(lambda e: e.activation, 
                    gT[:, 2 * g:2 * g + 2, :], ps[:, :].rearrange("p (f n) -> p f n", f=2), ACT.Silu), tok)
                b, ps = th.bank()
                for f in range(2):
                    for k in range(2):
                        bc_mm = tok = T.put(mm(ps[:, f * 256:f * 256 + 256], w_in[:, k, 1028 + f * P:1156 + f * P],
                                               hT[:, k, :], k == 0, k == 1))
                th.free[b] = bc_ok = A.put(op(lambda e: e.activation, 
                    BC[:, :, :], ps[:, :].rearrange("p (f n) -> p f n", f=2), ACT.Copy), tok)
                T.wait(loads["tri"])
                for i in range(TB):
                    ts = slice(i * P, i * P + P)
                    xt = (hl, h)[i].rearrange("p t (a n) -> p (t a) n", a=2)
                    Gh = (hT.rearrange("p k n -> p (k n)"), g2nd)[i].rearrange("p (f n) -> p f n", f=4)
                    E = cv[:, 2 * i:2 * i + 2, :].rearrange("p a (b n) -> p (a b) n", b=2)
                    cbm = th.sm(128)
                    b, ps = th.bank()
                    for f in range(4):
                        tok = T.put(op(lambda e: e.transpose, ps[:, f * P:f * P + P], sT[:, f, ts], ident), s_ok)
                    A.wait(xa)
                    th.free[b] = xt_ok = A.put(op(lambda e: e.activation, 
                    xt[:, :, :], ps[:, :].rearrange("p (f n) -> p f n", f=4), ACT.Copy), tok)
                    G.wait(dt_ok, loads["gt"], bc_mm)
                    for f in range(4):
                        gh = G.put(op(lambda e: e.tensor_scalar, Gh[:, f, :], SB["gt"][:, :],
                                      dz[:, 6, 4 * i + f:4 * i + f + 1], 1.0, ALU.mult, ALU.mult))
                    b, ps2 = th.bank()
                    cb = T.put(mm(ps2[:, 0:P], BC[:, 0, ts], BC[:, 1, ts], True, True), bc_ok)
                    th.free[b] = cm = V.put(op(lambda e: e.tensor_tensor, cbm, ps2[:, 0:P], SB["tri"][:, :], ALU.mult),
                                            cb, loads["tri"])
                    b, ps3 = th.bank()
                    for f in range(4):
                        tok = T.put(mm(ps3[:, f * P:f * P + P], Gh[:, f, :], SB["tri"][:, :], True, True), gh)
                    th.free[b] = ex = A.put(op(lambda e: e.activation, 
                    E, ps3[:, :].rearrange("p (f n) -> p f n", f=4), ACT.Exp), tok)
                    for f in range(4):
                        m_ok = V.put(op(lambda e: e.scalar_tensor_tensor, Gh[:, f, :], E[:, f, :],
                    dz[:, 5, 4 * i + f:4 * i + f + 1], cbm,
                    ALU.mult, ALU.mult), ex, cm)
                    b, ps4 = th.bank()
                    for f in range(4):
                        tok = T.put(mm(ps4[:, f * P:f * P + P], xt[:, f, :], Gh[:, f, :], True, True), m_ok, xt_ok)
                    V.wait(loads["dskip"])
                    for f in range(4):
                        y = V.put(op(lambda e: e.scalar_tensor_tensor, xt[:, f, :], sT[:, f, ts], SB["dskip"][:, f:f + 1],
                    ps4[:, f * P:f * P + P], ALU.mult, ALU.add), tok)
                    th.free[b] = y
                    y = G.put(op(lambda e: e.tensor_tensor, xt[:, :, :], xt[:, :, :], gT[:, :, ts], ALU.mult), y, g_ok)
                    b, ps5 = th.bank()
                    for f in range(4):
                        tok = T.put(mm(ps5[:, 0:256], xt[:, f, :], w_out[:, f, :], f == 0, f == 3), y, loads["w_out"])
                    th.free[b] = V.put(op(lambda e: e.tensor_tensor, X[:, t0 + i, :], ps5[:, 0:256], X[:, t0 + i, :],
                    ALU.add), tok, xa)
                th.end(blk)

            def products(th, hf):
                th.start()
                wkcq = th.cut(2 * 4 * 128, 96).rearrange("p (c h k) -> p c h k", c=2, h=4)
                wqr = th.cut(4 * 192, 64).rearrange("p (h c) -> p h c", h=4)
                wkr = th.cut(4 * 64, 64).rearrange("p (h c) -> p h c", h=4)
                wq = th.cut(4 * 256).rearrange("p (h c) -> p h c", h=4)
                wkc = th.cut(4 * 64).rearrange("p (h c) -> p h c", h=4)
                wo = th.cut(4 * 256).rearrange("p (h c) -> p h c", h=4)
                g1 = th.cut(2 * 4 * 64, 96).rearrange("p (c h d) -> p c h d", c=2, h=4)
                g2 = th.cut(4 * 64).rearrange("p (h d) -> p h d", h=4)
                hs = slice(4 * hf, 4 * hf + 4)
                L = {}
                for name, dst, src in (("wqr", wqr, t["wqr"][:, hs, :]), ("wkr", wkr, t["wkr"][:, hs, :]),
                                       ("wkcq", wkcq, t["wkcq"][:, :, hs, :]), ("wq", wq, t["wq"][:, hs, :]),
                                       ("wkc", wkc, t["wkc"][:, hs, :]), ("wo", wo, t["wo"][:, hs, :])):
                    L[name] = S.dma(op(lambda e: e.dma_start, dst, src), sem(f"l_{name}{hf}"))
                b, ps = th.bank()
                for c in range(2):
                    for h in range(4):
                        c0 = (4 * c + h) * 64
                        tok = T.put(mm(ps[0:96, c0:c0 + 64], wqr[:, h, c * 96:c * 96 + 96], wkr[:, h, :],
                                       True, True), L["wqr"], L["wkr"])
                th.free[b] = v = V.put(op(lambda e: e.tensor_copy, g1[:, :, :, :],
                                          ps[0:96, :].rearrange("p (c h d) -> p c h d", c=2, h=4)), tok)
                b, ps = th.bank()
                for h in range(4):
                    for c in range(2):
                        tok = T.put(mm(ps[:, h * 64:h * 64 + 64], wkcq[:, c, h, :], g1[:, c, h, :],
                                       c == 0, c == 1), v, L["wkcq"])
                th.free[b] = v = V.put(op(lambda e: e.tensor_copy, g2[:, :, :],
                                          ps[:, 0:256].rearrange("p (h d) -> p h d", h=4)), tok)
                b, ps = th.bank()
                for k in range(2):
                    for h in range(4):
                        c0 = (4 * k + h) * 64
                        tok = T.put(mm(ps[:, c0:c0 + 64], wq[:, h, k * P:k * P + P], g2[:, h, :],
                                       True, True), v, L["wq"])
                th.free[b] = a = A.put(op(lambda e: e.activation, Aw[:, :, hf * 256:hf * 256 + 256],
                                          ps[:, :].rearrange("p (k n) -> p k n", k=2), ACT.Copy), tok)
                pre_done.append(a)
                b, ps = th.bank()
                for q in range(2):
                    for e2 in range(2):
                        tok = T.put(mm(ps[64 * e2:64 * e2 + 64, q * 256:q * 256 + 256], wkc[:, 2 * q + e2, :],
                                       wo[:, 2 * q + e2, :], True, True), L["wkc"], L["wo"])
                th.free[b] = v = V.put(op(lambda e: e.tensor_copy, Bw[:, 2 * hf:2 * hf + 2, :],
                                          ps[:, :].rearrange("p (q n) -> p q n", q=2)), tok)
                pre_done.append(v)
                th.end()

            pre_done = []

            def ctx_rows(th, blk, dst):
                for e2 in range(2):
                    ct = S.dma(op(lambda e: e.dma_start, dst[64 * e2:64 * e2 + 64, :, :],
                                  t["ctx"][NB * blk:NB * blk + NB, :, :].rearrange("b l d -> l b d")), th.csem)
                return ct

            def row_softmax(th, src, dst, mxs, sms, groups, tok, scale=1.0, n=64):
                v = V.put(op(lambda e: e.tensor_reduce, mxs, src, AX, ALU.max), tok)
                free = v = V.put(op(lambda e: e.tensor_tensor, dst, src, mxs.unsqueeze(2).broadcast_to([P, groups, n]),
                    ALU.subtract), v)
                a = A.put(op(lambda e: e.activation, dst, dst, ACT.Exp, scale=scale), v)
                v = V.put(op(lambda e: e.tensor_reduce, sms, dst, AX, ALU.add), a)
                return free, V.put(op(lambda e: e.reciprocal, sms, sms), v)

            def stage2(th, blk):
                th.start(blk)
                t0 = blk * TB
                qT = th.cut(2048).rearrange("p (h n) -> p h n", h=8)
                BD = th.cut(512).rearrange("p (b d) -> p b d", b=NB)
                BDT = th.cut(512).rearrange("p (b d) -> p b d", b=NB)
                pm = th.cut(1024)
                CT, R1, R2 = (pm[:, 256 * n:256 * n + 256].rearrange("p (b d) -> p b d", b=NB) for n in range(3))
                Pm = pm.rearrange("p (h n) -> p h n", h=8)
                pt_ = th.cut(1024)
                h = pt_[:, 0:512].rearrange("p (t c) -> p t c", t=TB)
                hT = pt_[:, 512:1024].rearrange("p (k n) -> p k n", k=2)
                PT = pt_.rearrange("p (h n) -> p h n", h=8)
                ct = ctx_rows(th, blk, CT)
                z = G.put(op(lambda e: e.memset, BD[:, :, :], 0.0))
                hn = norm(th, blk, lambda i, x: [(h[:, i, :], x)])
                cosb = SB["cos"][:, :].unsqueeze(1).broadcast_to([P, NB, 64])
                r1 = G.put(op(lambda e: e.tensor_tensor, R1[:, :, :], CT[:, :, :], cosb, ALU.mult), ct, loads["cos"], loads["sin"])
                for a0 in range(2):
                    r1 = G.put(op(lambda e: e.tensor_tensor, 
                    R2[:, :, 32 * a0:32 * a0 + 32], CT[:, :, 32 - 32 * a0:64 - 32 * a0],
                    SB["sin"][:, 32 * a0:32 * a0 + 32].unsqueeze(1).broadcast_to([P, NB, 32]), ALU.mult))
                for e2 in range(2):
                    rows = slice(64 * e2, 64 * e2 + 64)
                    kv = V.put(op(lambda e: e.tensor_tensor, BD[rows, :, rows], R1[rows, :, :], R2[rows, :, :], ALU.add),
                               r1, z)
                ht = turned(th, h, hn, hT[:, :, :])
                b, ps = th.bank()
                for j in range(NB):
                    tok = T.put(op(lambda e: e.transpose, ps[:, j * P:j * P + P], BD[:, j, :], ident), kv)
                th.free[b] = kt = A.put(op(lambda e: e.activation, BDT[:, :, :], ps[:, :].rearrange("p (b n) -> p b n", b=NB),
                    ACT.Copy), tok)
                T.wait(*pre_done)
                for g in range(4):
                    b, ps = th.bank()
                    for f in range(2):
                        hp = 2 * g + f
                        for k in range(2):
                            tok = T.put(mm(ps[:, f * 256:f * 256 + 256], Aw[:, k, hp * P:hp * P + P], hT[:, k, :],
                                           k == 0, k == 1), ht)
                    th.free[b] = qk = A.put(op(lambda e: e.activation, 
                    qT[:, 2 * g:2 * g + 2, :], ps[:, :].rearrange("p (f n) -> p f n", f=2), ACT.Copy), tok)
                pv_read = None
                for i in range(TB):
                    mxs = th.sm(16)
                    sms = th.sm(16)
                    for g in range(2):
                        b, ps = th.bank()
                        for b2 in range(2):
                            for q in range(4):
                                tok = T.put(mm(ps[64 * b2:64 * b2 + 64, q * P:q * P + P],
                                               qT[:, 4 * g + q, i * P + 64 * b2:i * P + 64 * b2 + 64],
                                               BDT[:, 2 * i + b2, :], True, True), qk, kt)
                        dst = Pm[:, 4 * g:4 * g + 4, :].rearrange("p h (e l) -> p (h e) l", e=2)
                        V.wait(pv_read)
                        fr, v = row_softmax(th, ps[:, :].rearrange("p (h l) -> p h l", h=8), dst,
                                            mxs[:, 8 * g:8 * g + 8], sms[:, 8 * g:8 * g + 8], 8, tok)
                        th.free[b] = fr
                        p_ok = G.put(op(lambda e: e.tensor_tensor, 
                    dst, dst, sms[:, 8 * g:8 * g + 8].unsqueeze(2).broadcast_to([P, 8, 64]), ALU.mult), v)
                        b, ps = th.bank()
                        for q in range(4):
                            tok = T.put(op(lambda e: e.transpose, ps[:, q * P:q * P + P], Pm[:, 4 * g + q, :], ident), p_ok)
                        A.wait(pv_read)
                        th.free[b] = pt = A.put(op(lambda e: e.activation, 
                    PT[:, 4 * g:4 * g + 4, :], ps[:, :].rearrange("p (h n) -> p h n", h=4), ACT.Copy), tok)
                    cT = qT[:, :, i * P:i * P + P]
                    for b2 in range(2):
                        b, ps = th.bank()
                        tok = T.put(mm(ps[:, :], BD[:, 2 * i + b2, :], PT[:, :, 64 * b2:64 * b2 + 64], True, True), pt)
                        th.free[b] = cx = A.put(op(lambda e: e.activation, 
                    cT[:, :, 64 * b2:64 * b2 + 64], ps[:, :].rearrange("p (h n) -> p h n", h=8), ACT.Copy), tok)
                    pv_read = tok
                    b, ps = th.bank()
                    for q in range(8):
                        tok = T.put(mm(ps[:, 0:256], cT[:, q, :], Bw[:, q, :], q == 0, q == 7), cx)
                    th.free[b] = V.put(op(lambda e: e.tensor_tensor, X[:, t0 + i, :], ps[:, 0:256], X[:, t0 + i, :],
                    ALU.add), tok)
                th.end(blk)

            def load_moe():
                w = ()
                load("moe_r", moe_r, t["moe_r"], w)
                load("moe_b", moe_b, t["moe_b"], w)
                load("bdn", bdn[:, :], t["bdn"], w)
                for e in range(8):
                    load(f"moe{e}", BIG[:, 0:12288].rearrange("p (a e n) -> p a e n", a=3, e=8)[:, :, e, :],
                         t["moe_w"][:, e, :].rearrange("p (a n) -> p a n", a=3), w)

            def stage3(th, blk):
                th.start(blk)
                t0 = blk * TB
                h = th.cut(512).rearrange("p (t c) -> p t c", t=TB)
                hT = th.cut(512).rearrange("p (k n) -> p k n", k=2)
                U = [th.cut(512).rearrange("p (k n) -> p k n", k=2) for _ in range(2)]
                Z = [th.cut(512).rearrange("p (k n) -> p k n", k=2) for _ in range(2)]
                pT = th.cut(256, 8)
                hn = norm(th, blk, lambda i, x: [(h[:, i, :], x)])
                ht = turned(th, h, hn, hT[:, :, :])
                b, ps = th.bank()
                for i in range(TB):
                    for k in range(2):
                        tok = T.put(mm(ps[:, 8 * i:8 * i + 7], hT[:, k, i * P:i * P + P], moe_r[:, k, :],
                                       k == 0, k == 1), ht, loads["moe_r"])
                r = lambda n: th.sm(TB * n).rearrange("p (t n) -> p t n", t=TB)
                gl, W, W2, t8, ms, t2, gm, pr, mx, sm = (r(7), r(13), r(13), r(8), r(7), r(7), r(7), r(8), r(1), r(1))
                z = G.put(op(lambda e: e.memset, W[:, :, 7:13], 3.0e38))
                z = G.put(op(lambda e: e.memset, pr[:, :, 7:8], 1.0))
                bc = lambda n: SB[n][:, :].unsqueeze(1).broadcast_to([P, TB, 7])
                th.free[b] = v = V.put(op(lambda e: e.tensor_tensor, 
                    gl[:, :, :], ps[:, 0:16].rearrange("p (t n) -> p t n", t=TB)[:, :, 0:7], bc("rb"), ALU.add),
                    tok, loads["rb"], loads["gb"])
                v = V.put(op(lambda e: e.tensor_tensor, W[:, :, 0:7], gl[:, :, :], bc("gb"), ALU.add), v, z)
                for i in range(TB):
                    v1 = V.put(op(lambda e: e.max, t8[:, i, :], W[:, i, :]), v)
                    v1 = V.put(op(lambda e: e.match_replace, W2[:, i, :], t8[:, i, :], W[:, i, :], -3.3e38), v1)
                v = V.put(op(lambda e: e.tensor_tensor, ms[:, :, :], W2[:, :, 0:7], W[:, :, 0:7], ALU.not_equal), v1)
                v = V.put(op(lambda e: e.tensor_scalar, t2[:, :, :], ms[:, :, :], 1e30, -1e30, ALU.mult, ALU.add), v)
                v = V.put(op(lambda e: e.tensor_tensor, gm[:, :, :], gl[:, :, :], ms[:, :, :], ALU.mult), v)
                v = V.put(op(lambda e: e.tensor_tensor, gm[:, :, :], gm[:, :, :], t2[:, :, :], ALU.add), v)
                v = V.put(op(lambda e: e.tensor_reduce, mx[:, :, 0], gm[:, :, :], AX, ALU.max), v)
                v = V.put(op(lambda e: e.tensor_tensor, gm[:, :, :], gm[:, :, :], mx[:, :, :].broadcast_to([P, TB, 7]),
                    ALU.subtract), v)
                a = A.put(op(lambda e: e.activation, gm[:, :, :], gm[:, :, :], ACT.Exp), v)
                v = V.put(op(lambda e: e.tensor_reduce, sm[:, :, 0], gm[:, :, :], AX, ALU.add), a)
                v = V.put(op(lambda e: e.reciprocal, sm[:, :, :], sm[:, :, :]), v)
                prob = V.put(op(lambda e: e.tensor_tensor, pr[:, :, 0:7], gm[:, :, :], sm[:, :, :].broadcast_to([P, TB, 7]),
                    ALU.mult), v)
                ups, downs = {}, [None] * 2
                zfree = [None] * 2

                def up(x):
                    b, ps = th.bank()
                    for f in range(2):
                        for k in range(2):
                            tok = T.put(mm(ps[:, f * 256:f * 256 + 256], UP[:, x, k, f * P:f * P + P], hT[:, k, :],
                                           k == 0, k == 1), ht, loads[f"moe{x}"])
                    A.wait(loads["moe_b"], zfree[x % 2])
                    for f in range(2):
                        a = A.put(op(lambda e: e.activation, U[x % 2][:, f, :], ps[:, f * 256:f * 256 + 256], ACT.Identity,
                    bias=moe_b[:, 0, x, f:f + 1]), tok)
                    th.free[b] = ups[x] = a

                up(7)
                order = [7, 0, 1, 2, 3, 4, 5, 6]
                U_of = {}
                for n, x in enumerate(order):
                    b, ps = th.bank()
                    u = U[x % 2]
                    for f in range(2):
                        for k in range(2):
                            tok = T.put(mm(ps[:, f * 256:f * 256 + 256], UG[:, x, k, f * P:f * P + P], u[:, k, :],
                                           k == 0, k == 1), ups[x])
                    zz = Z[n % 2]
                    A.wait(downs[n % 2])
                    for f in range(2):
                        a = A.put(op(lambda e: e.activation, zz[:, f, :], ps[:, f * 256:f * 256 + 256], ACT.Silu,
                    bias=moe_b[:, 1, x, f:f + 1]), tok)
                    th.free[b] = a
                    zfree[x % 2] = zr = G.put(op(lambda e: e.tensor_tensor, zz[:, :, :], zz[:, :, :], u[:, :, :], ALU.mult), a)
                    if n < 7:
                        up(order[n + 1])
                    if n == 1:
                        b, ps = th.bank()
                        for i in range(TB):
                            tok = T.put(op(lambda e: e.transpose, ps[0:8, i * P:i * P + P], pr[:, i, :], ident), prob)
                        th.free[b] = pt = V.put(op(lambda e: e.tensor_copy, pT, ps[0:8, 0:256]), tok)
                    b, ps = th.bank()
                    for i in range(TB):
                        for k in range(2):
                            last = k == 1 and n != 2
                            tok = T.put(mm(ps[:, i * 256:i * 256 + 256], zz[:, k, i * P:i * P + P], UD[:, x, k, :],
                                           k == 0, last), zr)
                    downs[n % 2] = tok
                    if n == 0:
                        for i in range(TB):
                            v = V.put(op(lambda e: e.tensor_tensor, X[:, t0 + i, :], ps[:, i * 256:i * 256 + 256],
                    X[:, t0 + i, :], ALU.add), tok)
                    else:
                        for i in range(TB):
                            v = V.put(op(lambda e: e.scalar_tensor_tensor, 
                    X[:, t0 + i, :], ps[:, i * 256:i * 256 + 256], pr[:, i, x:x + 1], X[:, t0 + i, :],
                    ALU.mult, ALU.add), tok, prob, V.last)
                    th.free[b] = v
                b, ps = th.bank()
                for i in range(TB):
                    tok = T.put(mm(ps[:, i * 256:i * 256 + 256], pT[:, i * P:i * P + P], bdn[:, :], True, True),
                                pt, loads["bdn"])
                th.free[b] = V.put(op(lambda e: e.tensor_tensor, 
                    X[:, t0:t0 + TB, :], ps[:, :].rearrange("p (t n) -> p t n", t=TB), X[:, t0:t0 + TB, :], ALU.add),
                    tok, V.last)
                th.end(blk)
                moe_last.extend(th.done)

            moe_last = []

            def stage4(th, blk):
                th.start(blk)
                t0 = blk * TB
                h = th.cut(512).rearrange("p (t c) -> p t c", t=TB)
                pad = lambda: th.cut(2 * NB * 65)
                flat = {}

                def p4(n):
                    flat[n] = pad()
                    return flat[n].rearrange("p (k b s) -> p k b s", k=2, b=NB)

                f4 = lambda: th.cut(512).rearrange("p (k b s) -> p k b s", k=2, b=NB)
                H = p4("H")
                mx = [f4() for _ in range(3)]
                K, MX, E1, E2, GV = (p4(n) for n in ("K", "MX", "E1", "E2", "GV"))
                Vv = f4()
                C = mx[1]
                D = h.rearrange("p k (b s) -> p k b s", b=NB)
                for n, w, val in (("H", H, 0.0), ("K", K, NEG), ("E1", E1, 0.0), ("E2", E2, 0.0), ("GV", GV, 0.0)):
                    z = G.put(op(lambda e: e.memset, w[:, :, :, 0:1], val))
                hn = norm(th, blk, lambda i, x: [(h[:, i, :], x)])
                A.wait(z)
                ht = turned(th, h, hn, H[:, :, :, 1:65])
                for m in range(3):
                    for k in range(2):
                        g = G.put(op(lambda e: e.tensor_scalar, mx[m][:, k, :, :], H[:, k, :, 0:64], omx[:, m, k:k + 1], 1.0,
                                     ALU.mult, ALU.mult), ht, om_ok)
                        mok = V.put(op(lambda e: e.scalar_tensor_tensor, mx[m][:, k, :, :], H[:, k, :, 1:65],
                    mix[:, m, k:k + 1], mx[m][:, k, :, :],
                    ALU.mult, ALU.add), g)
                    b, ps = th.bank()
                    for f in range(2):
                        for k in range(2):
                            tok = T.put(mm(ps[:, f * 256:f * 256 + 256], kvro[:, m, k, f * P:f * P + P],
                                           mx[m][:, k, :, :], k == 0, k == 1), mok, loads["w_kvro"])
                    src = ps[:, :].rearrange("p (k b s) -> p k b s", k=2, b=NB)
                    if m == 0:
                        kok = A.put(op(lambda e: e.activation, K[:, :, :, 1:65], src, ACT.Copy), tok)
                    elif m == 1:
                        vok = kok = A.put(op(lambda e: e.activation, Vv[:, :, :, :], src, ACT.Copy), tok)
                    else:
                        rok = kok = A.put(op(lambda e: e.activation, mx[0][:, :, :, :], src, ACT.Exp, scale=-1.0), tok)
                    th.free[b] = kok
                    if m == 0:
                        k1 = kok
                pv, cu = slice(0, 64), slice(1, 65)
                v = V.put(op(lambda e: e.tensor_tensor_scan, flat["MX"], td65[:, :], flat["K"], NEG, ALU.add, ALU.max),
                          k1, td_ok)
                mxo = v
                for k in range(2):
                    e1 = V.put(op(lambda e: e.scalar_tensor_tensor, E1[:, k, :, cu], MX[:, k, :, pv], tdn[:, k:k + 1],
                    MX[:, k, :, cu], ALU.add, ALU.subtract), mxo)
                ee1 = A.put(op(lambda e: e.activation, E1[:, :, :, cu], E1[:, :, :, cu], ACT.Exp), e1)
                g = G.put(op(lambda e: e.tensor_tensor, E2[:, :, :, cu], K[:, :, :, cu], MX[:, :, :, cu], ALU.subtract), mxo)
                ee2 = A.put(op(lambda e: e.activation, E2[:, :, :, cu], E2[:, :, :, cu], ACT.Exp), g)
                V.wait(vok)
                for k in range(2):
                    c = V.put(op(lambda e: e.scalar_tensor_tensor, C[:, k, :, :], K[:, k, :, cu], tfn[:, k:k + 1],
                    MX[:, k, :, pv], ALU.add, ALU.max))
                for k in range(2):
                    d = V.put(op(lambda e: e.scalar_tensor_tensor, D[:, k, :, :], K[:, k, :, cu], tfn[:, k:k + 1],
                    C[:, k, :, :], ALU.add, ALU.subtract), c)
                g = G.put(op(lambda e: e.tensor_tensor, C[:, :, :, :], MX[:, :, :, pv], C[:, :, :, :], ALU.subtract), d)
                e2 = A.put(op(lambda e: e.activation, D[:, :, :, :], D[:, :, :, :], ACT.Exp), d)
                e1 = A.put(op(lambda e: e.activation, C[:, :, :, :], C[:, :, :, :], ACT.Exp), g)
                gv = G.put(op(lambda e: e.tensor_tensor, GV[:, :, :, cu], E2[:, :, :, cu], Vv[:, :, :, :], ALU.mult), ee2, vok)
                den = V.put(op(lambda e: e.tensor_tensor_scan, flat["H"], flat["E1"], flat["E2"], 0.0, ALU.mult, ALU.add),
                            ee1, ee2)
                num = V.put(op(lambda e: e.tensor_tensor_scan, flat["MX"], flat["E1"], flat["GV"], 0.0, ALU.mult, ALU.add),
                            gv, g)
                f_ = lambda a: a.rearrange("p k b s -> p (k b s)")
                q0, q1, q2 = f_(mx[0]), f_(C), f_(mx[2])
                d1 = V.put(op(lambda e: e.tensor_tensor, mx[2][:, :, :, :], C[:, :, :, :], H[:, :, :, pv], ALU.mult),
                           den, e1, rok)
                o1 = V.put(op(lambda e: e.tensor_tensor, C[:, :, :, :], C[:, :, :, :], MX[:, :, :, pv], ALU.mult),
                           num)
                d1 = V.put(op(lambda e: e.tensor_tensor, q2, q2, f_(D), ALU.add), d1, e2)
                o2 = G.put(op(lambda e: e.tensor_tensor, Vv[:, :, :, :], D[:, :, :, :], Vv[:, :, :, :], ALU.mult), e2)
                o3 = G.put(op(lambda e: e.tensor_tensor, C[:, :, :, :], C[:, :, :, :], Vv[:, :, :, :], ALU.add), o1, o2)
                d1 = V.put(op(lambda e: e.scalar_tensor_tensor, q2, q0, 1.0, q2, ALU.add, ALU.mult), d1)
                d1 = V.put(op(lambda e: e.reciprocal, q2, q2), d1)
                oo = V.put(op(lambda e: e.tensor_tensor, q1, q1, q2, ALU.mult), d1, o3)
                oT = C.rearrange("p k b s -> p k (b s)")
                b, ps = th.bank()
                for i in range(TB):
                    for k in range(2):
                        tok = T.put(mm(ps[:, i * 256:i * 256 + 256], oT[:, k, i * P:i * P + P], kvro[:, 3, k, :],
                                       k == 0, k == 1), oo)
                th.free[b] = V.put(op(lambda e: e.tensor_tensor, 
                    X[:, t0:t0 + TB, :], ps[:, :].rearrange("p (t n) -> p t n", t=TB), X[:, t0:t0 + TB, :], ALU.add), tok)
                th.end(blk)

            def stage5(th, blk):
                th.start(blk)
                t0 = blk * TB
                hq = th.cut(1024).rearrange("p (t g a kd) -> p t g a kd", t=TB, g=4, a=2)
                QB = th.cut(1024).rearrange("p (t g n) -> p t g n", t=TB, g=4)
                CT = th.cut(256).rearrange("p (b d) -> p b d", b=NB)
                CK = th.cut(128).rearrange("p (t l) -> p t l", t=TB)
                BK = th.cut(1024).rearrange("p (t k l) -> p t k l", t=TB, k=8)
                BV = th.cut(256).rearrange("p (b d) -> p b d", b=NB)
                Pm = [th.cut(512).rearrange("p (k l) -> p k l", k=8) for _ in range(2)]
                hqf = hq.rearrange("p t g a kd -> p (t g a kd)")
                PT = [hqf[:, 512 * n:512 * n + 512].rearrange("p (k l) -> p k l", k=4) for n in range(2)]
                O = th.cut(512).rearrange("p (t c) -> p t c", t=TB)
                ct = ctx_rows(th, blk, CT)
                ct = S.dma(op(lambda e: e.dma_start, CK[:, :, :], t["ctxT"][t0:t0 + TB, :, :].rearrange("t p l -> p t l")),
                           th.csem)
                z = G.put(op(lambda e: e.memset, QB[:, :, :, :], 0.0))
                mk = SB["mk"][:, :].unsqueeze(2).broadcast_to([P, 8, 64])
                G.wait(loads["mk"], loads["mv"])
                for i in range(TB):
                    bk = G.put(op(lambda e: e.tensor_tensor, BK[:, i, :, :], CK[:, i, :].unsqueeze(1).broadcast_to([P, 8, 64]),
                    mk, ALU.mult), ct)
                bv = G.put(op(lambda e: e.tensor_tensor, BV[:, :, :], CT[:, :, :],
                    SB["mv"][:, :].unsqueeze(1).broadcast_to([P, NB, 64]), ALU.mult))

                def views(i, x):
                    x = None if x is None else x.rearrange("p (k g d) -> p g k d", k=8, g=4)
                    return [(hq[:, i, :, a, :].rearrange("p g (k d) -> p g k d", k=8), x) for a in range(2)]

                hn = norm(th, blk, views)
                for i in range(TB):
                    b, ps = th.bank()
                    for g in range(4):
                        tok = T.put(op(lambda e: e.transpose, ps[:, g * P:g * P + P],
                    hq[:, i, g, :, :].rearrange("p a n -> p (a n)"), ident), hn)
                    for e2 in range(2):
                        rows = slice(64 * e2, 64 * e2 + 64)
                        qb = A.put(op(lambda e: e.activation, 
                    QB[rows, i, :, rows], ps[:, :].rearrange("p (g n) -> p g n", g=4)[rows, :, rows], ACT.Copy),
                            tok, z)
                    th.free[b] = qb
                ptr, tr = [None] * 2, [None] * 2
                for i in range(TB):
                    mxs = th.sm(32).rearrange("p (g k) -> p g k", g=4)
                    sms = th.sm(32).rearrange("p (g k) -> p g k", g=4)

                    def scores(g):
                        b, ps = th.bank()
                        tok = T.put(mm(ps[:, :], QB[:, i, g, :], BK[:, i, :, :], True, True), qb, bk)
                        V.wait(tr[g % 2])
                        fr, v = row_softmax(th, ps[:, :].rearrange("p (k l) -> p k l", k=8), Pm[g % 2][:, :, :],
                                            mxs[:, g, :], sms[:, g, :], 8, tok, scale=8.0 ** -0.5)
                        th.free[b] = fr
                        return v

                    v = scores(0)
                    for g in range(4):
                        vn = scores(g + 1) if g < 3 else None
                        b, ps = th.bank()
                        for q in range(4):
                            tr[g % 2] = tok = T.put(op(lambda e: e.transpose, ps[:, q * P:q * P + P],
                                                       Pm[g % 2][:, 2 * q:2 * q + 2, :].rearrange("p k l -> p (k l)"),
                                                       ident), v)
                        A.wait(ptr[g % 2])
                        th.free[b] = pt = A.put(op(lambda e: e.activation, PT[g % 2][:, :, :],
                                                   ps[:, :].rearrange("p (k l) -> p k l", k=4), ACT.Copy), tok)
                        b, ps = th.bank()
                        ov = ps[:, 0:128].rearrange("p (b n) -> p b n", b=2)
                        for q in range(4):
                            ptr[g % 2] = tok = T.put(mm(ov[:, :, 16 * q:16 * q + 16], PT[g % 2][:, q, :],
                                                        BV[:, 2 * i:2 * i + 2, 16 * q:16 * q + 16], True, True),
                                                     pt, bv)
                        for b2 in range(2):
                            rows = slice(64 * b2, 64 * b2 + 64)
                            o = V.put(op(lambda e: e.tensor_tensor,
                                         O[rows, i, :].rearrange("p (k g d) -> p g k d", k=8, g=4)[:, g, :, :],
                                         ov[rows, b2, :].rearrange("p (k d) -> p k d", k=8),
                                         sms[rows, g, :].unsqueeze(2).broadcast_to([64, 8, 8]), ALU.mult), tok, v)
                        th.free[b] = o
                        v = vn
                    G.put(op(lambda e: e.tensor_tensor, X[:, t0 + i, :], X[:, t0 + i, :], O[:, i, :], ALU.add), o)
                th.end(blk)

            def load_ffn():
                w = tuple(moe_last)
                load("WG", WG, t["wg"].rearrange("p (k n) -> p k n", k=2), w)
                load("MW", MW, t["mw"].rearrange("p (k n) -> p k n", k=2), w)
                load("GW", GW, t["gw"].rearrange("p (k n) -> p k n", k=2), w)
                load("WD", WD, t["wd"].rearrange("p (k n) -> p k n", k=11), w)

            def prep_ffn(th):
                th.start()
                f = th.cut(256, 64).rearrange("p (a n) -> p a n", a=4)
                v = V.put(op(lambda e: e.tensor_copy, f[:, 0, :], invt[:, :]), loads["invt"])
                v = V.put(op(lambda e: e.tensor_scalar, f[:, 1, :], f[:, 0, :], 0.0, 64.0, ALU.is_lt, ALU.mult), v)
                v = V.put(op(lambda e: e.tensor_tensor, f[:, 2, :], f[:, 0, :], f[:, 1, :], ALU.add), v)
                v = V.put(op(lambda e: e.tensor_scalar, f[:, 3, :], f[:, 2, :], 0.0, 63.0, ALU.max, ALU.min), v)
                pm = V.put(op(lambda e: e.tensor_scalar, PM, f[:, 3, :], SB["eid"][0:64, 0:1], None, ALU.is_equal),
                           v, loads["eid"], *moe_last)
                for g in range(8):
                    b, ps = th.bank()
                    for k in range(2):
                        tok = T.put(mm(ps[0:64, 0:352], MW[:, k, :], WG[:, k, g * 352:g * 352 + 352], k == 0, k == 1),
                                    loads["MW"], loads["WG"])
                    th.free[b] = v = V.put(op(lambda e: e.tensor_scalar, MG[:, g * 352:g * 352 + 352], ps[0:64, 0:352],
                    SB["mg"][0:64, g:g + 1], None, ALU.mult),
                                           tok, loads["mg"])
                ffn_ok.extend((pm, v))
                th.end()

            ffn_ok = []

            def stage6(th, blk):
                th.start(blk)
                t0 = blk * TB
                h = th.cut(512).rearrange("p (t c) -> p t c", t=TB)
                hT = th.cut(512).rearrange("p (k n) -> p k n", k=2)
                r = lambda n: th.cut(TB * n).rearrange("p (t n) -> p t n", t=TB)
                sc, we, t8 = r(64), r(64), r(8)
                mx = th.sm(32)
                weT = th.cut(256, 64)
                soT = th.cut(256, 64)
                s8 = th.cut(8 * 16).rearrange("p (a t g) -> p a t g", a=8, t=TB)
                fl, nz = r(64), r(64)
                sg = th.cut(2 * 176).rearrange("p (a n) -> p a n", a=2)
                AG = th.cut(1408)
                AT = th.cut(1408).rearrange("p (k n) -> p k n", k=11)
                hn = norm(th, blk, lambda i, x: [(h[:, i, :], x)])
                ht = turned(th, h, hn, hT[:, :, :])
                b, ps = th.bank()
                for i in range(TB):
                    for k in range(2):
                        tok = T.put(mm(ps[:, 64 * i:64 * i + 64], hT[:, k, i * P:i * P + P], GW[:, k, :],
                                       k == 0, k == 1), ht, loads["GW"])
                fr, v = row_softmax(th, ps[:, 0:128].rearrange("p (t n) -> p t n", t=TB), sc[:, :, :], mx[:, 0:2],
                                    mx[:, 2:4], TB, tok)
                th.free[b] = fr
                v = V.put(op(lambda e: e.tensor_tensor, sc[:, :, :], sc[:, :, :],
                    mx[:, 2:4].unsqueeze(2).broadcast_to([P, TB, 64]), ALU.mult), v)
                for i in range(TB):
                    v1 = V.put(op(lambda e: e.max, t8[:, i, :], sc[:, i, :]), v)
                    v1 = V.put(op(lambda e: e.match_replace, we[:, i, :], t8[:, i, :], sc[:, i, :], 0.0), v1)
                v = V.put(op(lambda e: e.tensor_tensor, we[:, :, :], sc[:, :, :], we[:, :, :], ALU.subtract), v1)
                b, ps = th.bank()
                for i in range(TB):
                    tok = T.put(op(lambda e: e.transpose, ps[0:64, i * P:i * P + P], we[:, i, :], ident), v)
                th.free[b] = v = V.put(op(lambda e: e.tensor_copy, weT, ps[0:64, 0:256]), tok)
                b, ps = th.bank()
                T.wait(*ffn_ok)
                for i in range(TB):
                    tok = T.put(mm(ps[:, 64 * i:64 * i + 64], weT[:, i * P:i * P + P], PM, True, True), v)
                f3 = ps[:, 0:128].rearrange("p (a i) -> p a i", i=8)
                s2 = lambda n: s8[:, n, :, :].rearrange("p t g -> p (t g)")
                g3 = lambda w: w[:, :, :].rearrange("p t (g i) -> p (t g) i", i=8)
                s_ok = V.put(op(lambda e: e.tensor_reduce, s2(0), f3, AX, ALU.add), tok)
                v = V.put(op(lambda e: e.tensor_scalar, g3(nz), f3, 0.0, -1e9, ALU.is_equal, ALU.mult))
                th.free[b] = v = V.put(op(lambda e: e.tensor_tensor, g3(fl), f3, g3(nz), ALU.add), v)
                v = V.put(op(lambda e: e.tensor_reduce, s2(1), g3(fl), AX, ALU.max), v)
                bc = lambda n: s2(n).unsqueeze(2).broadcast_to([P, TB * 8, 8])
                v = V.put(op(lambda e: e.tensor_tensor, g3(fl), g3(fl), bc(1), ALU.subtract), v)
                a = A.put(op(lambda e: e.activation, fl[:, :, :], fl[:, :, :], ACT.Exp), v)
                v = V.put(op(lambda e: e.tensor_reduce, s2(2), g3(fl), AX, ALU.add), a)
                v = V.put(op(lambda e: e.reciprocal, s2(3), s2(2)), v)
                v = V.put(op(lambda e: e.tensor_tensor, g3(fl), g3(fl), bc(3), ALU.mult), v)
                b, ps = th.bank()
                for i in range(TB):
                    tok = T.put(op(lambda e: e.transpose, ps[0:64, i * P:i * P + P], fl[:, i, :], ident), v)
                th.free[b] = so = V.put(op(lambda e: e.tensor_copy, soT, ps[0:64, 0:256]), tok)
                atr = None
                sgr = [None] * 2
                agr = None
                fin = []
                for i in range(TB):
                    ts = slice(i * P, i * P + P)
                    for g in range(8):
                        b, ps = th.bank()
                        gs = slice(g * 352, g * 352 + 352)
                        for k in range(2):
                            T.put(mm(ps[:, 0:352], hT[:, k, ts], WG[:, k, gs], k == 0, False))
                        tok = T.put(mm(ps[:, 0:352], soT[:, ts], MG[:, gs], False, True), so)
                        a = A.put(op(lambda e: e.activation, sg[:, g % 2, :], ps[:, 0:176], ACT.Silu), tok, sgr[g % 2])
                        V.wait(agr)
                        th.free[b] = sgr[g % 2] = v = V.put(op(lambda e: e.scalar_tensor_tensor, 
                    AG[:, g * 176:g * 176 + 176], sg[:, g % 2, :], s8[:, 0, i, g:g + 1], ps[:, 176:352],
                    ALU.mult, ALU.mult), a, s_ok)
                    for c in range(3):
                        b, ps = th.bank()
                        n = min(4, 11 - 4 * c)
                        for q in range(n):
                            c0 = (4 * c + q) * P
                            tok = T.put(op(lambda e: e.transpose, ps[:, q * P:q * P + P], AG[:, c0:c0 + P], ident), v)
                        th.free[b] = at = A.put(op(lambda e: e.activation, 
                    AT[:, 4 * c:4 * c + n, :], ps[:, 0:n * P].rearrange("p (k n) -> p k n", k=n), ACT.Copy),
                            tok, atr)
                    agr = tok
                    b, ps = th.bank()
                    for q in range(11):
                        tok = T.put(mm(ps[:, 0:256], AT[:, q, :], WD[:, q, :], q == 0, q == 10), at, loads["WD"])
                    atr = tok
                    th.free[b] = v = V.put(op(lambda e: e.tensor_tensor, X[:, t0 + i, :], ps[:, 0:256], X[:, t0 + i, :],
                    ALU.add), tok)
                    S.dma(op(lambda e: e.dma_start, out[(t0 + i) * P:(t0 + i) * P + P, :], X[:, t0 + i, :]), s_out, v)
                th.end(blk)

            s_out = sem("s_out")
            om_ok = V.put(op(lambda e: e.tensor_scalar, om[:, :], SB["mix"][:, :], -1.0, 1.0, ALU.mult, ALU.add),
                          loads["mix"])
            tdn, tfn = acst[:, 16:18], SB["tdf"][:, 2:4]
            a = A.put(op(lambda e: e.activation, acst[:, 12:14], SB["tdf"][:, 0:2], ACT.Exp), loads["tdf"])
            v = V.put(op(lambda e: e.tensor_scalar, tdn, acst[:, 12:14], -1.0, None, ALU.mult), a)
            z = G.put(op(lambda e: e.memset, td65[:, :], 0.0))
            for k in range(2):
                v = V.put(op(lambda e: e.tensor_scalar, td65v[:, k, :, 1:65], td65v[:, k, :, 1:65], tdn[:, k:k + 1],
                             None, ALU.add), v, z)
            td_ok = G.put(op(lambda e: e.memset, td65v[:, :, :, 0:1], NEG), v)
            load_moe()
            plan(threads, products, (stage1, stage2, stage3, stage4, stage5), load_ffn, prep_ffn, stage6)
            return queues

        T, V, A, G, S = program()
        print("estimated", order((T, V, A, G, S)) / 1000)
        block = ctx.enter_context(nc.Block())

        @block.sync
        def _(eng):
            S.play(eng)
            eng.wait_ge(sem("s_out"), 16 * NT)

        @block.tensor
        def _(eng):
            T.play(eng)

        @block.vector
        def _(eng):
            V.play(eng)

        @block.scalar
        def _(eng):
            A.play(eng)

        @block.gpsimd
        def _(eng):
            G.play(eng)


def plan(lanes, products, stages, load_ffn, prep_ffn, last):
    turn = [0]

    def lane():
        turn[0] += 1
        return lanes[turn[0] % len(lanes)]

    n = len(stages)
    for d in range(NBLK + n - 1):
        if d in (0, 1):
            products(lane(), 2 * d)
            products(lane(), 2 * d + 1)
        for s in range(n):
            if 0 <= d - s < NBLK:
                stages[s](lane(), d - s)
        if d == NBLK + 1:
            load_ffn()
            prep_ffn(lane())
    for b in range(NBLK):
        last(lane(), b)


def constants():
    i = np.arange(128)
    same = (i[:, None] // 64) == (i[None, :] // 64)
    f = np.float32
    inv = (f(1.0) / np.power(f(10000.0), np.arange(0, 64, 2, dtype=f) / f(64))).astype(f)
    fr = np.arange(64, dtype=f)[:, None] * inv[None, :]
    s, c = np.repeat(np.sin(fr), 2, axis=-1).astype(f), np.repeat(np.cos(fr), 2, axis=-1).astype(f)
    s[:, :32] = -s[:, :32]
    col = np.arange(64)
    return {
        "ident": np.eye(128, dtype=f),
        "tri": (same & (i[:, None] <= i[None, :])).astype(f),
        "gt": (same & (i[:, None] > i[None, :])).astype(f),
        "cos": np.ascontiguousarray(np.concatenate([c, c])), "sin": np.ascontiguousarray(np.concatenate([s, s])),
        "mv": ((i[:, None] // 64) == ((col[None, :] // 8) % 2)).astype(f),
        "mk": (((i[:, None] % 64) // 8) == np.arange(8)[None, :]).astype(f),
        "mg": (((i[:, None] % 64) // 8) == np.arange(8)[None, :]).astype(f),
        "eid": i[:, None].astype(f),
    }


def kernel(**inputs):
    import concourse.bacc as bacc
    from concourse.bass_utils import run_bass_kernel_spmd

    a = {k: np.asarray(v) for k, v in inputs.items()}

    def ks(w, k=2):
        n = w.shape[-1]
        return w.reshape(k, 128, n).transpose(1, 0, 2).reshape(128, k * n)

    def rep(v):
        return np.broadcast_to(v.reshape(1, -1), (128, v.size))

    L0 = lambda n: a["L0_" + n]
    L1 = lambda n: a["L1_" + n]
    ar = dict(constants())
    ctx = a["ctx_512"]
    ar["x"] = a["x"].reshape(4096, 256)
    ar["ctx"] = ctx
    ar["ctxT"] = ctx.transpose(0, 2, 1).reshape(32, 128, 64)
    ar["w_in"] = ks(L0("attn_in_proj_w"))
    ar["nscale"] = L0("attn_norm_scale").reshape(2, 128).T
    ar["convw"] = L0("attn_conv_weight").reshape(4, 4, 128).transpose(2, 1, 0).reshape(128, 16)
    ar["convb"] = L0("attn_conv_bias").reshape(4, 128).T
    ar["dskip"] = L0("attn_D").reshape(4, 128).T
    ar["alog"] = rep(L0("attn_A_log"))
    ar["dtb"] = rep(L0("attn_dt_bias"))
    ar["w_out"] = ks(L0("attn_out_proj_w"), 4)
    ar["wq"] = L0("xattn_Wq").reshape(16, 128, 256).transpose(1, 0, 2)
    ar["wkcq"] = L0("xattn_w_kc_q").reshape(16, 128, 2, 96).transpose(3, 2, 0, 1)
    ar["wqr"] = L0("xattn_W_qr").transpose(2, 0, 1)
    ar["wkr"] = L0("xattn_W_kr").transpose(2, 0, 1)
    ar["wkc"] = L0("xattn_w_kc_kv").transpose(1, 0, 2)
    ar["wo"] = L0("xattn_Wo").reshape(256, 16, 128).transpose(2, 1, 0)
    up = np.concatenate([L0("ffn_Wup"), L0("ffn_Wsu")[None]])
    ga = np.concatenate([L0("ffn_Wgate"), L0("ffn_Wsg")[None]])
    dn = np.concatenate([L0("ffn_Wdown"), L0("ffn_Wsd")[None]])
    w = np.stack([up, ga, dn]).reshape(3, 8, 2, 128, 256)
    ar["moe_w"] = w.transpose(3, 1, 0, 2, 4).reshape(128, 8, 1536)
    bb = np.stack([np.concatenate([L0("ffn_bup"), L0("ffn_bsu")[None]]),
                   np.concatenate([L0("ffn_bgate"), L0("ffn_bsg")[None]])])
    ar["moe_b"] = bb.reshape(2, 8, 2, 128).transpose(3, 0, 1, 2)
    ar["bdn"] = np.concatenate([L0("ffn_bdown"), L0("ffn_bsd")[None]])
    ar["moe_r"] = L0("ffn_Wr").reshape(2, 128, 7).transpose(1, 0, 2)
    ar["rb"] = rep(L0("ffn_br"))
    ar["gb"] = rep(L0("ffn_gate_bias"))
    mixes = np.stack([L1("attn_time_mix_key"), L1("attn_time_mix_value"), L1("attn_time_mix_receptance")])
    ar["mix"] = mixes.reshape(3, 2, 128).transpose(2, 0, 1).reshape(128, 6)
    ar["tdf"] = np.stack([L1("attn_time_decay"), L1("attn_time_first")]).reshape(4, 128).T
    ar["w_kvro"] = np.stack([L1("attn_Wk"), L1("attn_Wv"), L1("attn_Wr"), L1("attn_Wo")]) \
        .reshape(4, 2, 128, 256).transpose(2, 0, 1, 3).reshape(128, 2048)
    gu = np.concatenate([L1("ffn_gate_proj_w"), L1("ffn_up_proj_w")], axis=1)
    ar["wg"] = gu.reshape(8 * 352, 2, 128).transpose(2, 1, 0).reshape(128, 5632)
    ar["mw"] = L1("ffn_mask_up_w").transpose(1, 0, 2).reshape(2, 128, 64).transpose(1, 0, 2).reshape(128, 128)
    ar["gw"] = L1("ffn_gate_w").reshape(64, 2, 128).transpose(2, 1, 0).reshape(128, 128)
    ar["wd"] = L1("ffn_down_proj_w").transpose(0, 2, 1).reshape(11, 128, 256).transpose(1, 0, 2).reshape(128, 2816)
    ar["invt"] = np.broadcast_to(L1("ffn_inv_map").reshape(1, 64), (64, 64))

    nc = bacc.Bacc("TRN2", target_bir_lowering=False, num_devices=1)
    arrays, aps = {}, {}
    for name, v in ar.items():
        v = np.ascontiguousarray(v)
        arrays["in_" + name] = v
        aps[name] = nc.dram_tensor("in_" + name, v.shape, mybir.dt.from_np(v.dtype), kind="ExternalInput").ap()
    out = nc.dram_tensor("out_0", (4096, 256), F32, kind="ExternalOutput").ap()
    build(nc, aps, out)
    r = run_bass_kernel_spmd(nc, [arrays], core_ids=[0])
    return r.results[0]["out_0"].reshape(64, 64, 256)
```

```python
from contextlib import ExitStack

import numpy as np
import concourse.bass as bass
from concourse import mybir

ALU = mybir.AluOpType
ACT = mybir.ActivationFunctionType
F32 = mybir.dt.float32
U32 = mybir.dt.uint32
NJ = 70
I32 = mybir.dt.int32
AX = mybir.AxisListType.X

P = 128
NT = 32
TB = 2
NB = 4
NBLK = NT // TB
NTH = 4
LATER1, LATER2 = 13, 3
ARENA = 5680
SMALL = 400
LANE_BANKS = [(0, 1), (2, 3), (4, 5), (6, 7)]
NH = 16
NEG = -1.0e38


class Call:

    def __init__(self, select, args, kwargs):
        self.select, self.args, self.kwargs = select, args, kwargs

    def on(self, eng):
        return self.select(eng)(*self.args, **self.kwargs)


class Made(Call):

    def __init__(self, fn, ns):
        self.fn, self.ns, self.args = fn, ns, (None, None, None)

    def on(self, eng):
        return self.ns if isinstance(eng, Lengths) else self.fn(eng)


def op(select, *args, **kwargs):
    return Call(select, args, kwargs)


def width(ap):
    n = 1
    for d in ap.shape[1:]:
        n *= d
    return n


def pointers(args):
    return sum(not isinstance(a, (int, float)) and a is not None and len(a.shape) == 2 and a.shape[1] == 1
               for a in args)


class Lengths:

    def matmul(self, out, lhsT, rhs, **_):
        return max(4 * width(rhs) / 2.4, 107 + width(rhs) / 1.2)

    def transpose(self, out, in_, ident):
        return width(out) / 1.2

    def activation(self, out, in_, func, bias=0.0, **_):
        return 70 + width(out) / 1.2 + 93 * pointers([bias])

    def tensor_scalar(self, out, in0, scalar1, scalar2, *_):
        return 65 + width(out) / 0.96 / (2 if "SB" in str(in0.space) else 1) + 65 * min(1, pointers([scalar1, scalar2]))

    def scalar_tensor_tensor(self, out, in0, scalar, *_):
        return 65 + width(out) / 0.96 + 65 * pointers([scalar])

    def flat(self, out, *_):
        return 68 + width(out) / 0.96

    def reciprocal(self, out, in_):
        return 68 + 6.25 * width(out)

    def reduce(self, out, in_, *_):
        return 68 + width(in_) / 0.96

    def match_replace(self, out, *_):
        return 136 + width(out) / 0.96

    def scan(self, out, *_):
        return 68 + width(out) / 0.96

    def dma_start(self, out, in_):
        return 60

    tensor_tensor = tensor_copy = memset = bn_aggr = flat
    tensor_reduce = bn_stats = max = reduce
    tensor_tensor_scan = scan


class PoolLengths(Lengths):
    def tensor_tensor(self, out, in0, in1, how):
        return 150 + width(out) * (2.1 if how != ALU.pow else 250)

    def tensor_scalar(self, out, *_):
        return 150 + width(out) * 1.5

    def memset(self, out, _):
        return 40 + width(out) * 0.85

    def indirect_dma_start(self, *_):
        return 1000


TABLES = {ACT.Exp: 1, ACT.Silu: 2, ACT.Ln: 3}
TABLE_NS = 1283
SWITCH_NS = 1283
LAG = {"pe": 197, "act": 150, "dve": 128, "pool": 90, "sp": 2500}
PE_LAG = 125


class Ins:
    def __init__(self, queue, call, after, lane, job):
        self.queue, self.call, self.after, self.lane, self.job = queue, call, after, lane, job
        self.sem, self.step, self.value, self.end, self.used = None, 1, 0, None, False


class Queue:

    def __init__(self, name, sem, lengths):
        self.name, self.sem, self.lengths = name, sem, lengths
        self.lanes, self.pending, self.lane, self.job = {}, {}, -1, 0
        self.order = []

    def wait(self, *tokens):
        self.pending.setdefault(self.lane, []).extend(x for x in tokens if x is not None)

    def put(self, call, *tokens):
        self.wait(*tokens)
        ins = Ins(self, call, self.pending.pop(self.lane, []), self.lane, self.job)
        ins.sem = self.sem
        self.lanes.setdefault(self.lane, []).append(ins)
        return ins

    def dma(self, call, sem, *tokens):
        ins = self.put(call, *tokens)
        ins.sem, ins.step, ins.used = sem, 16, True
        return ins

    @property
    def last(self):
        lane = self.lanes.get(self.lane)
        return lane[-1] if lane else None

    def play(self, eng):
        seen = {}
        for ins in self.order:
            last = {}
            for dep in ins.after:
                if seen.get(id(dep.sem), 0) < dep.value:
                    seen[id(dep.sem)] = dep.value
                    last[id(dep.sem)] = dep.sem
            for key, sem in last.items():
                eng.wait_ge(sem, seen[key])
            done = ins.call.on(eng)
            if ins.used:
                done.then_inc(ins.sem, ins.step)


class ArrayClock:

    WINDOW = 4096 / 1.2

    def __init__(self):
        self.at, self.busy, self.cold = 0, 0.0, True

    def run(self, start, length):
        while True:
            while start >= (self.at + 1) * self.WINDOW:
                self.cold = self.busy < 0.4 * self.WINDOW
                self.at, self.busy = self.at + 1, 0.0
            rate = 0.5 if self.cold else 1.0
            room = (self.at + 1) * self.WINDOW - start
            if length / rate <= room:
                self.busy += length / rate
                return start + length / rate
            length -= room * rate
            self.busy += room
            start += room + 1e-6


def order(queues):
    clock = {q: 0.0 for q in queues}
    heads = {(q, lane): 0 for q in queues for lane in q.lanes}
    ready = {}
    counts = {}
    table = [0]
    clk = ArrayClock()

    def other(ins):
        t = TABLES.get(ins.call.args[2], 0) if ins.queue.name == "act" else 0
        return t if t != table[0] else 0

    left = sum(len(v) for q in queues for v in q.lanes.values())
    while left:
        best = None
        for (q, lane), n in heads.items():
            ins = q.lanes[lane][n] if n < len(q.lanes[lane]) else None
            if ins is None:
                continue
            at = ready.get(ins)
            if at is None:
                at = 0.0
                for dep in ins.after:
                    if dep.end is None:
                        at = None
                        break
                    at = max(at, dep.end + (LAG["sp"] if dep.step == 16 else LAG[dep.queue.name]) + (PE_LAG if q.name == "pe" else 0))
                if at is None:
                    continue
                ready[ins] = at
            key = (max(at, clock[q]) + (SWITCH_NS if other(ins) else 0), ins.job)
            if best is None or key < best[0]:
                best = (key, q, lane, ins)
        assert best is not None, "the lanes wait for each other"
        (start, _), q, lane, ins = best
        heads[(q, lane)] += 1
        length = ins.call.on(q.lengths)
        if other(ins):
            table[0] = other(ins)
            start += TABLE_NS - SWITCH_NS
        clock[q] = clk.run(start, length) if q.name == "pe" else start + length
        ins.end = clock[q]
        q.order.append(ins)
        left -= 1
    for q in queues:
        for ins in q.order:
            for dep in ins.after:
                dep.used = True
    for q in queues:
        for ins in q.order:
            if ins.used:
                counts[id(ins.sem)] = counts.get(id(ins.sem), 0) + ins.step
                ins.value = counts[id(ins.sem)]
    return max(clock.values())


CONSTS = {"ident": 128, "tri": 128, "gt": 128, "cos": 64, "sin": 64, "mv": 64, "mk": 8, "mg": 8, "eid": 1,
          "lt": 128, "one": 128, "jj": 70}
PARAMS = {
    "w_in": 2 * 1284, "nscale": 2, "convw": 16, "convb": 4, "dskip": 4, "alog": 4, "dtb": 4, "w_out": 4 * 256,
    "rb": 7, "gb": 7, "mix": 6, "tdf": 4, "w_kvro": 8 * 256,
}


def build(nc, t, out):
    ctx = ExitStack()
    with ctx:
        def sb(name, n, parts=P, dt=F32):
            return ctx.enter_context(nc.sbuf_tensor(name, [parts, n], dt))

        sems = {}

        def sem(name):
            if name not in sems:
                sems[name] = ctx.enter_context(nc.semaphore(name))
            return sems[name]

        SB = {n: sb("c_" + n, w) for n, w in {**CONSTS, **PARAMS}.items() if n not in ("w_in", "w_out")}
        EARLY = sb("EARLY", 2568 + 1024 + 2048 + 2048)
        SB["w_in"], SB["w_out"] = EARLY[:, 0:2568], EARLY[:, 2568:3592]
        X = sb("X", NT * 256)[:, :].rearrange("p (t c) -> p t c", t=NT)
        Aw = EARLY[:, 3592:5640].rearrange("p (k n) -> p k n", k=2)
        Bw = EARLY[:, 5640:7688].rearrange("p (h n) -> p h n", h=8)
        BIG = sb("BIG", 12448)
        acst = sb("acst", 64)
        mhalf = sb("mhalf", 8)
        td65 = sb("td65", 2 * NB * 65)
        zrow = sb("zrow", 256)
        om = sb("om", 6)
        invt = sb("invt", 64, 64, I32)
        MS = sb("MS", 224)[:, :].rearrange("p (e t) -> p e t", e=7)
        PR = sb("PR", 224)[:, :].rearrange("p (e t) -> p e t", e=7)
        pAB = sb("pAB", 64)[:, :].rearrange("p (a t) -> p a t", a=2)
        posi = sb("posi", 64, P, U32)[:, :].rearrange("p (a t) -> p a t", a=2)
        tei = sb("tei", 2 * NJ, P, I32)[:, :].rearrange("p (a t) -> p a t", a=2)
        hd = nc.dram_tensor("rows_by_token", (NT * P, 256), F32).ap()
        hs_d = nc.dram_tensor("rows_by_slot", (NJ * P, 256), F32).ap()
        ys_d = nc.dram_tensor("results_by_slot", (NJ * P, 256), F32).ap()
        bdn = sb("bdn", 256, 8)
        arenas = [sb(f"arena{i}", ARENA) for i in range(NTH - 1)] + [BIG]
        stores = [sb(f"small{i}", SMALL) for i in range(NTH)]
        banks = [ctx.enter_context(nc.psum_tensor(f"ps{i}", [P, 512], F32)) for i in range(8)]

        def program():
            T = Queue("pe", sem("s_pe"), Lengths())
            V = Queue("dve", sem("s_dve"), Lengths())
            A = Queue("act", sem("s_act"), Lengths())
            G = Queue("pool", sem("s_pool"), PoolLengths())
            S = Queue("sp", sem("s_sp"), Lengths())
            queues = (T, V, A, G, S)

            ident = SB["ident"][:, :]

            loads = {}

            def load(name, dst, src, wait=()):
                s = sem("l_" + name)
                S.wait(*wait)
                loads[name] = S.dma(op(lambda e: e.dma_start, dst, src), s)

            xsem = []

            def load_x(n):
                xsem.append(S.dma(op(lambda e: e.dma_start, X[:, 4 * n:4 * n + 4, :],
                    t["x"][512 * n:512 * n + 512, :].rearrange("(t p) c -> p t c", p=P)),
                      sem(f"l_x{n}")))

            load_x(0)
            for name in ("ident", "nscale", "w_in", "convw", "convb", "dskip", "alog", "dtb", "tri", "gt", "w_out"):
                load(name, SB[name][:, :], t[name])
            load_x(1)

            for n in range(2, 8):
                load_x(n)
            for name in ("cos", "sin", "lt", "one", "jj", "mv", "mk", "mg", "eid", "rb", "gb", "mix", "tdf", "w_kvro"):
                load(name, SB[name][:, :], t[name])
            load("invt", invt[:, :], t["invt"])

            ROUTED = BIG[:, 0:10752].rearrange("p (a e n) -> p a e n", a=3, e=7)
            SHARED = BIG[:, 10752:12288]
            UP, UG, UD = (SHARED[:, 512 * n:512 * n + 512].rearrange("p (k n) -> p k n", k=2) for n in range(3))
            moe_b = BIG[:, 12288:12320].rearrange("p (a e k) -> p a e k", a=2, e=8)
            moe_r = BIG[:, 12320:12334].rearrange("p (k n) -> p k n", k=2)
            WG = BIG[:, 0:5632].rearrange("p (k n) -> p k n", k=2)
            WD = BIG[:, 5632:8448].rearrange("p (k n) -> p k n", k=11)
            MG = BIG[0:64, 8448:11264]
            MW = BIG[:, 11264:11392].rearrange("p (k n) -> p k n", k=2)
            GW = BIG[:, 11392:11520].rearrange("p (k n) -> p k n", k=2)
            PM = BIG[0:64, 11520:11584]

            w_in = SB["w_in"][:, :].rearrange("p (k n) -> p k n", k=2)
            w_out = SB["w_out"][:, :].rearrange("p (k n) -> p k n", k=4)
            convw = SB["convw"][:, :].rearrange("p (f k) -> p f k", f=4)
            kvro = SB["w_kvro"][:, :].rearrange("p (m k n) -> p m k n", m=4, k=2)
            mix = SB["mix"][:, :].rearrange("p (m k) -> p m k", m=3)
            omx = om[:, :].rearrange("p (m k) -> p m k", m=3)
            td65v = td65[:, :].rearrange("p (k b s) -> p k b s", k=2, b=NB)
            tdf = SB["tdf"]

            def mm(out_ap, lhsT, rhs, start, stop):
                return op(lambda e: e.matmul, out_ap, lhsT, rhs, start=start, stop=stop, skip_group_check=True)

            half = V.put(op(lambda e: e.memset, mhalf[:, :], -0.5))
            win_ok = []
            V.wait(loads["w_in"], loads["nscale"])
            for k in range(2):
                win_ok.append(V.put(op(lambda e: e.tensor_scalar, w_in[:, k, :], w_in[:, k, :],
                    SB["nscale"][:, k:k + 1], None, ALU.mult)))
            win_ok = win_ok[-1]
            ea = A.put(op(lambda e: e.activation, acst[:, 0:4], SB["alog"][:, :], ACT.Exp), loads["alog"])
            a_ok = V.put(op(lambda e: e.tensor_scalar, acst[:, 4:8], acst[:, 0:4], -1.0, None, ALU.mult), ea)

            jobs = [0]

            class Thread:
                def __init__(self, i):
                    self.i, self.done, self.at = i, [], 0
                    self.banks = LANE_BANKS[i]
                    self.arena = arenas[i]
                    self.free = {b: None for b in self.banks}
                    self.csem = sem(f"s_ctx{i}")
                    self.esem = (sem(f"s_ea{i}"), sem(f"s_eb{i}"))
                    self.rsem, self.wsem, self.gsem = sem(f"s_rd{i}"), sem(f"s_wr{i}"), sem(f"s_sw{i}")

                def bank(self):
                    b = self.banks[self.at % len(self.banks)]
                    self.at += 1
                    T.wait(self.free[b])
                    return b, banks[b]

                def start(self, blk=None, rank=0):
                    jobs[0] += 1
                    for q in queues:
                        q.lane, q.job = self.i, jobs[0]
                    self.ao = self.so = 0
                    for q in (V, G, S, A):
                        q.wait(*self.done)
                    if blk is not None:
                        for q in (V, G):
                            q.wait(*xdone.get(blk, ()))

                def cut(self, n, parts=P):
                    self.ao += n
                    assert self.ao <= ARENA, self.ao
                    return self.arena[0:parts, self.ao - n:self.ao]

                def sm(self, n):
                    self.so += n
                    assert self.so <= SMALL, self.so
                    return stores[self.i][:, self.so - n:self.so]

                def end(self, blk=None):
                    self.done = [q.last for q in (T, V, A, G)]
                    if blk is not None:
                        xdone[blk] = list(self.done)
                    for q in queues:
                        q.lane, q.job = -1, 0

            xdone = {}
            threads = [Thread(i) for i in range(NTH)]

            def norm(th, blk, hview, rms=None):
                st = th.sm(12).rearrange("p (t c) -> p t c", t=TB)
                mv = th.sm(4).rearrange("p (t c) -> p t c", t=TB)
                w = th.sm(16).rearrange("p (a t) -> p a t", t=TB)
                V.wait(xsem[blk * TB // 4])
                for i in range(TB):
                    a = V.put(op(lambda e: e.bn_stats, st[:, i, :], X[:, blk * TB + i, :]))
                for i in range(TB):
                    a = V.put(op(lambda e: e.bn_aggr, mv[:, i, :], st[:, i, :]), a)
                a = V.put(op(lambda e: e.tensor_scalar, w[:, 0, :], mv[:, :, 1], 1e-5, None, ALU.add), a)
                g = G.put(op(lambda e: e.tensor_tensor, w[:, 1, :], w[:, 0, :], mhalf[:, 0:TB], ALU.pow), a, half)
                if rms is not None:
                    g = G.put(op(lambda e: e.tensor_tensor, w[:, 2, :], w[:, 1, :], w[:, 1, :], ALU.mult), g)
                    g = G.put(op(lambda e: e.tensor_tensor, w[:, 3, :], w[:, 2, :], mv[:, :, 1], ALU.mult), g)
                    g = G.put(op(lambda e: e.tensor_scalar, w[:, 4, :], w[:, 3, :], 1e-6, None, ALU.add), g)
                    g = G.put(op(lambda e: e.tensor_tensor, w[:, 5, :], w[:, 4, :], mhalf[:, 0:TB], ALU.pow), g)
                V.wait(g)
                for i in range(TB):
                    for dst, src in hview(i, X[:, blk * TB + i, :]):
                        a = V.put(op(lambda e: e.tensor_scalar, 
                    dst, src, mv[:, i, 0:1], w[:, 1, i:i + 1], ALU.subtract, ALU.mult))
                    if rms is not None:
                        b = V.put(op(lambda e: e.tensor_scalar, rms(i), hview(i, None)[0][0], w[:, 5, i:i + 1], None,
                    ALU.mult), a)
                        a = b
                return a

            def turned(th, h, ready, dst):
                b, ps = th.bank()
                T.wait(loads["ident"])
                for k in range(2):
                    for i in range(TB):
                        tok = T.put(op(lambda e: e.transpose, ps[:, k * 256 + i * P:k * 256 + i * P + P],
                    h[:, i, k * P:k * P + P], ident), ready)
                th.free[b] = c = A.put(op(lambda e: e.activation, dst, ps[:, :].rearrange("p (k n) -> p k n", k=2)
                    if len(dst.shape) == 3 else
                    ps[:, :].rearrange("p (k b s) -> p k b s", k=2, b=NB),
                    ACT.Copy), tok)
                return c

    
            def stage1(th, blk):
                th.start(blk)
                t0 = blk * TB
                hl = th.cut(512).rearrange("p (t c) -> p t c", t=TB)
                h = th.cut(512).rearrange("p (t c) -> p t c", t=TB)
                hT = th.cut(512).rearrange("p (k n) -> p k n", k=2)
                sT = th.cut(1024).rearrange("p (f n) -> p f n", f=4)
                gT = th.cut(1024).rearrange("p (f n) -> p f n", f=4)
                BC = th.cut(512).rearrange("p (f n) -> p f n", f=2)
                hn = norm(th, blk, lambda i, x: [(hl[:, i, :], x)], lambda i: h[:, i, :])
                xa = G.put(op(lambda e: e.tensor_tensor, X[:, t0:t0 + TB, :], X[:, t0:t0 + TB, :], hl[:, :, :], ALU.add), hn)
                ht = turned(th, h, hn, hT[:, :, :])
                dz = th.sm(64).rearrange("p (a c) -> p a c", a=8)
                b, ps = th.bank()
                T.wait(ht, win_ok)
                for i in range(TB):
                    for k in range(2):
                        tok = T.put(mm(ps[:, 4 * i:4 * i + 4], hT[:, k, i * P:i * P + P], w_in[:, k, 1024:1028],
                                       k == 0, k == 1))
                dtb = SB["dtb"][:, :].unsqueeze(1).broadcast_to([P, TB, 4])
                d2 = lambda j: dz[:, j, :].rearrange("p (t c) -> p t c", t=TB)
                th.free[b] = v = V.put(op(lambda e: e.tensor_tensor, d2(0), ps[:, 0:8].rearrange("p (t c) -> p t c", t=TB),
                    dtb, ALU.add), tok, loads["dtb"])
                v = V.put(op(lambda e: e.scalar_tensor_tensor, dz[:, 1, :], dz[:, 0, :], -1.0, dz[:, 0, :], ALU.mult, ALU.max), v)
                v2 = V.put(op(lambda e: e.tensor_scalar, dz[:, 4, :], dz[:, 0, :], 0.0, None, ALU.max))
                a = A.put(op(lambda e: e.activation, dz[:, 2, :], dz[:, 1, :], ACT.Exp, scale=-1.0), v)
                a = A.put(op(lambda e: e.activation, dz[:, 3, :], dz[:, 2, :], ACT.Ln, bias=1.0), a)
                v = V.put(op(lambda e: e.tensor_tensor, dz[:, 5, :], dz[:, 3, :], dz[:, 4, :], ALU.add), a, v2)
                dt_ok = V.put(op(lambda e: e.tensor_tensor, d2(6), d2(5), acst[:, 4:8].unsqueeze(1).broadcast_to([P, TB, 4]),
                    ALU.mult), v, a_ok)
                cv = th.cut(1024).rearrange("p (f n) -> p f n", f=4)
                g2nd = th.cut(512)
                V.wait(loads["convw"], loads["convb"])
                for g in range(2):
                    b, ps = th.bank()
                    for f in range(2):
                        for k in range(2):
                            c0 = 512 + (2 * g + f) * P
                            tok = T.put(mm(ps[:, f * 256:f * 256 + 256], w_in[:, k, c0:c0 + P], hT[:, k, :],
                                           k == 0, k == 1))
                    for f in range(2):
                        ff = 2 * g + f
                        src = ps[:, f * 256:f * 256 + 256]
                        s3 = src.rearrange("p (b s) -> p b s", b=NB)
                        c3 = cv[:, ff, :].rearrange("p (b s) -> p b s", b=NB)
                        v = V.put(op(lambda e: e.tensor_scalar, cv[:, ff, :], src, convw[:, ff, 3:4],
                    SB["convb"][:, ff:ff + 1], ALU.mult, ALU.add), tok)
                        for d in (1, 2, 3):
                            v = V.put(op(lambda e: e.scalar_tensor_tensor, c3[:, :, d:64], s3[:, :, 0:64 - d],
                    convw[:, ff, 3 - d:4 - d], c3[:, :, d:64],
                    ALU.mult, ALU.add), v)
                    th.free[b] = v
                    s_ok = A.put(op(lambda e: e.activation, sT[:, 2 * g:2 * g + 2, :], cv[:, 2 * g:2 * g + 2, :], ACT.Silu), v)
                for g in range(2):
                    b, ps = th.bank()
                    for f in range(2):
                        for k in range(2):
                            c0 = (2 * g + f) * P
                            tok = T.put(mm(ps[:, f * 256:f * 256 + 256], w_in[:, k, c0:c0 + P], hT[:, k, :],
                                           k == 0, k == 1))
                    th.free[b] = g_ok = A.put(op(lambda e: e.activation, 
                    gT[:, 2 * g:2 * g + 2, :], ps[:, :].rearrange("p (f n) -> p f n", f=2), ACT.Silu), tok)
                b, ps = th.bank()
                for f in range(2):
                    for k in range(2):
                        bc_mm = tok = T.put(mm(ps[:, f * 256:f * 256 + 256], w_in[:, k, 1028 + f * P:1156 + f * P],
                                               hT[:, k, :], k == 0, k == 1))
                th.free[b] = bc_ok = A.put(op(lambda e: e.activation, 
                    BC[:, :, :], ps[:, :].rearrange("p (f n) -> p f n", f=2), ACT.Copy), tok)
                T.wait(loads["tri"])
                for i in range(TB):
                    ts = slice(i * P, i * P + P)
                    xt = (hl, h)[i].rearrange("p t (a n) -> p (t a) n", a=2)
                    Gh = (hT.rearrange("p k n -> p (k n)"), g2nd)[i].rearrange("p (f n) -> p f n", f=4)
                    E = cv[:, 2 * i:2 * i + 2, :].rearrange("p a (b n) -> p (a b) n", b=2)
                    cbm = th.sm(128)
                    b, ps = th.bank()
                    for f in range(4):
                        tok = T.put(op(lambda e: e.transpose, ps[:, f * P:f * P + P], sT[:, f, ts], ident), s_ok)
                    A.wait(xa)
                    th.free[b] = xt_ok = A.put(op(lambda e: e.activation, 
                    xt[:, :, :], ps[:, :].rearrange("p (f n) -> p f n", f=4), ACT.Copy), tok)
                    G.wait(dt_ok, loads["gt"], bc_mm)
                    for f in range(4):
                        gh = G.put(op(lambda e: e.tensor_scalar, Gh[:, f, :], SB["gt"][:, :],
                                      dz[:, 6, 4 * i + f:4 * i + f + 1], 1.0, ALU.mult, ALU.mult))
                    b, ps2 = th.bank()
                    cb = T.put(mm(ps2[:, 0:P], BC[:, 0, ts], BC[:, 1, ts], True, True), bc_ok)
                    th.free[b] = cm = V.put(op(lambda e: e.tensor_tensor, cbm, ps2[:, 0:P], SB["tri"][:, :], ALU.mult),
                                            cb, loads["tri"])
                    b, ps3 = th.bank()
                    for f in range(4):
                        tok = T.put(mm(ps3[:, f * P:f * P + P], Gh[:, f, :], SB["tri"][:, :], True, True), gh)
                    th.free[b] = ex = A.put(op(lambda e: e.activation, 
                    E, ps3[:, :].rearrange("p (f n) -> p f n", f=4), ACT.Exp), tok)
                    for f in range(4):
                        m_ok = V.put(op(lambda e: e.scalar_tensor_tensor, Gh[:, f, :], E[:, f, :],
                    dz[:, 5, 4 * i + f:4 * i + f + 1], cbm,
                    ALU.mult, ALU.mult), ex, cm)
                    b, ps4 = th.bank()
                    for f in range(4):
                        tok = T.put(mm(ps4[:, f * P:f * P + P], xt[:, f, :], Gh[:, f, :], True, True), m_ok, xt_ok)
                    V.wait(loads["dskip"])
                    for f in range(4):
                        y = V.put(op(lambda e: e.scalar_tensor_tensor, xt[:, f, :], sT[:, f, ts], SB["dskip"][:, f:f + 1],
                    ps4[:, f * P:f * P + P], ALU.mult, ALU.add), tok)
                    th.free[b] = y
                    y = G.put(op(lambda e: e.tensor_tensor, xt[:, :, :], xt[:, :, :], gT[:, :, ts], ALU.mult), y, g_ok)
                    b, ps5 = th.bank()
                    for f in range(4):
                        tok = T.put(mm(ps5[:, 0:256], xt[:, f, :], w_out[:, f, :], f == 0, f == 3), y, loads["w_out"])
                    th.free[b] = V.put(op(lambda e: e.tensor_tensor, X[:, t0 + i, :], ps5[:, 0:256], X[:, t0 + i, :],
                    ALU.add), tok, xa)
                th.end(blk)

            def products(th, hf):
                th.start()
                wkcq = th.cut(2 * 4 * 128, 96).rearrange("p (c h k) -> p c h k", c=2, h=4)
                wqr = th.cut(4 * 192, 64).rearrange("p (h c) -> p h c", h=4)
                wkr = th.cut(4 * 64, 64).rearrange("p (h c) -> p h c", h=4)
                wq = th.cut(4 * 256).rearrange("p (h c) -> p h c", h=4)
                wkc = th.cut(4 * 64).rearrange("p (h c) -> p h c", h=4)
                wo = th.cut(4 * 256).rearrange("p (h c) -> p h c", h=4)
                g1 = th.cut(2 * 4 * 64, 96).rearrange("p (c h d) -> p c h d", c=2, h=4)
                g2 = th.cut(4 * 64).rearrange("p (h d) -> p h d", h=4)
                hs = slice(4 * hf, 4 * hf + 4)
                L = {}
                for name, dst, src in (("wqr", wqr, t["wqr"][:, hs, :]), ("wkr", wkr, t["wkr"][:, hs, :]),
                                       ("wkcq", wkcq, t["wkcq"][:, :, hs, :]), ("wq", wq, t["wq"][:, hs, :]),
                                       ("wkc", wkc, t["wkc"][:, hs, :]), ("wo", wo, t["wo"][:, hs, :])):
                    L[name] = S.dma(op(lambda e: e.dma_start, dst, src), sem(f"l_{name}{hf}"))
                b, ps = th.bank()
                for c in range(2):
                    for h in range(4):
                        c0 = (4 * c + h) * 64
                        tok = T.put(mm(ps[0:96, c0:c0 + 64], wqr[:, h, c * 96:c * 96 + 96], wkr[:, h, :],
                                       True, True), L["wqr"], L["wkr"])
                th.free[b] = v = V.put(op(lambda e: e.tensor_copy, g1[:, :, :, :],
                                          ps[0:96, :].rearrange("p (c h d) -> p c h d", c=2, h=4)), tok)
                b, ps = th.bank()
                for h in range(4):
                    for c in range(2):
                        tok = T.put(mm(ps[:, h * 64:h * 64 + 64], wkcq[:, c, h, :], g1[:, c, h, :],
                                       c == 0, c == 1), v, L["wkcq"])
                th.free[b] = v = V.put(op(lambda e: e.tensor_copy, g2[:, :, :],
                                          ps[:, 0:256].rearrange("p (h d) -> p h d", h=4)), tok)
                b, ps = th.bank()
                for k in range(2):
                    for h in range(4):
                        c0 = (4 * k + h) * 64
                        tok = T.put(mm(ps[:, c0:c0 + 64], wq[:, h, k * P:k * P + P], g2[:, h, :],
                                       True, True), v, L["wq"])
                th.free[b] = a = A.put(op(lambda e: e.activation, Aw[:, :, hf * 256:hf * 256 + 256],
                                          ps[:, :].rearrange("p (k n) -> p k n", k=2), ACT.Copy), tok)
                pre_done.append(a)
                b, ps = th.bank()
                for q in range(2):
                    for e2 in range(2):
                        tok = T.put(mm(ps[64 * e2:64 * e2 + 64, q * 256:q * 256 + 256], wkc[:, 2 * q + e2, :],
                                       wo[:, 2 * q + e2, :], True, True), L["wkc"], L["wo"])
                th.free[b] = v = V.put(op(lambda e: e.tensor_copy, Bw[:, 2 * hf:2 * hf + 2, :],
                                          ps[:, :].rearrange("p (q n) -> p q n", q=2)), tok)
                pre_done.append(v)
                th.end()

            pre_done = []

            def ctx_rows(th, blk, dst):
                for e2 in range(2):
                    ct = S.dma(op(lambda e: e.dma_start, dst[64 * e2:64 * e2 + 64, :, :],
                                  t["ctx"][NB * blk:NB * blk + NB, :, :].rearrange("b l d -> l b d")), th.csem)
                return ct

            def row_softmax(th, src, dst, mxs, sms, groups, tok, scale=1.0, n=64):
                v = V.put(op(lambda e: e.tensor_reduce, mxs, src, AX, ALU.max), tok)
                free = v = V.put(op(lambda e: e.tensor_tensor, dst, src, mxs.unsqueeze(2).broadcast_to([P, groups, n]),
                    ALU.subtract), v)
                a = A.put(op(lambda e: e.activation, dst, dst, ACT.Exp, scale=scale), v)
                v = V.put(op(lambda e: e.tensor_reduce, sms, dst, AX, ALU.add), a)
                return free, V.put(op(lambda e: e.reciprocal, sms, sms), v)

            def stage2(th, blk):
                th.start(blk)
                t0 = blk * TB
                qT = th.cut(2048).rearrange("p (h n) -> p h n", h=8)
                BD = th.cut(512).rearrange("p (b d) -> p b d", b=NB)
                BDT = th.cut(512).rearrange("p (b d) -> p b d", b=NB)
                pm = th.cut(1024)
                CT, R1, R2 = (pm[:, 256 * n:256 * n + 256].rearrange("p (b d) -> p b d", b=NB) for n in range(3))
                Pm = pm.rearrange("p (h n) -> p h n", h=8)
                pt_ = th.cut(1024)
                h = pt_[:, 0:512].rearrange("p (t c) -> p t c", t=TB)
                hT = pt_[:, 512:1024].rearrange("p (k n) -> p k n", k=2)
                PT = pt_.rearrange("p (h n) -> p h n", h=8)
                ct = ctx_rows(th, blk, CT)
                z = G.put(op(lambda e: e.memset, BD[:, :, :], 0.0))
                hn = norm(th, blk, lambda i, x: [(h[:, i, :], x)])
                cosb = SB["cos"][:, :].unsqueeze(1).broadcast_to([P, NB, 64])
                r1 = G.put(op(lambda e: e.tensor_tensor, R1[:, :, :], CT[:, :, :], cosb, ALU.mult), ct, loads["cos"], loads["sin"])
                for a0 in range(2):
                    r1 = G.put(op(lambda e: e.tensor_tensor, 
                    R2[:, :, 32 * a0:32 * a0 + 32], CT[:, :, 32 - 32 * a0:64 - 32 * a0],
                    SB["sin"][:, 32 * a0:32 * a0 + 32].unsqueeze(1).broadcast_to([P, NB, 32]), ALU.mult))
                for e2 in range(2):
                    rows = slice(64 * e2, 64 * e2 + 64)
                    kv = V.put(op(lambda e: e.tensor_tensor, BD[rows, :, rows], R1[rows, :, :], R2[rows, :, :], ALU.add),
                               r1, z)
                ht = turned(th, h, hn, hT[:, :, :])
                b, ps = th.bank()
                for j in range(NB):
                    tok = T.put(op(lambda e: e.transpose, ps[:, j * P:j * P + P], BD[:, j, :], ident), kv)
                th.free[b] = kt = A.put(op(lambda e: e.activation, BDT[:, :, :], ps[:, :].rearrange("p (b n) -> p b n", b=NB),
                    ACT.Copy), tok)
                T.wait(*pre_done)
                for g in range(4):
                    b, ps = th.bank()
                    for f in range(2):
                        hp = 2 * g + f
                        for k in range(2):
                            tok = T.put(mm(ps[:, f * 256:f * 256 + 256], Aw[:, k, hp * P:hp * P + P], hT[:, k, :],
                                           k == 0, k == 1), ht)
                    th.free[b] = qk = A.put(op(lambda e: e.activation, 
                    qT[:, 2 * g:2 * g + 2, :], ps[:, :].rearrange("p (f n) -> p f n", f=2), ACT.Copy), tok)
                mxs, sms = [th.sm(16) for _ in range(TB)], [th.sm(16) for _ in range(TB)]
                turned_p, pv_read, p_ok, pt = [None] * 2, [None], [None] * 2, [None]

                def scores(i, g):
                    b, ps = th.bank()
                    for b2 in range(2):
                        for q in range(4):
                            tok = T.put(mm(ps[64 * b2:64 * b2 + 64, q * P:q * P + P],
                                           qT[:, 4 * g + q, i * P + 64 * b2:i * P + 64 * b2 + 64],
                                           BDT[:, 2 * i + b2, :], True, True), qk, kt)
                    dst = Pm[:, 4 * g:4 * g + 4, :].rearrange("p h (e l) -> p (h e) l", e=2)
                    V.wait(turned_p[g])
                    fr, v = row_softmax(th, ps[:, :].rearrange("p (h l) -> p h l", h=8), dst,
                                        mxs[i][:, 8 * g:8 * g + 8], sms[i][:, 8 * g:8 * g + 8], 8, tok)
                    th.free[b] = fr
                    p_ok[g] = G.put(op(lambda e: e.tensor_tensor, dst, dst,
                                       sms[i][:, 8 * g:8 * g + 8].unsqueeze(2).broadcast_to([P, 8, 64]), ALU.mult), v)

                def turn(g):
                    b, ps = th.bank()
                    for q in range(4):
                        tok = T.put(op(lambda e: e.transpose, ps[:, q * P:q * P + P], Pm[:, 4 * g + q, :], ident),
                                    p_ok[g])
                    turned_p[g] = tok
                    A.wait(pv_read[0])
                    th.free[b] = pt[0] = A.put(op(lambda e: e.activation, PT[:, 4 * g:4 * g + 4, :],
                                                  ps[:, :].rearrange("p (h n) -> p h n", h=4), ACT.Copy), tok)

                def attended(i):
                    cT = qT[:, :, i * P:i * P + P]
                    for b2 in range(2):
                        b, ps = th.bank()
                        tok = T.put(mm(ps[:, :], BD[:, 2 * i + b2, :], PT[:, :, 64 * b2:64 * b2 + 64], True, True), pt[0])
                        th.free[b] = cx = A.put(op(lambda e: e.activation, cT[:, :, 64 * b2:64 * b2 + 64],
                                                   ps[:, :].rearrange("p (h n) -> p h n", h=8), ACT.Copy), tok)
                    pv_read[0] = tok
                    b, ps = th.bank()
                    for q in range(8):
                        tok = T.put(mm(ps[:, 0:256], cT[:, q, :], Bw[:, q, :], q == 0, q == 7), cx)
                    th.free[b] = V.put(op(lambda e: e.tensor_tensor, X[:, t0 + i, :], ps[:, 0:256], X[:, t0 + i, :],
                                          ALU.add), tok)

                scores(0, 0)
                scores(0, 1)
                turn(0)
                scores(1, 0)
                turn(1)
                attended(0)
                scores(1, 1)
                turn(0)
                turn(1)
                attended(1)
                th.end(blk)

            def load_moe():
                w = ()
                load("shared", SHARED, t["moe_w"][:, 7, :], w)
                load("moe_r", moe_r, t["moe_r"], w)
                load("moe_b", moe_b, t["moe_b"], w)
                load("bdn", bdn[:, :], t["bdn"], w)
                load_routed(2)

            def load_routed(a, *wait):
                load(f"moe{a}", ROUTED[:, a, :, :], t["moe_w"][:, 0:7, a * 512:a * 512 + 512], wait)

            def move_lane(th):
                load_routed(0, *th.done)
                load_routed(1, *th.done)
                th.arena = EARLY
                th.done = [x for o in threads for x in o.done] + th.done

            def stage3(th, blk, shared=True):
                th.start(blk)
                t0 = blk * TB
                h = th.cut(512).rearrange("p (t c) -> p t c", t=TB)
                hT = th.cut(512).rearrange("p (k n) -> p k n", k=2)
                hn = norm(th, blk, lambda i, x: [(h[:, i, :], x)])
                ht = turned(th, h, hn, hT[:, :, :])
                rows_st.append(S.dma(op(lambda e: e.dma_start, hd[t0 * P:(t0 + TB) * P, :].rearrange("(t p) c -> p t c", p=P),
                                        h[:, :, :]), th.wsem, hn))
                b, ps = th.bank()
                for i in range(TB):
                    for k in range(2):
                        tok = T.put(mm(ps[:, 8 * i:8 * i + 7], hT[:, k, i * P:i * P + P], moe_r[:, k, :],
                                       k == 0, k == 1), ht, loads["moe_r"])
                r = lambda n: th.sm(TB * n).rearrange("p (t n) -> p t n", t=TB)
                gl, W, W2, t8, ms, t2, gm, pr, mx, sm = (r(7), r(13), r(13), r(8), r(7), r(7), r(7), r(8), r(1), r(1))
                z = G.put(op(lambda e: e.memset, W[:, :, 7:13], 3.0e38))
                z = G.put(op(lambda e: e.memset, pr[:, :, 7:8], 1.0))
                bc = lambda n: SB[n][:, :].unsqueeze(1).broadcast_to([P, TB, 7])
                th.free[b] = v = V.put(op(lambda e: e.tensor_tensor, 
                    gl[:, :, :], ps[:, 0:16].rearrange("p (t n) -> p t n", t=TB)[:, :, 0:7], bc("rb"), ALU.add),
                    tok, loads["rb"], loads["gb"])
                v = V.put(op(lambda e: e.tensor_tensor, W[:, :, 0:7], gl[:, :, :], bc("gb"), ALU.add), v, z)
                for i in range(TB):
                    v1 = V.put(op(lambda e: e.max, t8[:, i, :], W[:, i, :]), v)
                    v1 = V.put(op(lambda e: e.match_replace, W2[:, i, :], t8[:, i, :], W[:, i, :], -3.3e38), v1)
                v = V.put(op(lambda e: e.tensor_tensor, ms[:, :, :], W2[:, :, 0:7], W[:, :, 0:7], ALU.not_equal), v1)
                V.put(op(lambda e: e.tensor_copy, MS[:, :, t0:t0 + TB], ms.rearrange("p t e -> p e t")), v)
                v = V.put(op(lambda e: e.tensor_scalar, t2[:, :, :], ms[:, :, :], 1e30, -1e30, ALU.mult, ALU.add), v)
                v = V.put(op(lambda e: e.tensor_tensor, gm[:, :, :], gl[:, :, :], ms[:, :, :], ALU.mult), v)
                v = V.put(op(lambda e: e.tensor_tensor, gm[:, :, :], gm[:, :, :], t2[:, :, :], ALU.add), v)
                v = V.put(op(lambda e: e.tensor_reduce, mx[:, :, 0], gm[:, :, :], AX, ALU.max), v)
                v = V.put(op(lambda e: e.tensor_tensor, gm[:, :, :], gm[:, :, :], mx[:, :, :].broadcast_to([P, TB, 7]),
                    ALU.subtract), v)
                a = A.put(op(lambda e: e.activation, gm[:, :, :], gm[:, :, :], ACT.Exp), v)
                v = V.put(op(lambda e: e.tensor_reduce, sm[:, :, 0], gm[:, :, :], AX, ALU.add), a)
                v = V.put(op(lambda e: e.reciprocal, sm[:, :, :], sm[:, :, :]), v)
                prob = V.put(op(lambda e: e.tensor_tensor, pr[:, :, 0:7], gm[:, :, :], sm[:, :, :].broadcast_to([P, TB, 7]),
                    ALU.mult), v)
                routed.append(V.put(op(lambda e: e.tensor_copy, PR[:, :, t0:t0 + TB],
                                       pr[:, :, 0:7].rearrange("p t e -> p e t")), prob))
                b, ps = th.bank()
                pT = th.cut(256, 8)
                for i in range(TB):
                    tok = T.put(op(lambda e: e.transpose, ps[0:8, i * P:i * P + P], pr[:, i, :], ident), prob)
                th.free[b] = pt = V.put(op(lambda e: e.tensor_copy, pT, ps[0:8, 0:256]), tok)
                b, ps = th.bank()
                for i in range(TB):
                    tok = T.put(mm(ps[:, i * 256:i * 256 + 256], pT[:, i * P:i * P + P], bdn[:, :], True, True),
                                pt, loads["bdn"])
                th.free[b] = v = V.put(op(lambda e: e.tensor_tensor,
                    X[:, t0:t0 + TB, :], ps[:, :].rearrange("p (t n) -> p t n", t=TB), X[:, t0:t0 + TB, :], ALU.add),
                    tok)
                if shared:
                    shared_expert(th, t0, hT, ht, v)
                th.end(blk)
                th.done.append(rows_st[blk])

            def shared_later(th, blk):
                th.start(blk)
                t0 = blk * TB
                h = th.cut(512).rearrange("p (t c) -> p t c", t=TB)
                hT = th.cut(512).rearrange("p (k n) -> p k n", k=2)
                ld = S.dma(op(lambda e: e.dma_start, h[:, :, :],
                              hd[t0 * P:(t0 + TB) * P, :].rearrange("(t p) c -> p t c", p=P)), th.rsem, rows_st[blk])
                ht = turned(th, h, ld, hT[:, :, :])
                shared_expert(th, t0, hT, ht, None)
                th.end(blk)
                moe_last.extend(th.done)

            def shared_expert(th, t0, hT, ht, xv):
                u = th.cut(512).rearrange("p (k n) -> p k n", k=2)
                zz = th.cut(512).rearrange("p (k n) -> p k n", k=2)
                b, ps = th.bank()
                for f in range(2):
                    for k in range(2):
                        tok = T.put(mm(ps[:, f * 256:f * 256 + 256], UP[:, k, f * P:f * P + P], hT[:, k, :],
                                       k == 0, k == 1), ht, loads["shared"])
                A.wait(loads["moe_b"])
                for f in range(2):
                    a = A.put(op(lambda e: e.activation, u[:, f, :], ps[:, f * 256:f * 256 + 256], ACT.Identity,
                                 bias=moe_b[:, 0, 7, f:f + 1]), tok)
                th.free[b] = a
                b, ps = th.bank()
                for f in range(2):
                    for k in range(2):
                        tok = T.put(mm(ps[:, f * 256:f * 256 + 256], UG[:, k, f * P:f * P + P], u[:, k, :],
                                       k == 0, k == 1), a)
                for f in range(2):
                    a = A.put(op(lambda e: e.activation, zz[:, f, :], ps[:, f * 256:f * 256 + 256], ACT.Silu,
                                 bias=moe_b[:, 1, 7, f:f + 1]), tok)
                th.free[b] = a
                zr = V.put(op(lambda e: e.tensor_tensor, zz[:, :, :], zz[:, :, :], u[:, :, :], ALU.mult), a)
                b, ps = th.bank()
                for i in range(TB):
                    for k in range(2):
                        tok = T.put(mm(ps[:, i * 256:i * 256 + 256], zz[:, k, i * P:i * P + P], UD[:, k, :],
                                       k == 0, k == 1), zr)
                th.free[b] = V.put(op(lambda e: e.tensor_tensor,
                    X[:, t0:t0 + TB, :], ps[:, :].rearrange("p (t n) -> p t n", t=TB), X[:, t0:t0 + TB, :], ALU.add),
                    tok, xv)

            rows_st, routed, tabled, scattered, stored = [], [], [], [], []

            def clear_slots():
                z = G.put(op(lambda e: e.memset, zrow[:, :], 0.0))
                hv = hs_d.rearrange("(j p) c -> p j c", p=P)
                for c in range(0, NJ, 14):
                    cleared.append(S.dma(op(lambda e: e.dma_start, hv[:, c:c + 14, :],
                                            zrow[:, :].unsqueeze(1).broadcast_to([P, 14, 256])), sem("s_clr"), z))

            cleared = []

            def tables(th):
                th.start()
                w = lambda: th.cut(224)
                tot, exc, pos, t1, t2, one = (w() for _ in range(6))
                e3 = lambda a: a.rearrange("p (e t) -> p e t", e=7)
                te3 = lambda a: a.rearrange("p (e t) -> p t e", e=7)
                s_ = th.sm(100)
                Cp, n, kp, E, base = s_[:, 0:8], s_[:, 8:15], s_[:, 16:23], s_[:, 24:31], s_[:, 32:39]
                z7 = s_[:, 40:47]
                mxa, mxb = th.cut(32), th.cut(32)
                ni = th.cut(16)
                le = th.cut(NJ * 7)
                te = th.cut(NJ)
                msf, prf = MS.rearrange("p e t -> p (e t)"), PR.rearrange("p e t -> p (e t)")
                z = G.put(op(lambda e: e.memset, one, 1.0))
                z = G.put(op(lambda e: e.memset, s_[:, 0:48], 0.0))
                b, ps = th.bank()
                T.wait(loads["lt"], loads["one"], *routed)
                T.put(mm(ps[:, 0:224], SB["lt"][:, :], msf, True, True))
                tok = T.put(mm(ps[:, 256:480], SB["one"][:, :], msf, True, True))
                v = V.put(op(lambda e: e.tensor_copy, tot, ps[:, 256:480]), tok)
                v = V.put(op(lambda e: e.tensor_tensor_scan, exc, one, tot, 0.0, ALU.mult, ALU.add), v, z)
                v = V.put(op(lambda e: e.tensor_copy, Cp[:, 1:8], e3(exc)[:, :, 31]), v)
                v = V.put(op(lambda e: e.tensor_tensor, exc, exc, tot, ALU.subtract), v)
                v = V.put(op(lambda e: e.tensor_tensor, n, Cp[:, 1:8], Cp[:, 0:7], ALU.subtract), v)
                v = V.put(op(lambda e: e.tensor_scalar, n, n, 127.0, None, ALU.add), v)
                nii = ni[:, 0:7].bitcast(I32)
                v = V.put(op(lambda e: e.tensor_copy, nii, n), v)
                v = V.put(op(lambda e: e.tensor_scalar, nii, nii, 7, 7, ALU.arith_shift_right,
                             ALU.logical_shift_left), v)
                v = V.put(op(lambda e: e.tensor_copy, kp, nii), v)
                v = V.put(op(lambda e: e.tensor_tensor_scan, E, z7, kp, 0.0, ALU.add, ALU.add), v)
                v = V.put(op(lambda e: e.tensor_tensor, base, E, kp, ALU.subtract), v)
                v = V.put(op(lambda e: e.tensor_tensor, base, base, Cp[:, 0:7], ALU.subtract), v)
                v2 = V.put(op(lambda e: e.tensor_tensor, le.rearrange("p (j e) -> p j e", e=7),
                              SB["jj"][:, :].unsqueeze(2).broadcast_to([P, NJ, 7]),
                              E.unsqueeze(1).broadcast_to([P, NJ, 7]), ALU.is_ge), v, loads["jj"])
                v2 = V.put(op(lambda e: e.tensor_reduce, te, le.rearrange("p (j e) -> p j e", e=7), AX, ALU.add), v2)
                v2 = V.put(op(lambda e: e.tensor_scalar, te, te, 6.0, 512.0, ALU.min, ALU.mult), v2)
                v2 = V.put(op(lambda e: e.tensor_copy, tei[:, 0, :], te), v2)
                v2 = V.put(op(lambda e: e.tensor_scalar, te, te, 2.0 / 512.0, None, ALU.mult), v2)
                te_ok = V.put(op(lambda e: e.tensor_copy, tei[:, 1, :], te), v2)
                v = V.put(op(lambda e: e.tensor_tensor, pos, exc, ps[:, 0:224], ALU.add), v)
                th.free[b] = v
                v = V.put(op(lambda e: e.tensor_tensor, e3(pos), e3(pos),
                             base.unsqueeze(2).broadcast_to([P, 7, 32]), ALU.add), v)
                v = V.put(op(lambda e: e.tensor_scalar, t1, msf, -1.0e6, 1.0e6, ALU.mult, ALU.add), v)
                v = V.put(op(lambda e: e.tensor_tensor, t1, t1, pos, ALU.add), v)
                v = V.put(op(lambda e: e.tensor_reduce, mxa, te3(t1), AX, ALU.min), v)
                v = V.put(op(lambda e: e.scalar_tensor_tensor, t2, pos, 1.0, msf, ALU.add, ALU.mult), v)
                v = V.put(op(lambda e: e.tensor_reduce, mxb, te3(t2), AX, ALU.max), v)
                v = V.put(op(lambda e: e.tensor_copy, posi[:, 0, :], mxa), v)
                v = V.put(op(lambda e: e.tensor_tensor, e3(t1), e3(t1), mxa.unsqueeze(1).broadcast_to([P, 7, 32]),
                             ALU.is_equal), v)
                v = V.put(op(lambda e: e.tensor_tensor, e3(t2), e3(t2), mxb.unsqueeze(1).broadcast_to([P, 7, 32]),
                             ALU.is_equal), v)
                v = V.put(op(lambda e: e.tensor_scalar, mxb, mxb, 1.0, None, ALU.subtract), v)
                pos_ok = V.put(op(lambda e: e.tensor_copy, posi[:, 1, :], mxb), v)
                v = V.put(op(lambda e: e.tensor_tensor, t1, t1, prf, ALU.mult), v)
                v = V.put(op(lambda e: e.tensor_reduce, pAB[:, 0, :], te3(t1), AX, ALU.add), v)
                v = V.put(op(lambda e: e.tensor_tensor, t2, t2, prf, ALU.mult), v)
                v = V.put(op(lambda e: e.tensor_reduce, pAB[:, 1, :], te3(t2), AX, ALU.add), v)
                tabled.extend((te_ok, pos_ok, v))
                th.end()

            def scatter(th, n):
                th.start()
                h = th.cut(2048).rearrange("p (t c) -> p t c", t=8)
                ld = S.dma(op(lambda e: e.dma_start, h[:, :, :],
                              hd[n * 1024:n * 1024 + 1024, :].rearrange("(t p) c -> p t c", p=P)), th.rsem, *rows_st)
                for i in range(8):
                    for a in range(2):
                        idx = bass.IndirectOffsetOnAxis(ap=posi[:, a, 8 * n + i:8 * n + i + 1], axis=0)
                        g = G.dma(op(lambda e: e.indirect_dma_start, hs_d, idx, h[:, i, :], None), th.gsem,
                                  ld, tabled[1], *cleared)
                scattered.append(g)
                th.end()
                th.done.append(g)

            regs = {}

            def expert_load(q, lane, row, j):
                def fn(eng):
                    regs[q.name, lane] = eng.value_load(tei[0:1, row, j:j + 1], min_val=0,
                                                        max_val=3072 if row == 0 else 12)
                return Made(fn, 300)

            def expert_mm(lane, out_ap, lhsT, base, start, stop):
                return Made(lambda eng: eng.matmul(out_ap, lhsT, BIG[:, bass.ds(regs["pe", lane] + base, 256)],
                                                   start=start, stop=stop, skip_group_check=True), 427)

            def expert_act(lane, out_ap, in_ap, func, base):
                m = Made(lambda eng: eng.activation(out_ap, in_ap, func,
                                                    bias=BIG[:, bass.ds(regs["act", lane] + base, 1)]), 280)
                m.args = (None, None, func)
                return m

            def experts(th, js):
                th.start()
                B = {}
                for n, j in enumerate(js):
                    cu = lambda: th.cut(256)
                    B[j] = dict(h=cu(), hT=cu(), u=cu(), uT=cu(), g=cu(), z=cu())
                    B[j]["ld"] = S.dma(op(lambda e: e.dma_start, B[j]["h"], hs_d[j * P:j * P + P, :]), th.esem[n],
                                       *scattered)
                for j in js:
                    turn_rows(th, B[j], "h", "hT", B[j]["ld"])
                for step, (src, dst, w0, out) in enumerate((("hT", "u", 0, "uT"), ("uT", "g", 3584, "z"),
                                                            ("z", "h", 7168, None))):
                    for j in js:
                        T.wait(tabled[0], loads["moe0"], loads["moe1"], loads["moe2"])
                        T.put(expert_load(T, th.i, 0, j))
                        b, ps = th.bank()
                        T.wait(B[j][src + "_ok"])
                        for k in range(2):
                            tok = T.put(expert_mm(th.i, ps[:, 0:256], B[j][src][:, k * P:k * P + P],
                                                  w0 + k * 256, k == 0, k == 1))
                        th.free[b] = B[j][dst + "_ok"] = V.put(op(lambda e: e.tensor_copy, B[j][dst], ps[:, 0:256]),
                                                               tok)
                    for j in js:
                        if out is None:
                            stored.append(S.dma(op(lambda e: e.dma_start, ys_d[j * P:j * P + P, :], B[j]["h"]),
                                                th.wsem, B[j]["h_ok"]))
                            continue
                        b, ps = th.bank()
                        for k in range(2):
                            tok = T.put(op(lambda e: e.transpose, ps[:, k * P:k * P + P],
                                           B[j][dst][:, k * P:k * P + P], ident), B[j][dst + "_ok"])
                        A.wait(tabled[0], loads["moe_b"])
                        A.put(expert_load(A, th.i, 1, j))
                        for k in range(2):
                            a = A.put(expert_act(th.i, B[j][out][:, k * P:k * P + P], ps[:, k * P:k * P + P],
                                                 ACT.Identity if step == 0 else ACT.Silu,
                                                 12288 + 16 * step + k), tok)
                        th.free[b] = a
                        if step == 1:
                            a = G.put(op(lambda e: e.tensor_tensor, B[j]["z"], B[j]["z"], B[j]["uT"], ALU.mult), a)
                        B[j][out + "_ok"] = a
                th.end()
                moe_last.extend(th.done)
                th.done.append(stored[-1])

            def turn_rows(th, bj, src, dst, ready):
                b, ps = th.bank()
                for k in range(2):
                    tok = T.put(op(lambda e: e.transpose, ps[:, k * P:k * P + P], bj[src][:, k * P:k * P + P], ident),
                                ready)
                th.free[b] = bj[dst + "_ok"] = A.put(op(lambda e: e.activation, bj[dst], ps[:, 0:256], ACT.Copy), tok)

            def combine(th, blk, ya, yb):
                t0 = blk * TB
                for i in range(TB):
                    for a, y in enumerate((ya, yb)):
                        idx = bass.IndirectOffsetOnAxis(ap=posi[:, a, t0 + i:t0 + i + 1], axis=0)
                        g = G.dma(op(lambda e: e.indirect_dma_start, y[:, i * 256:i * 256 + 256], None, ys_d, idx),
                                  th.gsem, tabled[1], *stored)
                v = None
                for i in range(TB):
                    for a, y in enumerate((ya, yb)):
                        v = V.put(op(lambda e: e.scalar_tensor_tensor, X[:, t0 + i, :], y[:, i * 256:i * 256 + 256],
                                     pAB[:, a, t0 + i:t0 + i + 1], X[:, t0 + i, :], ALU.mult, ALU.add),
                                  g, v, tabled[2])
                return v

            moe_last = []

            def stage4(th, blk):
                th.start(blk)
                t0 = blk * TB
                h = th.cut(512).rearrange("p (t c) -> p t c", t=TB)
                pad = lambda: th.cut(2 * NB * 65)
                flat = {}

                def p4(n):
                    flat[n] = pad()
                    return flat[n].rearrange("p (k b s) -> p k b s", k=2, b=NB)

                f4 = lambda: th.cut(512).rearrange("p (k b s) -> p k b s", k=2, b=NB)
                H = p4("H")
                mx = [f4() for _ in range(3)]
                K, MX, E1, E2, GV = (p4(n) for n in ("K", "MX", "E1", "E2", "GV"))
                Vv = f4()
                C = mx[1]
                D = h.rearrange("p k (b s) -> p k b s", b=NB)
                for n, w, val in (("H", H, 0.0), ("K", K, NEG), ("E1", E1, 0.0), ("E2", E2, 0.0), ("GV", GV, 0.0)):
                    z = G.put(op(lambda e: e.memset, w[:, :, :, 0:1], val))
                V.wait(combine(th, blk, mx[1].rearrange("p k b s -> p (k b s)"), mx[2].rearrange("p k b s -> p (k b s)")))
                hn = norm(th, blk, lambda i, x: [(h[:, i, :], x)])
                A.wait(z)
                ht = turned(th, h, hn, H[:, :, :, 1:65])
                for m in range(3):
                    for k in range(2):
                        g = G.put(op(lambda e: e.tensor_scalar, mx[m][:, k, :, :], H[:, k, :, 0:64], omx[:, m, k:k + 1], 1.0,
                                     ALU.mult, ALU.mult), ht, om_ok)
                        mok = V.put(op(lambda e: e.scalar_tensor_tensor, mx[m][:, k, :, :], H[:, k, :, 1:65],
                    mix[:, m, k:k + 1], mx[m][:, k, :, :],
                    ALU.mult, ALU.add), g)
                    b, ps = th.bank()
                    for f in range(2):
                        for k in range(2):
                            tok = T.put(mm(ps[:, f * 256:f * 256 + 256], kvro[:, m, k, f * P:f * P + P],
                                           mx[m][:, k, :, :], k == 0, k == 1), mok, loads["w_kvro"])
                    src = ps[:, :].rearrange("p (k b s) -> p k b s", k=2, b=NB)
                    if m == 0:
                        kok = A.put(op(lambda e: e.activation, K[:, :, :, 1:65], src, ACT.Copy), tok)
                    elif m == 1:
                        vok = kok = A.put(op(lambda e: e.activation, Vv[:, :, :, :], src, ACT.Copy), tok)
                    else:
                        rok = kok = A.put(op(lambda e: e.activation, mx[0][:, :, :, :], src, ACT.Exp, scale=-1.0), tok)
                    th.free[b] = kok
                    if m == 0:
                        k1 = kok
                pv, cu = slice(0, 64), slice(1, 65)
                v = V.put(op(lambda e: e.tensor_tensor_scan, flat["MX"], td65[:, :], flat["K"], NEG, ALU.add, ALU.max),
                          k1, td_ok)
                mxo = v
                for k in range(2):
                    e1 = V.put(op(lambda e: e.scalar_tensor_tensor, E1[:, k, :, cu], MX[:, k, :, pv], tdn[:, k:k + 1],
                    MX[:, k, :, cu], ALU.add, ALU.subtract), mxo)
                ee1 = A.put(op(lambda e: e.activation, E1[:, :, :, cu], E1[:, :, :, cu], ACT.Exp), e1)
                g = G.put(op(lambda e: e.tensor_tensor, E2[:, :, :, cu], K[:, :, :, cu], MX[:, :, :, cu], ALU.subtract), mxo)
                ee2 = A.put(op(lambda e: e.activation, E2[:, :, :, cu], E2[:, :, :, cu], ACT.Exp), g)
                V.wait(vok)
                for k in range(2):
                    c = V.put(op(lambda e: e.scalar_tensor_tensor, C[:, k, :, :], K[:, k, :, cu], tfn[:, k:k + 1],
                    MX[:, k, :, pv], ALU.add, ALU.max))
                for k in range(2):
                    d = V.put(op(lambda e: e.scalar_tensor_tensor, D[:, k, :, :], K[:, k, :, cu], tfn[:, k:k + 1],
                    C[:, k, :, :], ALU.add, ALU.subtract), c)
                g = G.put(op(lambda e: e.tensor_tensor, C[:, :, :, :], MX[:, :, :, pv], C[:, :, :, :], ALU.subtract), d)
                e2 = A.put(op(lambda e: e.activation, D[:, :, :, :], D[:, :, :, :], ACT.Exp), d)
                e1 = A.put(op(lambda e: e.activation, C[:, :, :, :], C[:, :, :, :], ACT.Exp), g)
                gv = G.put(op(lambda e: e.tensor_tensor, GV[:, :, :, cu], E2[:, :, :, cu], Vv[:, :, :, :], ALU.mult), ee2, vok)
                den = V.put(op(lambda e: e.tensor_tensor_scan, flat["H"], flat["E1"], flat["E2"], 0.0, ALU.mult, ALU.add),
                            ee1, ee2)
                num = V.put(op(lambda e: e.tensor_tensor_scan, flat["MX"], flat["E1"], flat["GV"], 0.0, ALU.mult, ALU.add),
                            gv, g)
                f_ = lambda a: a.rearrange("p k b s -> p (k b s)")
                q0, q1, q2 = f_(mx[0]), f_(C), f_(mx[2])
                d1 = V.put(op(lambda e: e.tensor_tensor, mx[2][:, :, :, :], C[:, :, :, :], H[:, :, :, pv], ALU.mult),
                           den, e1, rok)
                o1 = V.put(op(lambda e: e.tensor_tensor, C[:, :, :, :], C[:, :, :, :], MX[:, :, :, pv], ALU.mult),
                           num)
                d1 = V.put(op(lambda e: e.tensor_tensor, q2, q2, f_(D), ALU.add), d1, e2)
                o2 = G.put(op(lambda e: e.tensor_tensor, Vv[:, :, :, :], D[:, :, :, :], Vv[:, :, :, :], ALU.mult), e2)
                o3 = G.put(op(lambda e: e.tensor_tensor, C[:, :, :, :], C[:, :, :, :], Vv[:, :, :, :], ALU.add), o1, o2)
                d1 = V.put(op(lambda e: e.scalar_tensor_tensor, q2, q0, 1.0, q2, ALU.add, ALU.mult), d1)
                d1 = V.put(op(lambda e: e.reciprocal, q2, q2), d1)
                oo = V.put(op(lambda e: e.tensor_tensor, q1, q1, q2, ALU.mult), d1, o3)
                oT = C.rearrange("p k b s -> p k (b s)")
                b, ps = th.bank()
                for i in range(TB):
                    for k in range(2):
                        tok = T.put(mm(ps[:, i * 256:i * 256 + 256], oT[:, k, i * P:i * P + P], kvro[:, 3, k, :],
                                       k == 0, k == 1), oo)
                th.free[b] = V.put(op(lambda e: e.tensor_tensor, 
                    X[:, t0:t0 + TB, :], ps[:, :].rearrange("p (t n) -> p t n", t=TB), X[:, t0:t0 + TB, :], ALU.add), tok)
                th.end(blk)

            def stage5(th, blk):
                th.start(blk)
                t0 = blk * TB
                hq = th.cut(1024).rearrange("p (t g a kd) -> p t g a kd", t=TB, g=4, a=2)
                QB = th.cut(1024).rearrange("p (t g n) -> p t g n", t=TB, g=4)
                CT = th.cut(256).rearrange("p (b d) -> p b d", b=NB)
                CK = th.cut(128).rearrange("p (t l) -> p t l", t=TB)
                BK = th.cut(1024).rearrange("p (t k l) -> p t k l", t=TB, k=8)
                BV = th.cut(288).rearrange("p (b q c) -> p b q c", b=NB, q=4)
                Pm = [th.cut(512).rearrange("p (k l) -> p k l", k=8) for _ in range(2)]
                hqf = hq.rearrange("p t g a kd -> p (t g a kd)")
                PT = [hqf[:, 512 * n:512 * n + 512].rearrange("p (k l) -> p k l", k=4) for n in range(2)]
                O = th.cut(512).rearrange("p (t c) -> p t c", t=TB)
                ct = ctx_rows(th, blk, CT)
                ct = S.dma(op(lambda e: e.dma_start, CK[:, :, :], t["ctxT"][t0:t0 + TB, :, :].rearrange("t p l -> p t l")),
                           th.csem)
                z = G.put(op(lambda e: e.memset, QB[:, :, :, :], 0.0))
                mk = SB["mk"][:, :].unsqueeze(2).broadcast_to([P, 8, 64])
                G.wait(loads["mk"], loads["mv"])
                for i in range(TB):
                    bk = G.put(op(lambda e: e.tensor_tensor, BK[:, i, :, :], CK[:, i, :].unsqueeze(1).broadcast_to([P, 8, 64]),
                    mk, ALU.mult), ct)
                for j in range(NB):
                    bv = G.put(op(lambda e: e.tensor_tensor, BV[:, j, :, 0:16],
                                  CT[:, j, :].rearrange("p (q c) -> p q c", q=4),
                                  SB["mv"][:, :].rearrange("p (q c) -> p q c", q=4), ALU.mult))
                bv = G.put(op(lambda e: e.tensor_scalar, BV[:, :, :, 16:18].rearrange("p b q c -> p (b q) c"),
                              SB["mv"][:, 0:9:8].unsqueeze(1).broadcast_to([P, 4 * NB, 2]), 1.0, 1.0,
                              ALU.mult, ALU.mult))

                def views(i, x):
                    x = None if x is None else x.rearrange("p (k g d) -> p g k d", k=8, g=4)
                    return [(hq[:, i, :, a, :].rearrange("p g (k d) -> p g k d", k=8), x) for a in range(2)]

                hn = norm(th, blk, views)
                for i in range(TB):
                    b, ps = th.bank()
                    for g in range(4):
                        tok = T.put(op(lambda e: e.transpose, ps[:, g * P:g * P + P],
                    hq[:, i, g, :, :].rearrange("p a n -> p (a n)"), ident), hn)
                    for e2 in range(2):
                        rows = slice(64 * e2, 64 * e2 + 64)
                        qb = A.put(op(lambda e: e.activation, 
                    QB[rows, i, :, rows], ps[:, :].rearrange("p (g n) -> p g n", g=4)[rows, :, rows], ACT.Copy),
                            tok, z)
                    th.free[b] = qb
                ptr, tr = [None] * 2, [None] * 2
                mxs = [th.sm(32).rearrange("p (g k) -> p g k", g=4) for _ in range(TB)]
                sms = [th.sm(32).rearrange("p (g k) -> p g k", g=4) for _ in range(TB)]

                def scores(i, g):
                    b, ps = th.bank()
                    tok = T.put(mm(ps[:, :], QB[:, i, g, :], BK[:, i, :, :], True, True), qb, bk)
                    src, m = ps[:, :].rearrange("p (k l) -> p k l", k=8), mxs[i][:, g, :]
                    v = V.put(op(lambda e: e.tensor_reduce, m, src, AX, ALU.max), tok, tr[g % 2])
                    th.free[b] = v = V.put(op(lambda e: e.tensor_tensor, Pm[g % 2][:, :, :], src,
                                              m.unsqueeze(2).broadcast_to([P, 8, 64]), ALU.subtract), v)
                    return A.put(op(lambda e: e.activation, Pm[g % 2][:, :, :], Pm[g % 2][:, :, :], ACT.Exp,
                                    scale=8.0 ** -0.5), v)

                units = [(i, g) for i in range(TB) for g in range(4)]
                v = scores(*units[0])
                for n, (i, g) in enumerate(units):
                    vn = scores(*units[n + 1]) if n + 1 < len(units) else None
                    b, ps = th.bank()
                    for q in range(4):
                        tr[g % 2] = tok = T.put(op(lambda e: e.transpose, ps[:, q * P:q * P + P],
                                                   Pm[g % 2][:, 2 * q:2 * q + 2, :].rearrange("p k l -> p (k l)"),
                                                   ident), v)
                    A.wait(ptr[g % 2])
                    th.free[b] = pt = A.put(op(lambda e: e.activation, PT[g % 2][:, :, :],
                                               ps[:, :].rearrange("p (k l) -> p k l", k=4), ACT.Copy), tok)
                    b, ps = th.bank()
                    ov = ps[:, 0:144].rearrange("p (b q c) -> p b q c", b=2, q=4)
                    for q in range(4):
                        ptr[g % 2] = tok = T.put(mm(ov[:, :, q, :], PT[g % 2][:, q, :], BV[:, 2 * i:2 * i + 2, q, :],
                                                    True, True), pt, bv)
                    for b2 in range(2):
                        rows = slice(64 * b2, 64 * b2 + 64)
                        o = V.put(op(lambda e: e.reciprocal, sms[i][rows, g, :].rearrange("p (q c) -> p q c", q=4),
                                     ov[rows, b2, :, 16:18]), tok)
                    for b2 in range(2):
                        rows = slice(64 * b2, 64 * b2 + 64)
                        o = V.put(op(lambda e: e.tensor_tensor,
                                     O[rows, i, :].rearrange("p (q e g d) -> p q e g d", q=4, e=2, g=4)[:, :, :, g, :],
                                     ov[rows, b2, :, 0:16].rearrange("p q (e d) -> p q e d", e=2),
                                     sms[i][rows, g, :].rearrange("p (q e) -> p q e", q=4).unsqueeze(3)
                                     .broadcast_to([64, 4, 2, 8]), ALU.mult), o)
                    th.free[b] = o
                    v = vn
                    if g == 3:
                        G.put(op(lambda e: e.tensor_tensor, X[:, t0 + i, :], X[:, t0 + i, :], O[:, i, :], ALU.add), o)
                th.end(blk)

            def load_ffn():
                w = tuple(moe_last)
                load("WG", WG, t["wg"].rearrange("p (k n) -> p k n", k=2), w)
                load("MW", MW, t["mw"].rearrange("p (k n) -> p k n", k=2), w)
                load("GW", GW, t["gw"].rearrange("p (k n) -> p k n", k=2), w)
                load("WD", WD, t["wd"].rearrange("p (k n) -> p k n", k=11), w)

            def prep_ffn(th):
                th.start()
                f = th.cut(256, 64).rearrange("p (a n) -> p a n", a=4)
                v = V.put(op(lambda e: e.tensor_copy, f[:, 0, :], invt[:, :]), loads["invt"])
                v = V.put(op(lambda e: e.tensor_scalar, f[:, 1, :], f[:, 0, :], 0.0, 64.0, ALU.is_lt, ALU.mult), v)
                v = V.put(op(lambda e: e.tensor_tensor, f[:, 2, :], f[:, 0, :], f[:, 1, :], ALU.add), v)
                v = V.put(op(lambda e: e.tensor_scalar, f[:, 3, :], f[:, 2, :], 0.0, 63.0, ALU.max, ALU.min), v)
                pm = V.put(op(lambda e: e.tensor_scalar, PM, f[:, 3, :], SB["eid"][0:64, 0:1], None, ALU.is_equal),
                           v, loads["eid"], *moe_last)
                for g in range(8):
                    b, ps = th.bank()
                    for k in range(2):
                        tok = T.put(mm(ps[0:64, 0:352], MW[:, k, :], WG[:, k, g * 352:g * 352 + 352], k == 0, k == 1),
                                    loads["MW"], loads["WG"])
                    th.free[b] = v = V.put(op(lambda e: e.tensor_scalar, MG[:, g * 352:g * 352 + 352], ps[0:64, 0:352],
                    SB["mg"][0:64, g:g + 1], None, ALU.mult),
                                           tok, loads["mg"])
                ffn_ok.extend((pm, v))
                th.end()

            ffn_ok = []

            def stage6(th, blk):
                th.start(blk)
                t0 = blk * TB
                h = th.cut(512).rearrange("p (t c) -> p t c", t=TB)
                hT = th.cut(512).rearrange("p (k n) -> p k n", k=2)
                r = lambda n: th.cut(TB * n).rearrange("p (t n) -> p t n", t=TB)
                sc, we, t8 = r(64), r(64), r(8)
                mx = th.sm(32)
                weT = th.cut(256, 64)
                soT = th.cut(256, 64)
                s8 = th.cut(8 * 16).rearrange("p (a t g) -> p a t g", a=8, t=TB)
                fl, nz = r(64), r(64)
                sg = th.cut(2 * 176).rearrange("p (a n) -> p a n", a=2)
                AG = th.cut(1408)
                AT = th.cut(1408).rearrange("p (k n) -> p k n", k=11)
                hn = norm(th, blk, lambda i, x: [(h[:, i, :], x)])
                ht = turned(th, h, hn, hT[:, :, :])
                b, ps = th.bank()
                for i in range(TB):
                    for k in range(2):
                        tok = T.put(mm(ps[:, 64 * i:64 * i + 64], hT[:, k, i * P:i * P + P], GW[:, k, :],
                                       k == 0, k == 1), ht, loads["GW"])
                fr, v = row_softmax(th, ps[:, 0:128].rearrange("p (t n) -> p t n", t=TB), sc[:, :, :], mx[:, 0:2],
                                    mx[:, 2:4], TB, tok)
                th.free[b] = fr
                v = V.put(op(lambda e: e.tensor_tensor, sc[:, :, :], sc[:, :, :],
                    mx[:, 2:4].unsqueeze(2).broadcast_to([P, TB, 64]), ALU.mult), v)
                for i in range(TB):
                    v1 = V.put(op(lambda e: e.max, t8[:, i, :], sc[:, i, :]), v)
                    v1 = V.put(op(lambda e: e.match_replace, we[:, i, :], t8[:, i, :], sc[:, i, :], 0.0), v1)
                v = V.put(op(lambda e: e.tensor_tensor, we[:, :, :], sc[:, :, :], we[:, :, :], ALU.subtract), v1)
                b, ps = th.bank()
                for i in range(TB):
                    tok = T.put(op(lambda e: e.transpose, ps[0:64, i * P:i * P + P], we[:, i, :], ident), v)
                th.free[b] = v = V.put(op(lambda e: e.tensor_copy, weT, ps[0:64, 0:256]), tok)
                b, ps = th.bank()
                T.wait(*ffn_ok)
                for i in range(TB):
                    tok = T.put(mm(ps[:, 64 * i:64 * i + 64], weT[:, i * P:i * P + P], PM, True, True), v)
                f3 = ps[:, 0:128].rearrange("p (a i) -> p a i", i=8)
                s2 = lambda n: s8[:, n, :, :].rearrange("p t g -> p (t g)")
                g3 = lambda w: w[:, :, :].rearrange("p t (g i) -> p (t g) i", i=8)
                s_ok = V.put(op(lambda e: e.tensor_reduce, s2(0), f3, AX, ALU.add), tok)
                v = V.put(op(lambda e: e.tensor_scalar, g3(nz), f3, 0.0, -1e9, ALU.is_equal, ALU.mult))
                th.free[b] = v = V.put(op(lambda e: e.tensor_tensor, g3(fl), f3, g3(nz), ALU.add), v)
                v = V.put(op(lambda e: e.tensor_reduce, s2(1), g3(fl), AX, ALU.max), v)
                bc = lambda n: s2(n).unsqueeze(2).broadcast_to([P, TB * 8, 8])
                v = V.put(op(lambda e: e.tensor_tensor, g3(fl), g3(fl), bc(1), ALU.subtract), v)
                a = A.put(op(lambda e: e.activation, fl[:, :, :], fl[:, :, :], ACT.Exp), v)
                v = V.put(op(lambda e: e.tensor_reduce, s2(2), g3(fl), AX, ALU.add), a)
                v = V.put(op(lambda e: e.reciprocal, s2(3), s2(2)), v)
                v = V.put(op(lambda e: e.tensor_tensor, g3(fl), g3(fl), bc(3), ALU.mult), v)
                b, ps = th.bank()
                for i in range(TB):
                    tok = T.put(op(lambda e: e.transpose, ps[0:64, i * P:i * P + P], fl[:, i, :], ident), v)
                th.free[b] = so = V.put(op(lambda e: e.tensor_copy, soT, ps[0:64, 0:256]), tok)
                atr = None
                sgr = [None] * 2
                agr = None
                fin = []
                for i in range(TB):
                    ts = slice(i * P, i * P + P)
                    for g in range(8):
                        b, ps = th.bank()
                        gs = slice(g * 352, g * 352 + 352)
                        for k in range(2):
                            T.put(mm(ps[:, 0:352], hT[:, k, ts], WG[:, k, gs], k == 0, False))
                        tok = T.put(mm(ps[:, 0:352], soT[:, ts], MG[:, gs], False, True), so)
                        a = A.put(op(lambda e: e.activation, sg[:, g % 2, :], ps[:, 0:176], ACT.Silu), tok, sgr[g % 2])
                        V.wait(agr)
                        th.free[b] = sgr[g % 2] = v = V.put(op(lambda e: e.scalar_tensor_tensor, 
                    AG[:, g * 176:g * 176 + 176], sg[:, g % 2, :], s8[:, 0, i, g:g + 1], ps[:, 176:352],
                    ALU.mult, ALU.mult), a, s_ok)
                    for c in range(3):
                        b, ps = th.bank()
                        n = min(4, 11 - 4 * c)
                        for q in range(n):
                            c0 = (4 * c + q) * P
                            tok = T.put(op(lambda e: e.transpose, ps[:, q * P:q * P + P], AG[:, c0:c0 + P], ident), v)
                        th.free[b] = at = A.put(op(lambda e: e.activation, 
                    AT[:, 4 * c:4 * c + n, :], ps[:, 0:n * P].rearrange("p (k n) -> p k n", k=n), ACT.Copy),
                            tok, atr)
                    agr = tok
                    b, ps = th.bank()
                    for q in range(11):
                        tok = T.put(mm(ps[:, 0:256], AT[:, q, :], WD[:, q, :], q == 0, q == 10), at, loads["WD"])
                    atr = tok
                    th.free[b] = v = V.put(op(lambda e: e.tensor_tensor, X[:, t0 + i, :], ps[:, 0:256], X[:, t0 + i, :],
                    ALU.add), tok)
                    S.dma(op(lambda e: e.dma_start, out[(t0 + i) * P:(t0 + i) * P + P, :], X[:, t0 + i, :]), s_out, v)
                th.end(blk)

            s_out = sem("s_out")
            om_ok = V.put(op(lambda e: e.tensor_scalar, om[:, :], SB["mix"][:, :], -1.0, 1.0, ALU.mult, ALU.add),
                          loads["mix"])
            tdn, tfn = acst[:, 16:18], SB["tdf"][:, 2:4]
            a = A.put(op(lambda e: e.activation, acst[:, 12:14], SB["tdf"][:, 0:2], ACT.Exp), loads["tdf"])
            v = V.put(op(lambda e: e.tensor_scalar, tdn, acst[:, 12:14], -1.0, None, ALU.mult), a)
            z = G.put(op(lambda e: e.memset, td65[:, :], 0.0))
            for k in range(2):
                v = V.put(op(lambda e: e.tensor_scalar, td65v[:, k, :, 1:65], td65v[:, k, :, 1:65], tdn[:, k:k + 1],
                             None, ALU.add), v, z)
            td_ok = G.put(op(lambda e: e.memset, td65v[:, :, :, 0:1], NEG), v)
            load_moe()
            clear_slots()
            plan(threads, products, stage1, stage2, stage3, move_lane, shared_later, tables, scatter, experts, stage4, stage5,
                 load_ffn, prep_ffn, stage6)
            return queues

        T, V, A, G, S = program()
        order((T, V, A, G, S))
        block = ctx.enter_context(nc.Block())

        totals = {}

        @block.sync
        def _(eng):
            S.play(eng)
            for ins in S.order + G.order:
                if ins.step == 16:
                    totals[id(ins.sem)] = (ins.sem, ins.value)
            for s_, value in totals.values():
                eng.wait_ge(s_, value)

        @block.tensor
        def _(eng):
            T.play(eng)

        @block.vector
        def _(eng):
            V.play(eng)

        @block.scalar
        def _(eng):
            A.play(eng)

        @block.gpsimd
        def _(eng):
            G.play(eng)


def plan(lanes, products, stage1, stage2, stage3, move_lane, shared_later, tables, scatter, experts, stage4, stage5,
         load_ffn, prep_ffn, stage6):
    turn = [0]

    def lane(n=NTH):
        turn[0] += 1
        return lanes[turn[0] % n]

    for d in range(NBLK + 2):
        if d in (0, 1):
            products(lane(), 2 * d)
            products(lane(), 2 * d + 1)
        if d < NBLK:
            stage1(lane(), d)
        if 0 <= d - 1 < NBLK:
            stage2(lane(), d - 1)
        if 0 <= d - 2 < NBLK:
            stage3(lane(), d - 2, d - 2 < NBLK - LATER1 - LATER2)
    last = lanes[-1]
    move_lane(last)
    tables(last)
    for n in range(4):
        scatter(last, n)
    for b in range(NBLK - LATER1 - LATER2, NBLK - LATER2):
        shared_later(lane(NTH - 1), b)
    for j in range(0, NJ, 2):
        experts(lane(), (j, j + 1))
    for b in range(NBLK - LATER2, NBLK):
        shared_later(lane(), b)
    load_ffn()
    for d in range(NBLK + 2):
        if d < NBLK:
            stage4(lane(), d)
        if 0 <= d - 1 < NBLK:
            stage5(lane(), d - 1)
        if d == 1:
            prep_ffn(lane())
        if 0 <= d - 2 < NBLK:
            stage6(lane(), d - 2)


def constants():
    i = np.arange(128)
    same = (i[:, None] // 64) == (i[None, :] // 64)
    f = np.float32
    inv = (f(1.0) / np.power(f(10000.0), np.arange(0, 64, 2, dtype=f) / f(64))).astype(f)
    fr = np.arange(64, dtype=f)[:, None] * inv[None, :]
    s, c = np.repeat(np.sin(fr), 2, axis=-1).astype(f), np.repeat(np.cos(fr), 2, axis=-1).astype(f)
    s[:, :32] = -s[:, :32]
    col = np.arange(64)
    return {
        "ident": np.eye(128, dtype=f),
        "tri": (same & (i[:, None] <= i[None, :])).astype(f),
        "gt": (same & (i[:, None] > i[None, :])).astype(f),
        "cos": np.ascontiguousarray(np.concatenate([c, c])), "sin": np.ascontiguousarray(np.concatenate([s, s])),
        "mv": ((i[:, None] // 64) == ((col[None, :] // 8) % 2)).astype(f),
        "mk": (((i[:, None] % 64) // 8) == np.arange(8)[None, :]).astype(f),
        "mg": (((i[:, None] % 64) // 8) == np.arange(8)[None, :]).astype(f),
        "eid": i[:, None].astype(f),
        "lt": (i[:, None] < i[None, :]).astype(f),
        "one": np.ones((128, 128), f),
        "jj": np.ascontiguousarray(np.broadcast_to((np.arange(NJ, dtype=f) * 128)[None, :], (128, NJ))),
    }


def kernel(**inputs):
    import concourse.bacc as bacc
    from concourse.bass_utils import run_bass_kernel_spmd

    a = {k: np.asarray(v) for k, v in inputs.items()}

    def ks(w, k=2):
        n = w.shape[-1]
        return w.reshape(k, 128, n).transpose(1, 0, 2).reshape(128, k * n)

    def rep(v):
        return np.broadcast_to(v.reshape(1, -1), (128, v.size))

    L0 = lambda n: a["L0_" + n]
    L1 = lambda n: a["L1_" + n]
    ar = dict(constants())
    ctx = a["ctx_512"]
    ar["x"] = a["x"].reshape(4096, 256)
    ar["ctx"] = ctx
    ar["ctxT"] = ctx.transpose(0, 2, 1).reshape(32, 128, 64)
    ar["w_in"] = ks(L0("attn_in_proj_w"))
    ar["nscale"] = L0("attn_norm_scale").reshape(2, 128).T
    ar["convw"] = L0("attn_conv_weight").reshape(4, 4, 128).transpose(2, 1, 0).reshape(128, 16)
    ar["convb"] = L0("attn_conv_bias").reshape(4, 128).T
    ar["dskip"] = L0("attn_D").reshape(4, 128).T
    ar["alog"] = rep(L0("attn_A_log"))
    ar["dtb"] = rep(L0("attn_dt_bias"))
    ar["w_out"] = ks(L0("attn_out_proj_w"), 4)
    ar["wq"] = L0("xattn_Wq").reshape(16, 128, 256).transpose(1, 0, 2)
    ar["wkcq"] = L0("xattn_w_kc_q").reshape(16, 128, 2, 96).transpose(3, 2, 0, 1)
    ar["wqr"] = L0("xattn_W_qr").transpose(2, 0, 1)
    ar["wkr"] = L0("xattn_W_kr").transpose(2, 0, 1)
    ar["wkc"] = L0("xattn_w_kc_kv").transpose(1, 0, 2)
    ar["wo"] = L0("xattn_Wo").reshape(256, 16, 128).transpose(2, 1, 0)
    up = np.concatenate([L0("ffn_Wup"), L0("ffn_Wsu")[None]])
    ga = np.concatenate([L0("ffn_Wgate"), L0("ffn_Wsg")[None]])
    dn = np.concatenate([L0("ffn_Wdown"), L0("ffn_Wsd")[None]])
    w = np.stack([up, ga, dn]).reshape(3, 8, 2, 128, 256)
    ar["moe_w"] = w.transpose(3, 1, 0, 2, 4).reshape(128, 8, 1536)
    bb = np.stack([np.concatenate([L0("ffn_bup"), L0("ffn_bsu")[None]]),
                   np.concatenate([L0("ffn_bgate"), L0("ffn_bsg")[None]])])
    ar["moe_b"] = bb.reshape(2, 8, 2, 128).transpose(3, 0, 1, 2)
    ar["bdn"] = np.concatenate([L0("ffn_bdown"), L0("ffn_bsd")[None]])
    ar["moe_r"] = L0("ffn_Wr").reshape(2, 128, 7).transpose(1, 0, 2)
    ar["rb"] = rep(L0("ffn_br"))
    ar["gb"] = rep(L0("ffn_gate_bias"))
    mixes = np.stack([L1("attn_time_mix_key"), L1("attn_time_mix_value"), L1("attn_time_mix_receptance")])
    ar["mix"] = mixes.reshape(3, 2, 128).transpose(2, 0, 1).reshape(128, 6)
    ar["tdf"] = np.stack([L1("attn_time_decay"), L1("attn_time_first")]).reshape(4, 128).T
    ar["w_kvro"] = np.stack([L1("attn_Wk"), L1("attn_Wv"), L1("attn_Wr"), L1("attn_Wo")]) \
        .reshape(4, 2, 128, 256).transpose(2, 0, 1, 3).reshape(128, 2048)
    gu = np.concatenate([L1("ffn_gate_proj_w"), L1("ffn_up_proj_w")], axis=1)
    ar["wg"] = gu.reshape(8 * 352, 2, 128).transpose(2, 1, 0).reshape(128, 5632)
    ar["mw"] = L1("ffn_mask_up_w").transpose(1, 0, 2).reshape(2, 128, 64).transpose(1, 0, 2).reshape(128, 128)
    ar["gw"] = L1("ffn_gate_w").reshape(64, 2, 128).transpose(2, 1, 0).reshape(128, 128)
    ar["wd"] = L1("ffn_down_proj_w").transpose(0, 2, 1).reshape(11, 128, 256).transpose(1, 0, 2).reshape(128, 2816)
    ar["invt"] = np.broadcast_to(L1("ffn_inv_map").reshape(1, 64), (64, 64))

    nc = bacc.Bacc("TRN2", target_bir_lowering=False, num_devices=1)
    arrays, aps = {}, {}
    for name, v in ar.items():
        v = np.ascontiguousarray(v)
        arrays["in_" + name] = v
        aps[name] = nc.dram_tensor("in_" + name, v.shape, mybir.dt.from_np(v.dtype), kind="ExternalInput").ap()
    out = nc.dram_tensor("out_0", (4096, 256), F32, kind="ExternalOutput").ap()
    build(nc, aps, out)
    r = run_bass_kernel_spmd(nc, [arrays], core_ids=[0])
    return r.results[0]["out_0"].reshape(64, 64, 256)
```
